# Optimizing a Trainium2 kernel written in Bass

```python
import numpy as np
import jax
import jax.numpy as jnp

def _softmax(x, axis=-1):
    return jax.nn.softmax(x, axis=axis)

def _gelu(x):
    return jax.nn.gelu(x, approximate=True)

def _silu(x):
    return jax.nn.silu(x)

def _sigmoid(x):
    return jax.nn.sigmoid(x)

def _layernorm(x, axis=-1, eps=1e-05):
    m = jnp.mean(x, axis=axis, keepdims=True)
    v = jnp.var(x, axis=axis, keepdims=True)
    return (x - m) / jnp.sqrt(v + eps)

def _scatter_add(tgt, idx, src, axis=0):
    return tgt.at[idx].add(src)

def _segment_sum(src, seg, n):
    return jax.ops.segment_sum(src, seg, n)
kernel_name = 'mk_xattn_ffn_d2_seqx_r8_3b5448'

def setup_inputs(seed: int=0):
    np.random.seed(seed)
    _w = jnp.asarray

    def _rec_inputs():
        import jax
        import jax.numpy as jnp
        _rk = jax.random.key(seed)
        x = -0.0003929 + 0.9999 * jax.random.normal(jax.random.fold_in(_rk, 1), (4, 256, 512), jnp.float32)
        _lenS = 256 - jax.random.randint(jax.random.fold_in(_rk, 7), (4,), 0, max(1, 256 // 4) + 1, jnp.int32)
        _lenS2 = 1601 - jax.random.randint(jax.random.fold_in(_rk, 8), (4,), 0, max(1, 1601 // 4) + 1, jnp.int32)
        _ctx_4096P = jax.random.normal(jax.random.fold_in(_rk, 11), (4, 16, 512), jnp.float32)
        _ctx_4096c = jax.random.dirichlet(jax.random.fold_in(_rk, 511), 0.3 * jnp.ones((16,), jnp.float32), (4, 1601))
        _ctx_4096t = jnp.einsum('bsk,bkd->bsd', _ctx_4096c, _ctx_4096P)
        _ctx_4096t = _ctx_4096t * jax.lax.rsqrt(jnp.mean(jnp.square(_ctx_4096t)) + 1e-12) * 0.953939
        ctx_4096 = 2.81802e-05 + 1.00001 * (_ctx_4096t + 0.3 * jax.random.normal(jax.random.fold_in(_rk, 611), (4, 1601, 512), jnp.float32))
        return (x, ctx_4096)
    x, ctx_4096 = _rec_inputs()

    def _L0_xattn_setup():
        import jax, jax.numpy as jnp
        import numpy as np
        B, N, NKV = (2, 256, 256)
        E = 512
        H = 16
        HD = E // H
        LQ = E // 8
        LKV = E // 16
        key = jax.random.key(seed)
        ks = jax.random.split(key, 6)
        Q = jax.random.normal(ks[0], (B, N, E), dtype=jnp.float32)
        K = jax.random.normal(ks[1], (B, NKV, E), dtype=jnp.float32)
        Wq_d = jax.random.normal(ks[2], (E, LQ), dtype=jnp.float32) / np.sqrt(E)
        W_qk = jax.random.normal(ks[3], (LQ, H * LKV), dtype=jnp.float32) / np.sqrt(LQ)
        Wkv_d = jax.random.normal(ks[4], (E, LKV), dtype=jnp.float32) / np.sqrt(E)
        Wv_u = jax.random.normal(ks[5], (LKV, H * HD), dtype=jnp.float32) / np.sqrt(LKV)
        return {'Q': Q, 'K': K, 'Wq_d': Wq_d, 'W_qk': W_qk, 'Wkv_d': Wkv_d, 'Wv_u': Wv_u}
    _L0_xattn_all = _L0_xattn_setup()
    _L0_xattn_in = {k: v for k, v in _L0_xattn_all.items() if k in ('Wq_d', 'W_qk', 'Wkv_d', 'Wv_u')}
    del _L0_xattn_all

    def _L0_ffn_setup():
        import jax, jax.numpy as jnp
        import numpy as np
        GROUP_SIZE = 128

        def dequantize_int4(weight_q, scale, zero_point, group_size):
            out_f, in_f = weight_q.shape
            n_groups = in_f // group_size
            w = weight_q.astype(jnp.float32).reshape(out_f, n_groups, group_size)
            w = (w - zero_point[:, :, None]) * scale[:, :, None]
            return w.reshape(out_f, in_f)
        key = jax.random.key(seed)
        k1, k2, k3, k4, k5 = jax.random.split(key, 5)
        B, S, D_IN, D_OUT = (2, 256, 512, 512)
        n_groups = D_IN // GROUP_SIZE
        x = jax.random.normal(k1, (B, S, D_IN), dtype=jnp.float32)
        weight_q = jax.random.randint(k2, (D_OUT, D_IN), 0, 16, dtype=jnp.int32)
        scale = jax.random.uniform(k3, (D_OUT, n_groups), dtype=jnp.float32, minval=0.001, maxval=0.02)
        zero_point = jax.random.uniform(k4, (D_OUT, n_groups), dtype=jnp.float32, minval=0.0, maxval=15.0)
        bias = jax.random.normal(k5, (D_OUT,), dtype=jnp.float32)
        return {'x': x, 'weight_q': weight_q, 'scale': scale, 'zero_point': zero_point, 'bias': bias}
    _L0_ffn_all = _L0_ffn_setup()
    _L0_ffn_in = {k: v for k, v in _L0_ffn_all.items() if k in ('weight_q', 'scale', 'zero_point', 'bias')}
    del _L0_ffn_all

    def _L1_xattn_setup():
        import jax, jax.numpy as jnp
        import numpy as np
        B, Q, D = (8, 64, 512)
        CTX = 512
        H, KV, HD = (16, 4, 96)
        G = H // KV
        key = jax.random.key(seed)
        ks = jax.random.split(key, 6)
        s = 0.02
        return {'latents': jax.random.normal(ks[0], (B, Q, D), jnp.float32), 'context': jax.random.normal(ks[1], (B, CTX, D), jnp.float32), 'Wq': jax.random.normal(ks[2], (H * HD, D), jnp.float32) * s, 'Wk': jax.random.normal(ks[3], (KV * HD, D), jnp.float32) * s, 'Wv': jax.random.normal(ks[4], (KV * HD, D), jnp.float32) * s, 'Wo': jax.random.normal(ks[5], (D, H * HD), jnp.float32) * s}
    _L1_xattn_all = _L1_xattn_setup()
    _L1_xattn_in = {k: v for k, v in _L1_xattn_all.items() if k in ('Wq', 'Wk', 'Wv', 'Wo')}
    del _L1_xattn_all

    def _L1_ffn_setup():
        import jax, jax.numpy as jnp
        import numpy as np
        NUM_EXPERTS = 8
        RANK = 32
        ALPHA = 16.0
        TOP_K = 2
        TEMPERATURE = 1.0
        GAMMA = 0.5
        SOFT_TOPK_TEMP = 0.5
        N_GRAM = 2
        EPS = 1e-06
        key = jax.random.key(seed)
        ks = jax.random.split(key, 6)
        d_in, d_out = (512, 512)
        Bsz, T = (4, 256)
        x = jax.random.normal(ks[0], (Bsz, T, d_in), dtype=jnp.float32)
        W = jax.random.normal(ks[1], (d_out, d_in), dtype=jnp.float32) / np.sqrt(d_in)
        b = jax.random.normal(ks[2], (d_out,), dtype=jnp.float32) * 0.01
        A = jax.random.normal(ks[3], (d_in, RANK), dtype=jnp.float32) / np.sqrt(d_in)
        Bmat = jax.random.normal(ks[4], (RANK, d_out), dtype=jnp.float32) * 0.01
        LiMEs = jax.random.normal(ks[5], (NUM_EXPERTS, RANK), dtype=jnp.float32) * 0.1
        return {'x': x, 'W': W, 'b': b, 'A': A, 'Bmat': Bmat, 'LiMEs': LiMEs}
    _L1_ffn_all = _L1_ffn_setup()
    _L1_ffn_in = {k: v for k, v in _L1_ffn_all.items() if k in ('W', 'b', 'A', 'Bmat', 'LiMEs')}
    del _L1_ffn_all
    return {'x': x, 'ctx_4096': ctx_4096, 'L0_xattn_Wq_d': _L0_xattn_in['Wq_d'], 'L0_xattn_W_qk': _L0_xattn_in['W_qk'], 'L0_xattn_Wkv_d': _L0_xattn_in['Wkv_d'], 'L0_xattn_Wv_u': _L0_xattn_in['Wv_u'], 'L0_ffn_weight_q': _L0_ffn_in['weight_q'], 'L0_ffn_scale': _L0_ffn_in['scale'], 'L0_ffn_zero_point': _L0_ffn_in['zero_point'], 'L0_ffn_bias': _L0_ffn_in['bias'], 'L1_xattn_Wq': _L1_xattn_in['Wq'], 'L1_xattn_Wk': _L1_xattn_in['Wk'], 'L1_xattn_Wv': _L1_xattn_in['Wv'], 'L1_xattn_Wo': _L1_xattn_in['Wo'], 'L1_ffn_W': _L1_ffn_in['W'], 'L1_ffn_b': _L1_ffn_in['b'], 'L1_ffn_A': _L1_ffn_in['A'], 'L1_ffn_Bmat': _L1_ffn_in['Bmat'], 'L1_ffn_LiMEs': _L1_ffn_in['LiMEs']}

def reference(x, ctx_4096, L0_xattn_Wq_d, L0_xattn_W_qk, L0_xattn_Wkv_d, L0_xattn_Wv_u, L0_ffn_weight_q, L0_ffn_scale, L0_ffn_zero_point, L0_ffn_bias, L1_xattn_Wq, L1_xattn_Wk, L1_xattn_Wv, L1_xattn_Wo, L1_ffn_W, L1_ffn_b, L1_ffn_A, L1_ffn_Bmat, L1_ffn_LiMEs):
    import jax
    import jax.numpy as jnp

    def _L0_xattn_ref(Q, K, Wq_d, W_qk, Wkv_d, Wv_u):
        import jax, jax.numpy as jnp
        import numpy as np
        B, N, NKV = (2, 256, 256)
        E = 512
        H = 16
        HD = E // H
        LQ = E // 8
        LKV = E // 16
        b, n, _ = Q.shape
        nkv = K.shape[1]
        C_q = Q @ Wq_d
        C_kv = K @ Wkv_d
        CqWqk = (C_q @ W_qk).reshape(b, n, H, LKV)
        scores = jnp.einsum('bnhl,bkl->bhnk', CqWqk, C_kv) / jnp.sqrt(jnp.asarray(LKV, dtype=Q.dtype))
        attn = jax.nn.softmax(scores, axis=-1)
        V_up = (C_kv @ Wv_u).reshape(b, nkv, H, HD)
        out = jnp.einsum('bhnk,bkhd->bnhd', attn, V_up)
        return out.reshape(b, n, H * HD)

    def _L0_ffn_ref(x, weight_q, scale, zero_point, bias):
        import jax, jax.numpy as jnp
        import numpy as np
        GROUP_SIZE = 128

        def dequantize_int4(weight_q, scale, zero_point, group_size):
            out_f, in_f = weight_q.shape
            n_groups = in_f // group_size
            w = weight_q.astype(jnp.float32).reshape(out_f, n_groups, group_size)
            w = (w - zero_point[:, :, None]) * scale[:, :, None]
            return w.reshape(out_f, in_f)
        w = dequantize_int4(weight_q, scale, zero_point, GROUP_SIZE).astype(x.dtype)
        return jnp.einsum('bsi,oi->bso', x, w) + bias

    def _L1_xattn_ref(latents, context, Wq, Wk, Wv, Wo):
        import jax, jax.numpy as jnp
        import numpy as np
        B, Q, D = (8, 64, 512)
        CTX = 512
        H, KV, HD = (16, 4, 96)
        G = H // KV
        b, q_len, _ = latents.shape
        hidden = jnp.concatenate([context, latents], axis=1)
        s_len = hidden.shape[1]
        q = (latents @ Wq.T).reshape(b, q_len, H, HD)
        k = (hidden @ Wk.T).reshape(b, s_len, KV, HD)
        v = (hidden @ Wv.T).reshape(b, s_len, KV, HD)
        q = q.transpose(0, 2, 1, 3).reshape(b, KV, G, q_len, HD)
        k = k.transpose(0, 2, 1, 3)
        v = v.transpose(0, 2, 1, 3)
        scale = 1.0 / jnp.sqrt(jnp.asarray(HD, q.dtype))
        scores = jnp.einsum('bkgqd,bksd->bkgqs', q, k) * scale
        attn = jax.nn.softmax(scores.astype(jnp.float32), axis=-1).astype(q.dtype)
        out = jnp.einsum('bkgqs,bksd->bkgqd', attn, v)
        out = out.reshape(b, H, q_len, HD).transpose(0, 2, 1, 3).reshape(b, q_len, H * HD)
        return out @ Wo.T

    def _L1_ffn_ref(x, W, b, A, Bmat, LiMEs):
        import jax, jax.numpy as jnp
        import numpy as np
        NUM_EXPERTS = 8
        RANK = 32
        ALPHA = 16.0
        TOP_K = 2
        TEMPERATURE = 1.0
        GAMMA = 0.5
        SOFT_TOPK_TEMP = 0.5
        N_GRAM = 2
        EPS = 1e-06
        Bsz, T, d_in = x.shape
        E = LiMEs.shape[0]
        scaling = ALPHA / RANK
        H = jnp.einsum('btd,od->bto', x, W) + b
        z = jnp.einsum('btd,dr->btr', x, A)
        anchors = jnp.arange(N_GRAM - 1, T, N_GRAM)
        H_slice = H[:, anchors, :E]
        delta_slice = jnp.einsum('bar,er->bae', z[:, anchors], LiMEs)
        H_scale = jnp.maximum(jnp.max(jnp.abs(H_slice)), EPS)
        d_scale = jnp.maximum(jnp.max(jnp.abs(delta_slice)), EPS)
        logits = ((1.0 - GAMMA) * (H_slice / H_scale) + GAMMA * (delta_slice / d_scale)) / TEMPERATURE
        probs = jax.nn.softmax(logits, axis=-1)
        topk_vals, _ = jax.lax.top_k(probs, TOP_K)
        thresh = topk_vals[..., -1:]
        mask = jax.nn.sigmoid((probs - thresh) / SOFT_TOPK_TEMP)
        weights = probs * mask
        weights = weights / (jnp.sum(weights, axis=-1, keepdims=True) + 1e-09)
        weights_full = jnp.repeat(weights, N_GRAM, axis=1)
        p_mix = jnp.einsum('bte,er->btr', weights_full, LiMEs)
        delta = jnp.einsum('btr,ro->bto', z * p_mix, Bmat) * scaling
        return H + delta
    x = x + _L0_xattn_ref(_layernorm(x, axis=-1), ctx_4096, L0_xattn_Wq_d, L0_xattn_W_qk, L0_xattn_Wkv_d, L0_xattn_Wv_u)
    x = x + _L0_ffn_ref(_layernorm(x, axis=-1), L0_ffn_weight_q, L0_ffn_scale, L0_ffn_zero_point, L0_ffn_bias)
    x = x + _L1_xattn_ref(_layernorm(x, axis=-1), ctx_4096, L1_xattn_Wq, L1_xattn_Wk, L1_xattn_Wv, L1_xattn_Wo)
    x = x + _L1_ffn_ref(_layernorm(x, axis=-1), L1_ffn_W, L1_ffn_b, L1_ffn_A, L1_ffn_Bmat, L1_ffn_LiMEs)
    return x

_drawn_inputs = setup_inputs


def setup_inputs(seed=0):
    import zlib

    import numpy as np

    out = dict(_drawn_inputs(seed))
    spreads = {}
    factors = {'L1_xattn_Wq': 8.0,
     'L1_xattn_Wk': 8.0,
     'L1_ffn_b': 8.0,
     'L1_ffn_A': 8.0,
     'L1_ffn_Bmat': 8.0,
     'L1_ffn_LiMEs': 8.0}
    for name, (base, spread) in spreads.items():
        noise = np.random.default_rng([zlib.crc32(name.encode()), seed]).standard_normal(out[name].shape)
        drawn = base * np.exp(spread * noise) if base else spread * noise
        out[name] = jnp.asarray(drawn.astype(out[name].dtype))
    for name, factor in factors.items():
        out[name] = (out[name] * factor).astype(out[name].dtype)
    return out
```

```python
from contextlib import ExitStack

import concourse.bass as bass
from concourse import mybir

F32 = mybir.dt.float32
F32R = mybir.dt.float32r
I32 = mybir.dt.int32
ALU = mybir.AluOpType
ACT = mybir.ActivationFunctionType
AX = mybir.AxisListType.X
ds = bass.ds

P = 128
BANK = 512
B, T, D = 4, 256, 512
NC = 1601
DC = D // P
TT = T // P
EPS = 1e-5

H0, HD0, LQ = 16, 32, 64
S0 = float(HD0) ** -0.5
H1, KV1, HD1 = 16, 4, 96
S1 = float(HD1) ** -0.5
G = 4
NG = H0 // G
GC = G * T
QT = GC // P
R, NE = 32, 8
ONE = 1
RSQRT_GUESS = float(0x5F3759DF)


def widths(total, parts):
    w = total // parts
    cuts = [(i * w, w) for i in range(parts - 1)] + [((parts - 1) * w, total - (parts - 1) * w)]
    return [(s, n, n + n % 2) for s, n in cuts]


class Chain:

    def __init__(self, engine, sem, per, b=0):
        self.engine, self.sem, self.n = engine, sem, 0
        self.base = b * per + ONE if per else 0

    def mark(self, ins):
        self.n += 1
        ins.then_inc(self.sem, 1)

    def link(self, ins):
        self.mark(ins)
        self.engine.wait_ge(self.sem, self.base + self.n)


def layernorm(dve, chain, out, x, st, mv, v, t, u, y):
    chain.link(dve.bn_stats(st[:, 0, :], x[:, 0, :]))
    chain.mark(dve.bn_stats(st[:, 1, :], x[:, 1, :]))
    chain.link(dve.bn_aggr(mv[:, 0, :], st[:, 0, :]))
    chain.mark(dve.tensor_scalar(v[:, 0:1], mv[:, 0, 1:2], EPS, None, ALU.add))
    chain.link(dve.bn_aggr(mv[:, 1, :], st[:, 1, :]))
    chain.link(dve.tensor_scalar(v[:, 1:2], mv[:, 1, 1:2], EPS, None, ALU.add))
    chain.link(dve.tensor_scalar(t[:, :].bitcast(I32), v[:, :].bitcast(I32), 1, None, ALU.logical_shift_right))
    chain.link(dve.tensor_scalar(y[:, :].bitcast(I32), t[:, :].bitcast(I32), -1.0, RSQRT_GUESS, ALU.mult, ALU.add))
    for _ in range(3):
        chain.link(dve.tensor_tensor(t[:, :], y[:, :], y[:, :], ALU.mult))
        chain.link(dve.scalar_tensor_tensor(u[:, :], t[:, :], -0.5, v[:, :], ALU.mult, ALU.mult))
        chain.link(dve.scalar_tensor_tensor(y[:, :], u[:, :], 1.5, y[:, :], ALU.add, ALU.mult))
    last = None
    for i in range(TT):
        last = dve.tensor_scalar(out[:, i, :], x[:, i, :], mv[:, i, 0:1], y[:, i:i + 1], ALU.subtract, ALU.mult)
        if i < TT - 1:
            chain.link(last)
    return last


LN_STEPS = 6 + 2 + 9 + TT - 1


def build(nc, A, out):
    q_scr = nc.dram_tensor("q_scr", (B, NG, 2, HD1, GC), F32, kind="Internal").ap()
    x_scr = nc.dram_tensor("x_scr", (B, P, TT * D), F32, kind="Internal").ap()
    lt_scr = nc.dram_tensor("lt_scr", (B, P, DC * T), F32, kind="Internal").ap()
    y_scr = nc.dram_tensor("y_scr", (B, P, TT * D), F32, kind="Internal").ap()
    z_scr = nc.dram_tensor("z_scr", (B, R, T), F32, kind="Internal").ap()
    with ExitStack() as ctx:
        ident = ctx.enter_context(nc.sbuf_tensor("ident", [P, P], F32))
        ps = ctx.enter_context(nc.psum_tensor("ps", [P, 8 * BANK], F32))
        ln = {n: ctx.enter_context(nc.sbuf_tensor(f"ln_{n}", s, F32)) for n, s in
              (("st", [P, TT, 6]), ("mv", [P, TT, 2]), ("v", [P, TT]), ("t", [P, TT]), ("u", [P, TT]), ("y", [P, TT]))}
        latent_attention_and_ffn(nc, A, ident, ps, ln, q_scr, x_scr, lt_scr)
        wkvh = ctx.enter_context(nc.sbuf_tensor("wkvh", [P, DC, 2 * KV1 * HD1], F32R))
        wkvl = ctx.enter_context(nc.sbuf_tensor("wkvl", [P, DC, 2 * KV1 * HD1], F32R))
        woT = ctx.enter_context(nc.sbuf_tensor("woT", [HD1, H1, D], F32))
        w1T = ctx.enter_context(nc.sbuf_tensor("w1T", [P, DC, D], F32))
        h8all = ctx.enter_context(nc.sbuf_tensor("h8all", [P, B, NE], F32))
        dlall = ctx.enter_context(nc.sbuf_tensor("dlall", [P, B, NE], F32))
        turn_weights(nc, A, ident, ps, wkvh, wkvl, woT, w1T)
        grouped_attention(nc, A, ident, ps, ln, q_scr, x_scr, lt_scr, y_scr, z_scr,
                          wkvh, wkvl, woT, w1T, h8all, dlall)
        mixture(nc, A, ident, ps, y_scr, z_scr, h8all, dlall, out)


def latent_attention_and_ffn(nc, A, ident, ps, ln, q_scr, x_scr, lt_scr):
    NP = 4
    rows = [BANK, BANK, BANK, NC - 3 * BANK]
    KT = -(-NC // P)
    last_rows = NC - (KT - 1) * P
    keys = [P] * (KT - 1) + [last_rows]
    cuts = widths(NC, 4)
    NI = QT * len(cuts)
    per_step = -(-NI // (KT - 2))
    HW = HD0 + 1
    DVE_STEPS = 3 * LN_STEPS + NG * (1 + TT * 2 - 1) + 2

    with ExitStack() as ctx:
        def sb(name, shape, dt=F32):
            return ctx.enter_context(nc.sbuf_tensor(name, shape, dt))

        def sem(name):
            return ctx.enter_context(nc.semaphore(name))

        in_loop = []

        def counted(name):
            in_loop.append(sem(name))
            return in_loop[-1]

        wqn = sb("wqn", [P, H1 * HD1 // P, D])
        w0i = sb("w0i", [P, DC, D], I32)
        w0n = sb("w0n", [P, DC, D])
        w0s = sb("w0s", [P, DC, D // P])
        w0z = sb("w0z", [P, DC, D // P])
        bias0 = sb("bias0", [P, D])
        wqd = sb("wqd", [P, DC, LQ])
        wqk = sb("wqk", [LQ, H0, 3 * HD0])
        wkv = sb("wkv", [P, DC, 3 * HD0])
        wvu = sb("wvu", [P, NG * 2, 2, HW])
        w0T = sb("w0T", [P, DC, D])
        wqT = sb("wqT", [P, DC, H1 * HD1])
        x = sb("x", [P, TT, D])
        xh = sb("xh", [P, TT, D])
        xT = sb("xT", [P, DC, T])
        cnat = sb("cnat", [P, 2, 4, D])
        cT = sb("cT", [P, DC, BANK])
        cst = sb("cst", [HD1 + 1, NC + 1], F32R)
        cf = sb("cf", [HD0, BANK])
        cv = sb("cv", [P, KT, 64])
        cq = sb("cq", [LQ, T])
        ast = sb("ast", [HD1 + 1, H0 * T], F32R)
        pr = sb("pr", [P, 2, GC])
        osb = sb("osb", [P, BANK])
        pm = sb("pm", [P, QT, len(cuts)])
        mx = sb("mx", [P, QT])
        rec = sb("rec", [P, TT * G])
        tmp = sb("tmp", [P, TT, G * HD0])
        qst = sb("qst", [HD1, 2, 2, BANK], F32R)

        const = sem("const")
        w_q, w_0, w_small = sem("w_q_loaded"), sem("w_0_loaded"), sem("w_small_loaded")
        w_deq, w_tp, w_ev = sem("w_dequantised"), sem("w_turned"), sem("w_copied")
        x_in = counted("x_in")
        ctx_in = [counted("ctx_in0"), counted("ctx_in1")]
        ctx_tp, c_mm, cnat_tp = counted("ctx_turned"), counted("c_product"), counted("c_turned")
        ctxT_a, ctxT_d = counted("ctxT_by_act"), counted("ctxT_by_dve")
        cf_done, cst_done, cv_done = counted("c_copied"), counted("c_split"), counted("cv_copied")
        xh_done, xT_tp, xT_a, xT_d = counted("xh_ready"), counted("x_turned"), counted("xT_by_act"), counted("xT_by_dve")
        cq_mm, cq_done, a_mm, ahi, alo = counted("cq_product"), counted("cq_copied"), counted("a_product"), counted("a_hi"), counted("a_lo")
        mx_mm, mx_done, mxr_done = counted("max_scores"), counted("max_part"), counted("max_ready")
        row_mm, row_done = counted("max_turned"), counted("max_row")
        s_mm, exp_done, av_mm, o_done = counted("scores"), counted("probs"), counted("values"), counted("o_copied")
        bd_mm, post_done = counted("o_turned"), counted("x_attended")
        ffn_mm, ffn_done = counted("ffn_product"), counted("ffn_added")
        q_mm, qhi, qlo = counted("q_product"), counted("q_hi"), counted("q_lo")
        q_st = [counted("q_stored0"), counted("q_stored1")]
        x1_st = counted("x1_stored")
        step = counted("dve_step")
        block = ctx.enter_context(nc.Block())

        def bank(i, n=BANK):
            return ps[:, i * BANK:i * BANK + n]

        OB, M0, M2 = 4, 5, 7

        @block.sync
        def _(sp):
            sp.dma_start(w0i[:, :, :], A["L0_ffn_weight_q"].rearrange("(a p) i -> p a i", p=P)).then_inc(w_0, 16)
            sp.dma_start(w0s[:, :, :], A["L0_ffn_scale"].rearrange("(a p) i -> p a i", p=P)).then_inc(w_0, 16)
            sp.dma_start(w0z[:, :, :], A["L0_ffn_zero_point"].rearrange("(a p) i -> p a i", p=P)).then_inc(w_0, 16)
            sp.dma_start(wqn[:, :, :], A["L1_xattn_Wq"].rearrange("(a p) i -> p a i", p=P)).then_inc(w_q, 16)
            sp.wait_ge(const, 3)
            sp.dma_start(bias0[:, :], A["L0_ffn_bias"].rearrange("(a n) -> a n", a=1).to_broadcast([P, D]))\
                .then_inc(w_small, 16)
            sp.dma_start(wqd[:, :, :], A["L0_xattn_Wq_d"].rearrange("(c p) n -> p c n", p=P)).then_inc(w_small, 16)
            for r in range(3):
                sp.dma_start(wqk[:, :, r * HD0:(r + 1) * HD0],
                             A["L0_xattn_W_qk"].rearrange("l (h e) -> l h e", e=HD0)).then_inc(w_small, 16)
                sp.dma_start(wkv[:, :, r * HD0:(r + 1) * HD0],
                             A["L0_xattn_Wkv_d"].rearrange("(c p) n -> p c n", p=P)).then_inc(w_small, 16)
            up = A["L0_xattn_Wv_u"].rearrange("l (g h c e) -> l h g c e", g=NG, h=2, c=2)
            for h in range(2):
                for c in range(2):
                    sp.dma_start(wvu[64 * h:64 * h + HD0, c:2 * NG:2, h, 0:HD0], up[:, h, :, c, :])\
                        .then_inc(w_small, 16)
            with sp.Fori(0, B) as b:
                for p in range(NP):
                    sp.wait_ge(ctx_tp, ONE + b * 16 + 4 * max(p - 1, 0))
                    n = -(-rows[p] // P)
                    r0 = p * BANK
                    if rows[p] == BANK:
                        src = A["ctx_4096"][ds(b, 1), r0:r0 + BANK, :].rearrange("o (a p) d -> p (o a) d", p=P)
                        sp.dma_start(cnat[:, p % 2, :, :], src).then_inc(ctx_in[p % 2], 16)
                    else:
                        src = A["ctx_4096"][ds(b, 1), r0:r0 + rows[p], :].rearrange("o p d -> p (o d)")
                        sp.dma_start(cnat[0:rows[p], p % 2, 0, :], src).then_inc(ctx_in[p % 2], 16)
                    if p == 1:
                        sp.wait_ge(x1_st, ONE + b * 32)
                        sp.dma_start(x[:, :, :], A["x"][ds(b, 1), :, :].rearrange("o (t p) d -> p (o t) d", p=P))\
                            .then_inc(x_in, 16)
            sp.wait_ge(x1_st, ONE + B * 32)
            sp.wait_ge(q_st[0], ONE + B * 128)
            sp.wait_ge(q_st[1], ONE + B * 128)

        @block.gpsimd
        def _(pool):
            for s in in_loop:
                pool.sem_inc(s, ONE)
            ready = Chain(pool, const, 0)
            ready.link(pool.memset(ident[:, :], 0.0))
            ready.link(pool.affine_select(out=ident[:, :], in_=ident[:, :], compare_op=ALU.not_equal, fill=1.0,
                                          base=0, pattern=[[-1, P]], channel_multiplier=1))
            ready.link(pool.memset(wvu[:, :, :, :], 0.0))
            for h in range(2):
                ready.link(pool.memset(wvu[64 * h + HD0:64 * h + HW, :, h, HD0:HW], 1.0))
            ready.link(pool.memset(cst[HD1:HD1 + 1, :].bitcast(F32), 1.0))
            ready.link(pool.memset(cst[0:HD1, NC:NC + 1].bitcast(F32), 0.0))
            ready.link(pool.memset(cv[:, :, HD0:64], 0.0))
            ready.link(pool.memset(cv[:, :, HD0:HW], 1.0))

        @block.tensor
        def _(pe):
            pe.wait_ge(const, 9)
            pe.wait_ge(w_deq, 1)
            for n in range(4 + 12):
                if n == 4:
                    pe.wait_ge(w_q, 16)
                if n >= 2:
                    pe.wait_ge(w_ev, n - 1)
                for c in range(DC):
                    src = w0n[:, n, c * P:(c + 1) * P] if n < 4 else wqn[:, n - 4, c * P:(c + 1) * P]
                    tp = pe.transpose(ps[:, (n % 2) * BANK + c * P:(n % 2) * BANK + (c + 1) * P], src, ident[:, :])
                tp.then_inc(w_tp, 1)
            pe.wait_ge(w_ev, 16)
            pe.wait_ge(w_small, 16 * 12)

            with pe.Fori(0, B) as b:
                def turn_ctx(p):
                    pe.wait_ge(ctx_in[p % 2], ONE + b * 32 + 16 * (p // 2 + 1))
                    pe.wait_ge(ctxT_a, ONE + b * 8 + 2 * p)
                    pe.wait_ge(ctxT_d, ONE + b * 8 + 2 * p)
                    for c in range(DC):
                        for t in range(-(-rows[p] // P)):
                            m = min(P, rows[p] - t * P)
                            tp = pe.transpose(ps[:, c * BANK + t * P:c * BANK + t * P + m],
                                              cnat[0:m, p % 2, t, c * P:(c + 1) * P], ident[0:m, 0:m])
                        tp.then_inc(ctx_tp, 1)

                def c_product(p):
                    pe.wait_ge(ctxT_a, ONE + b * 8 + 2 * p + 2)
                    pe.wait_ge(ctxT_d, ONE + b * 8 + 2 * p + 2)
                    if p == 0:
                        pe.wait_ge(qlo, ONE + b * 8)
                    pe.wait_ge(cst_done, ONE + b * 4 + p)
                    for c in range(DC):
                        mm = pe.matmul(bank(M0)[0:HD1, 0:rows[p]], wkv[:, c, :], cT[:, c, 0:rows[p]],
                                       start=(c == 0), stop=(c == DC - 1))
                    mm.then_inc(c_mm, 1)

                def turn_c(p):
                    pe.wait_ge(cf_done, ONE + b * 4 + p + 1)
                    pe.wait_ge(cv_done, ONE + b * 4 + p)
                    for t in range(-(-rows[p] // P)):
                        m = min(P, rows[p] - t * P)
                        tp = pe.matmul(bank(M0 + 1)[0:m, t * HD0:(t + 1) * HD0], cf[:, t * P:t * P + m],
                                       ident[0:HD0, 0:HD0], start=True, stop=True)
                    tp.then_inc(cnat_tp, 1)

                def turn_x(k):
                    pe.wait_ge(xh_done, ONE + b * 3 + k + 1)
                    for half in range(2):
                        for c in range(2):
                            for t in range(TT):
                                tp = pe.transpose(bank(M0 + half)[:, c * T + t * P:c * T + (t + 1) * P],
                                                  xh[:, t, (2 * half + c) * P:(2 * half + c + 1) * P], ident[:, :])
                        tp.then_inc(xT_tp, 1)
                    pe.wait_ge(xT_a, ONE + b * 3 + k + 1)
                    pe.wait_ge(xT_d, ONE + b * 3 + k + 1)

                turn_ctx(0)
                for p in range(NP):
                    c_product(p)
                    if p + 1 < NP:
                        turn_ctx(p + 1)
                    turn_c(p)
                pe.wait_ge(cst_done, ONE + b * 4 + 4)
                pe.wait_ge(cv_done, ONE + b * 4 + 4)

                turn_x(0)
                pe.wait_ge(post_done, ONE + b * 4)
                for c in range(DC):
                    mm = pe.matmul(bank(M2)[0:LQ, 0:T], wqd[:, c, :], xT[:, c, :], start=(c == 0), stop=(c == DC - 1))
                mm.then_inc(cq_mm, 1)
                pe.wait_ge(cq_done, ONE + b + 1)
                for hp in range(8):
                    if hp >= 2:
                        pe.wait_ge(alo, ONE + b * 8 + hp - 1)
                    for j in range(2):
                        mm = pe.matmul(bank(M0 + hp % 2)[0:HD1, j * T:(j + 1) * T], wqk[:, 2 * hp + j, :], cq[:, :],
                                       start=True, stop=True)
                    mm.then_inc(a_mm, 1)
                pe.wait_ge(alo, ONE + b * 8 + 8)

                def max_item(g, i):
                    n = g * NI + i
                    if i < 2:
                        pe.wait_ge(row_done, ONE + b * 8 + 2 * g)
                    if n >= 2:
                        pe.wait_ge(mx_done, ONE + b * NG * NI + n - 1)
                    j, (k0, _, k) = i // len(cuts), cuts[i % len(cuts)]
                    pe.matmul(bank(M0 + i % 2)[:, 0:k], ast[0:HD1, g * GC + j * P:g * GC + (j + 1) * P],
                              cst[0:HD1, k0:k0 + k], start=True, stop=True).then_inc(mx_mm, 1)

                def max_rows(g):
                    pe.wait_ge(mxr_done, ONE + b * NG + g + 1)
                    for half in range(2):
                        for j in range(4):
                            mm = pe.matmul(bank(M0 + half)[HD1:HD1 + 1, j * P:(j + 1) * P],
                                           mx[:, 4 * half + j:4 * half + j + 1], ident[:, :], start=True, stop=True)
                        mm.then_inc(row_mm, 1)

                def scores(g, kt):
                    n = g * KT + kt
                    if kt == 0:
                        pe.wait_ge(row_done, ONE + b * 8 + 2 * g + 2)
                    if n >= 2:
                        pe.wait_ge(exp_done, ONE + b * NG * KT + n - 1)
                    for half in range(2):
                        mm = pe.matmul(ps[0:keys[kt], ((n % 2) * 2 + half) * BANK:((n % 2) * 2 + half + 1) * BANK],
                                       cst[0:HD1 + 1, kt * P:kt * P + keys[kt]],
                                       ast[:, g * GC + half * BANK:g * GC + (half + 1) * BANK], start=True, stop=True)
                    mm.then_inc(s_mm, 1)

                def values(g, kt):
                    n = g * KT + kt
                    if kt == 0:
                        pe.wait_ge(o_done, ONE + b * NG + g)
                    pe.wait_ge(exp_done, ONE + b * NG * KT + n + 1)
                    for half in range(2):
                        mm = pe.matmul(bank(OB)[64 * half:64 * half + 64, :], cv[0:keys[kt], kt, :],
                                       pr[0:keys[kt], n % 2, half * BANK:(half + 1) * BANK],
                                       start=(kt == 0), stop=(kt == KT - 1))
                    mm.then_inc(av_mm, 1)

                def raise_values(g):
                    pe.wait_ge(o_done, ONE + b * NG + g + 1)
                    pe.wait_ge(post_done, ONE + b * NG + g)
                    for t in range(TT):
                        for c in range(2):
                            mm = pe.matmul(bank(M2)[:, (t * 2 + c) * 2 * HW:(t * 2 + c + 1) * 2 * HW],
                                           osb[:, c * T + t * P:c * T + (t + 1) * P],
                                           wvu[:, 2 * g + c, :, :].rearrange("p h e -> p (h e)"),
                                           start=True, stop=True)
                    mm.then_inc(bd_mm, 1)

                for i in range(NI):
                    max_item(0, i)
                max_rows(0)
                for g in range(NG):
                    scores(g, 0)
                    for kt in range(KT):
                        if kt + 1 < KT:
                            scores(g, kt + 1)
                        if g + 1 < NG:
                            for i in range(kt * per_step, min(NI, (kt + 1) * per_step)):
                                max_item(g + 1, i)
                            if kt == KT - 2:
                                max_rows(g + 1)
                        if kt == 2 and g > 0:
                            raise_values(g - 1)
                        values(g, kt)
                raise_values(NG - 1)

                turn_x(1)
                for t in range(TT):
                    for c in range(DC):
                        mm = pe.matmul(bank(M0 + t), xT[:, c, t * P:(t + 1) * P], w0T[:, c, :],
                                       start=(c == 0), stop=(c == DC - 1))
                    mm.then_inc(ffn_mm, 1)
                turn_x(2)
                for hp in range(8):
                    if hp >= 2:
                        pe.wait_ge(qlo, ONE + b * 8 + hp - 1)
                    for j in range(2):
                        h = 2 * hp + j
                        for c in range(DC):
                            mm = pe.matmul(bank(M0 + hp % 2)[0:HD1, j * T:(j + 1) * T],
                                           wqT[:, c, h * HD1:(h + 1) * HD1], xT[:, c, :],
                                           start=(c == 0), stop=(c == DC - 1))
                    mm.then_inc(q_mm, 1)

        @block.scalar
        def _(act):
            for n in range(0, 16, 2):
                act.wait_ge(w_tp, n + 1)
                if n:
                    act.wait_ge(w_ev, n)
                dst = w0T[:, :, n * P:(n + 1) * P] if n < 4 else wqT[:, :, (n - 4) * P:(n - 3) * P]
                act.copy(dst, bank(0).rearrange("p (c m) -> p c m", c=DC)).then_inc(w_ev, 1)
            with act.Fori(0, B) as b:
                def turned_ctx(p):
                    for i, c in enumerate((0, 2)):
                        act.wait_ge(ctx_tp, ONE + b * 16 + 4 * p + c + 1)
                        act.wait_ge(c_mm, ONE + b * 4 + p)
                        act.copy(cT[:, c, 0:rows[p]], bank(c, rows[p])).then_inc(ctxT_a, 1)

                def turned_x(k, wait):
                    act.wait_ge(xT_tp, ONE + b * 6 + 2 * k + 1)
                    for s, v in wait:
                        act.wait_ge(s, v)
                    act.copy(xT[:, 0:2, :], bank(M0).rearrange("p (c m) -> p c m", c=2)).then_inc(xT_a, 1)

                turned_ctx(0)
                for p in range(NP):
                    act.wait_ge(c_mm, ONE + b * 4 + p + 1)
                    act.copy(cst[0:HD1, p * BANK:p * BANK + rows[p]], bank(M0)[0:HD1, 0:rows[p]])
                    act.wait_ge(cnat_tp, ONE + b * 4 + p)
                    act.copy(cf[:, 0:rows[p]], bank(M0)[0:HD0, 0:rows[p]]).then_inc(cf_done, 1)
                    if p + 1 < NP:
                        turned_ctx(p + 1)
                turned_x(0, [(q_mm, ONE + b * 8), (x1_st, ONE + b * 32)])
                act.wait_ge(cq_mm, ONE + b + 1)
                act.copy(cq[:, :], bank(M2)[0:LQ, 0:T]).then_inc(cq_done, 1)
                for hp in range(8):
                    act.wait_ge(a_mm, ONE + b * 8 + hp + 1)
                    act.copy(ast[0:HD1, hp * BANK:(hp + 1) * BANK], bank(M0 + hp % 2)[0:HD1, :]).then_inc(ahi, 1)

                def rows_of(g):
                    for half in range(2):
                        act.wait_ge(row_mm, ONE + b * 8 + 2 * g + half + 1)
                        act.mul(ast[HD1:HD1 + 1, g * GC + half * BANK:g * GC + (half + 1) * BANK],
                                bank(M0 + half)[HD1:HD1 + 1, :], -1.0).then_inc(row_done, 1)

                def store_q(hp):
                    act.wait_ge(qhi, ONE + b * 8 + hp + 1)
                    act.wait_ge(qlo, ONE + b * 8 + hp + 1)
                    for part in range(2):
                        dst = q_scr[ds(b, 1), hp // 2, part, :, (hp % 2) * BANK:(hp % 2 + 1) * BANK]
                        act.dma_start(dst.rearrange("o p n -> p (o n)"), qst[:, hp % 2, part, :].bitcast(F32))\
                            .then_inc(q_st[hp % 2], 16)

                rows_of(0)
                for g in range(NG):
                    for kt in range(KT):
                        n = g * KT + kt
                        if kt == KT - 1 and g + 1 < NG:
                            rows_of(g + 1)
                        act.wait_ge(s_mm, ONE + b * NG * KT + n + 1)
                        act.wait_ge(av_mm, ONE + b * NG * KT + max(n - 1, 0))
                        act.activation(pr[0:keys[kt], n % 2, :],
                                       ps[0:keys[kt], (n % 2) * 2 * BANK:((n % 2) * 2 + 2) * BANK],
                                       ACT.Exp, scale=S0).then_inc(exp_done, 1)
                    act.wait_ge(av_mm, ONE + b * NG * KT + (g + 1) * KT)
                    act.wait_ge(bd_mm, ONE + b * NG + g)
                    act.copy(osb[:, :], bank(OB)).then_inc(o_done, 1)
                turned_x(1, [(cq_mm, ONE + b + 1)])
                turned_x(2, [(ffn_mm, ONE + b * 2 + 2)])
                for hp in range(8):
                    act.wait_ge(q_mm, ONE + b * 8 + hp + 1)
                    act.wait_ge(q_st[hp % 2], ONE + b * 128 + 32 * (hp // 2))
                    act.copy(qst[:, hp % 2, 0, :], bank(M0 + hp % 2)[0:HD1, :]).then_inc(qhi, 1)
                    if hp:
                        store_q(hp - 1)
                store_q(7)
                act.wait_ge(xT_d, ONE + b * 3 + 3)
                act.wait_ge(xT_a, ONE + b * 3 + 3)
                act.wait_ge(ffn_done, ONE + b * 2 + 2)
                act.wait_ge(step, ONE + (b + 1) * DVE_STEPS)
                act.dma_start(x_scr[ds(b, 1), :, :].rearrange("o p n -> p (o n)"),
                              x[:, :, :].rearrange("p a b -> p (a b)")).then_inc(x1_st, 16)
                act.dma_start(lt_scr[ds(b, 1), :, :].rearrange("o p n -> p (o n)"),
                              xT[:, :, :].rearrange("p a b -> p (a b)")).then_inc(x1_st, 16)

        @block.vector
        def _(dve):
            dve.wait_ge(w_0, 48)
            for o in range(DC):
                for i in range(DC):
                    last = dve.tensor_scalar(w0n[:, o, i * P:(i + 1) * P], w0i[:, o, i * P:(i + 1) * P],
                                             w0z[:, o, i:i + 1], w0s[:, o, i:i + 1], ALU.subtract, ALU.mult)
            last.then_inc(w_deq, 1)
            for n in range(1, 16, 2):
                dve.wait_ge(w_tp, n + 1)
                dve.wait_ge(w_ev, n)
                dst = w0T[:, :, n * P:(n + 1) * P] if n < 4 else wqT[:, :, (n - 4) * P:(n - 3) * P]
                dve.tensor_copy(dst, bank(1).rearrange("p (c m) -> p c m", c=DC)).then_inc(w_ev, 1)
            dve.wait_ge(const, 9)
            dve.wait_ge(w_small, 192)
            with dve.Fori(0, B) as b:
                chain = Chain(dve, step, DVE_STEPS, b)

                def turned_ctx(p):
                    for i, c in enumerate((1, 3)):
                        dve.wait_ge(ctx_tp, ONE + b * 16 + 4 * p + c + 1)
                        dve.wait_ge(c_mm, ONE + b * 4 + p)
                        dve.tensor_copy(cT[:, c, 0:rows[p]], bank(c, rows[p])).then_inc(ctxT_d, 1)

                def normalise(k):
                    dve.wait_ge(xT_tp, ONE + b * 6 + 2 * k)
                    layernorm(dve, chain, xh, x, ln["st"], ln["mv"], ln["v"], ln["t"], ln["u"], ln["y"])\
                        .then_inc(xh_done, 1)

                def turned_x(k, wait):
                    dve.wait_ge(xT_tp, ONE + b * 6 + 2 * k + 2)
                    for s, v in wait:
                        dve.wait_ge(s, v)
                    dve.tensor_copy(xT[:, 2:4, :], bank(M0 + 1).rearrange("p (c m) -> p c m", c=2)).then_inc(xT_d, 1)

                turned_ctx(0)
                for p in range(NP):
                    c0 = p * BANK
                    dve.wait_ge(cf_done, ONE + b * 4 + p + 1)
                    dve.tensor_tensor(cst[HD0:2 * HD0, c0:c0 + rows[p]], bank(M0)[HD0:2 * HD0, 0:rows[p]],
                                      cst[HD0:2 * HD0, c0:c0 + rows[p]], ALU.subtract).then_inc(cst_done, 1)
                    if p + 1 < NP:
                        turned_ctx(p + 1)
                    dve.wait_ge(cnat_tp, ONE + b * 4 + p + 1)
                    nt, m = -(-rows[p] // P), min(P, rows[p])
                    dve.tensor_copy(cv[0:m, 4 * p:4 * p + nt, 0:HD0],
                                    bank(M0 + 1)[0:m, 0:nt * HD0].rearrange("p (t e) -> p t e", e=HD0))\
                        .then_inc(cv_done, 1)
                    if p == 2:
                        dve.wait_ge(x_in, ONE + b * 16 + 16)
                        normalise(0)
                turned_x(0, [(q_mm, ONE + b * 8), (x1_st, ONE + b * 32)])
                for hp in range(8):
                    dve.wait_ge(ahi, ONE + b * 8 + hp + 1)
                    lo = ast[2 * HD0:3 * HD0, hp * BANK:(hp + 1) * BANK]
                    dve.tensor_tensor(lo, bank(M0 + hp % 2)[2 * HD0:3 * HD0, :], lo, ALU.subtract).then_inc(alo, 1)

                def max_part(g, i):
                    n = g * NI + i
                    if i == 0:
                        dve.wait_ge(mxr_done, ONE + b * NG + g)
                    dve.wait_ge(mx_mm, ONE + b * NG * NI + n + 1)
                    j, ch = i // len(cuts), i % len(cuts)
                    dve.reduce_max(pm[:, j, ch:ch + 1], bank(M0 + i % 2)[:, 0:cuts[ch][1]], AX).then_inc(mx_done, 1)

                def max_all(g):
                    dve.wait_ge(mx_done, ONE + b * NG * NI + (g + 1) * NI)
                    dve.wait_ge(row_mm, ONE + b * 8 + 2 * g)
                    dve.reduce_max(mx[:, :], pm[:, :, :], AX).then_inc(mxr_done, 1)

                def attended(g):
                    dve.wait_ge(bd_mm, ONE + b * NG + g + 1)
                    o = bank(M2)[:, 0:TT * G * HW].rearrange("p (t c h e) -> p t c h e", t=TT, c=2, h=2)
                    r = rec[:, :].rearrange("p (t c h e) -> p t c h e", t=TT, c=2, e=1)
                    chain.link(dve.reciprocal(rec[:, :], bank(M2)[:, 0:TT * G * HW]
                                              .rearrange("p (n e) -> p n e", e=HW)[:, :, HD0]))
                    for t in range(TT):
                        xs = x[:, t, g * P:(g + 1) * P].rearrange("p (h c e) -> p c h e", h=2, c=2)
                        tm = tmp[:, t, :].rearrange("p (c h e) -> p c h e", c=2, h=2)
                        chain.link(dve.tensor_tensor(tm, o[:, t, :, :, 0:HD0],
                                                     r[:, t].broadcast_to([P, 2, 2, HD0]), ALU.mult))
                        last = dve.tensor_tensor(xs, xs, tm, ALU.add)
                        if t < TT - 1:
                            chain.link(last)
                    last.then_inc(post_done, 1)
                    dve.wait_ge(post_done, ONE + b * NG + g + 1)

                for i in range(NI):
                    max_part(0, i)
                max_all(0)
                for g in range(NG):
                    for kt in range(KT):
                        if g + 1 < NG:
                            for i in range(kt * per_step, min(NI, (kt + 1) * per_step)):
                                max_part(g + 1, i)
                            if kt == KT - 3:
                                max_all(g + 1)
                        if kt == 2 and g > 0:
                            attended(g - 1)
                attended(NG - 1)
                normalise(1)
                turned_x(1, [(cq_mm, ONE + b + 1)])
                for t in range(TT):
                    dve.wait_ge(ffn_mm, ONE + b * 2 + t + 1)
                    dve.tensor_tensor(x[:, t, :], bank(M0 + t), x[:, t, :], ALU.add).then_inc(ffn_done, 1)
                    dve.wait_ge(ffn_done, ONE + b * 2 + t + 1)
                    chain.link(dve.tensor_tensor(x[:, t, :], x[:, t, :], bias0[:, :], ALU.add))
                normalise(2)
                turned_x(2, [(ffn_mm, ONE + b * 2 + 2)])
                for hp in range(8):
                    dve.wait_ge(qhi, ONE + b * 8 + hp + 1)
                    dve.tensor_tensor(qst[:, hp % 2, 1, :], bank(M0 + hp % 2)[0:HD1, :], qst[:, hp % 2, 0, :],
                                      ALU.subtract).then_inc(qlo, 1)
                assert chain.n == DVE_STEPS, (chain.n, DVE_STEPS)


def turn_weights(nc, A, ident, ps, wkvh, wkvl, woT, w1T):
    with ExitStack() as ctx:
        def sem(name):
            return ctx.enter_context(nc.semaphore(name))

        W = KV1 * HD1
        wk = ctx.enter_context(nc.sbuf_tensor("wk_rows", [P, 2, W // P, D], F32))
        wo = ctx.enter_context(nc.sbuf_tensor("wo_rows", [P, DC, H1 * HD1], F32))
        w1 = ctx.enter_context(nc.sbuf_tensor("w1_rows", [P, DC, D], F32))
        kv_in, w1_in, wo_in = sem("kv_rows_in"), sem("w1_rows_in"), sem("wo_rows_in")
        tp, hi, done = sem("rows_turned"), sem("rows_hi"), sem("rows_copied")
        NKV = 2 * W // P
        block = ctx.enter_context(nc.Block())

        def bank(i):
            return ps[:, i * BANK:(i + 1) * BANK]

        N = NKV + DC + H1

        @block.sync
        def _(sp):
            for i, name in enumerate(("L1_xattn_Wk", "L1_xattn_Wv")):
                sp.dma_start(wk[:, i, :, :], A[name].rearrange("(a p) i -> p a i", p=P)).then_inc(kv_in, 16)
            sp.dma_start(w1[:, :, :], A["L1_ffn_W"].rearrange("(a p) i -> p a i", p=P)).then_inc(w1_in, 16)
            sp.dma_start(wo[:, :, :], A["L1_xattn_Wo"].rearrange("(a p) i -> p a i", p=P)).then_inc(wo_in, 16)

        @block.tensor
        def _(pe):
            for n in range(N):
                if n in (0, NKV, NKV + DC):
                    s, v = {0: (kv_in, 32), NKV: (w1_in, 16), NKV + DC: (wo_in, 16)}[n]
                    pe.wait_ge(s, v)
                if n >= 2:
                    pe.wait_ge(done, n - 1)
                for c in range(DC):
                    if n < NKV:
                        src = wk[:, n // 3, n % 3, c * P:(c + 1) * P]
                    elif n < NKV + DC:
                        src = w1[:, n - NKV, c * P:(c + 1) * P]
                    else:
                        h = n - NKV - DC
                        src = wo[:, c, h * HD1:(h + 1) * HD1]
                    m = pe.transpose(bank(n % 2)[0:src.shape[1], c * P:(c + 1) * P], src, ident[:, :])
                m.then_inc(tp, 1)

        @block.scalar
        def _(act):
            for n in range(N):
                act.wait_ge(tp, n + 1)
                src = bank(n % 2).rearrange("p (c m) -> p c m", c=DC)
                if n < NKV:
                    act.copy(wkvh[:, :, n * P:(n + 1) * P], src).then_inc(hi, 1)
                elif n % 2:
                    act.wait_ge(done, n)
                    dst = w1T[:, :, (n - NKV) * P:(n - NKV + 1) * P] if n < NKV + DC else woT[:, n - NKV - DC, :]
                    if n >= NKV + DC:
                        src = bank(n % 2)[0:HD1, :]
                    act.copy(dst, src).then_inc(done, 1)

        @block.vector
        def _(dve):
            for n in range(N):
                src = bank(n % 2).rearrange("p (c m) -> p c m", c=DC)
                if n < NKV:
                    dve.wait_ge(hi, n + 1)
                    dve.tensor_tensor(wkvl[:, :, n * P:(n + 1) * P], src, wkvh[:, :, n * P:(n + 1) * P], ALU.subtract)\
                        .then_inc(done, 1)
                elif n % 2 == 0:
                    dve.wait_ge(tp, n + 1)
                    dve.wait_ge(done, n)
                    dst = w1T[:, :, (n - NKV) * P:(n - NKV + 1) * P] if n < NKV + DC else woT[:, n - NKV - DC, :]
                    if n >= NKV + DC:
                        src = bank(n % 2)[0:HD1, :]
                    dve.tensor_copy(dst, src).then_inc(done, 1)


def grouped_attention(nc, A, ident, ps, ln, q_scr, x_scr, lt_scr, y_scr, z_scr, wkvh, wkvl, woT, w1T, h8all, dlall):
    W = KV1 * HD1
    NP = 7
    rows = [T] * 6 + [NC - 5 * T]
    NK = T + NC
    KT = -(-NK // P)
    keys = [P] * (KT - 1) + [NK - (KT - 1) * P]
    cuts = widths(NK, 4)
    NI = QT * len(cuts)
    per_step = -(-NI // (KT - 3))
    XW = rows[-1] + 1
    DVE_STEPS = LN_STEPS + 2

    with ExitStack() as ctx:
        def sb(name, shape, dt=F32):
            return ctx.enter_context(nc.sbuf_tensor(name, shape, dt))

        def sem(name):
            return ctx.enter_context(nc.semaphore(name))

        in_loop = []

        def counted(name):
            in_loop.append(sem(name))
            return in_loop[-1]

        kh = sb("kh", [HD1 + 1, KV1, NK + 1], F32R)
        kl = sb("kl", [HD1, KV1, NK + 1], F32R)
        v = sb("v", [P, KT, KV1, HD1 + 1])
        qh = sb("qh", [HD1 + 1, 2, GC], F32R)
        ql = sb("ql", [HD1, 2, GC], F32R)
        pr = sb("pr1", [P, 2, GC])
        nat = sb("nat", [P, 3, D])
        xh = sb("xTh", [P, DC, XW], F32R)
        xl = sb("xTl", [P, DC, XW], F32R)
        x = sb("x1", [P, TT, D])
        o = sb("o1", [P, GC])
        rb = sb("rb", [HD1 + 1, GC])
        pm = sb("pm1", [P, QT, len(cuts)])
        mx = sb("mx1", [P, QT])
        aw = sb("aw", [P, DC, R])
        liT = sb("liT", [R, NE])
        bias8 = sb("bias8", [P, NE])
        zb = sb("zb", [R, T])
        spare = sb("spare", [1, 2])

        w_small, const = sem("w_small1"), sem("const1")
        x_in, piece_in = counted("x1_in"), counted("piece_in")
        q_in = [counted("q_in0"), counted("q_in1")]
        tp, xh_done, xl_done = counted("piece_turned"), counted("piece_hi"), counted("piece_lo")
        k_mm, khi, klo, v_mm, v_done = counted("k_product"), counted("k_hi"), counted("k_lo"), counted("v_product"), counted("v_copied")
        mx_mm, mx_done, mxr_done = counted("max_scores1"), counted("max_part1"), counted("max_ready1")
        row_mm, row_done = counted("max_turned1"), counted("max_row1")
        s_mm, exp_done, av_mm, o_done = counted("scores1"), counted("probs1"), counted("values1"), counted("o_copied1")
        rec_done, bc_done, on_done = counted("sum_inverted"), counted("sum_spread"), counted("o_scaled")
        wo_mm, post_done = counted("wo_product"), counted("wo_added")
        n_done, xT_tp, xT_a, xT_d = counted("x_normal"), counted("x_turned1"), counted("xT1_by_act"), counted("xT1_by_dve")
        z_mm, z_done, h8_mm, h8_done = counted("z_product"), counted("z_copied"), counted("h8_product"), counted("h8_kept")
        dl_mm, dl_done, h_mm, h_done = counted("dl_product"), counted("dl_kept"), counted("h_product"), counted("h_added")
        y_st, z_st = counted("y_stored"), counted("z_stored")
        step = counted("dve_step1")
        block = ctx.enter_context(nc.Block())
        OB, M0 = 4, 6

        def bank(i, n=BANK):
            return ps[:, i * BANK:i * BANK + n]

        lt = nat[:, :, :].rearrange("p a d -> p (a d)")[:, 0:DC * T].rearrange("p (c m) -> p c m", c=DC)
        xn = o[:, :].rearrange("p (t d) -> p t d", t=TT)
        xT = pr[:, 0, :].rearrange("p (c m) -> p c m", c=DC)

        @block.sync
        def _(sp):
            sp.dma_start(aw[:, :, :], A["L1_ffn_A"].rearrange("(c p) r -> p c r", p=P)).then_inc(w_small, 16)
            with nc.allow_non_contiguous_dma(reason="256 values"):
                sp.dma_start(liT[:, :], A["L1_ffn_LiMEs"].rearrange("e r -> r e")).then_inc(w_small, 16)
            sp.dma_start(bias8[:, :], A["L1_ffn_b"][0:NE].rearrange("(a n) -> a n", a=1).to_broadcast([P, NE]))\
                .then_inc(w_small, 16)
            with sp.Fori(0, B) as b:
                def load_q(kv):
                    for part, q in ((0, qh[0:HD1, kv % 2, :]), (1, ql[:, kv % 2, :])):
                        sp.dma_start(q.bitcast(F32), q_scr[ds(b, 1), kv, part, :, :].rearrange("o p n -> p (o n)"))\
                            .then_inc(q_in[kv % 2], 16)

                sp.wait_ge(tp, ONE + b * 4 * (NP - 1))
                sp.dma_start(lt, lt_scr[ds(b, 1), :, :].rearrange("o p (c m) -> p (o c) m", c=DC))\
                    .then_inc(piece_in, 16)
                for p in range(1, NP):
                    if p == 1:
                        sp.wait_ge(xl_done, ONE + b * NP + 1)
                    else:
                        sp.wait_ge(tp, ONE + b * 4 * (NP - 1) + 4 * (p - 1))
                    r0 = (p - 1) * T
                    n2 = 2 * P
                    src = A["ctx_4096"][ds(b, 1), r0:r0 + n2, :].rearrange("o (a p) d -> p (o a) d", p=P)
                    sp.dma_start(nat[:, 0:2, :], src).then_inc(piece_in, 16)
                    if rows[p] > n2:
                        src = A["ctx_4096"][ds(b, 1), r0 + n2:r0 + rows[p], :].rearrange("o p d -> p (o d)")
                        sp.dma_start(nat[0:rows[p] - n2, 2, :], src).then_inc(piece_in, 16)
                    if p == 1:
                        sp.wait_ge(av_mm, ONE + b * KV1 * KT)
                        load_q(0)
                        load_q(1)
                        sp.wait_ge(y_st, ONE + b * 16)
                        sp.dma_start(x[:, :, :].rearrange("p a b -> p (a b)"),
                                     x_scr[ds(b, 1), :, :].rearrange("o p n -> p (o n)")).then_inc(x_in, 16)
                for kv in (2, 3):
                    sp.wait_ge(av_mm, ONE + b * KV1 * KT + (kv - 1) * KT)
                    load_q(kv)
            sp.wait_ge(y_st, ONE + B * 16)
            sp.wait_ge(z_st, ONE + B * 16)

        @block.gpsimd
        def _(pool):
            for s in in_loop:
                pool.sem_inc(s, ONE)
            ready = Chain(pool, const, 0)
            ready.link(pool.memset(spare[:, :], 0.0))
            ready.link(pool.memset(kh[HD1:HD1 + 1, :, :].bitcast(F32), 1.0))
            ready.link(pool.memset(xh[:, :, XW - 1:XW].bitcast(F32), 0.0))
            ready.link(pool.memset(xl[:, :, XW - 1:XW].bitcast(F32), 0.0))
            ready.link(pool.memset(v[:, :, :, HD1:HD1 + 1], 1.0))
            with pool.Fori(0, B) as b:
                for kv in range(KV1):
                    pool.wait_ge(rec_done, ONE + b * KV1 + kv + 1)
                    pool.wait_ge(on_done, ONE + b * KV1 + kv)
                    pool.tensor_tensor(spare[:, 1:2], spare[:, 0:1], spare[:, 0:1], ALU.add)
                    pool.partition_broadcast(rb[0:HD1, :], rb[HD1:HD1 + 1, :], channels=HD1).then_inc(bc_done, 1)

        @block.tensor
        def _(pe):
            pe.wait_ge(w_small, 48)
            pe.wait_ge(const, 5)
            with pe.Fori(0, B) as b:
                def turn(p):
                    pe.wait_ge(piece_in, ONE + b * 16 * (NP + 1) + 16 * (p + 1) + (16 if rows[p] > T else 0))
                    pe.wait_ge(xl_done, ONE + b * NP + p)
                    for c in range(DC):
                        for t in range(-(-rows[p] // P)):
                            m = min(P, rows[p] - t * P)
                            mm = pe.transpose(bank(c)[:, t * P:t * P + m], nat[0:m, t, c * P:(c + 1) * P],
                                              ident[0:m, 0:m])
                        mm.then_inc(tp, 1)

                def three(out, lhs, rhs):
                    n = 0
                    for l, r in ((0, 0), (1, 0), (0, 1)):
                        for c in range(DC):
                            mm = pe.matmul(out, lhs(l, c), rhs(r, c), start=(n == 0), stop=(n == 3 * DC - 1))
                            n += 1
                    return mm

                def project(p):
                    pe.wait_ge(xl_done, ONE + b * NP + p + 1)
                    n = rows[p] + rows[p] % 2
                    for kv in range(KV1):
                        i = p * KV1 + kv
                        if i >= 2:
                            pe.wait_ge(klo, ONE + b * NP * KV1 + i - 1)
                        three(bank(OB + i % 2)[0:HD1, 0:n],
                              lambda l, c: (wkvh, wkvl)[l][:, c, kv * HD1:(kv + 1) * HD1],
                              lambda r, c: (xh, xl)[r][:, c, 0:n]).then_inc(k_mm, 1)
                    for t in range(-(-rows[p] // P)):
                        i, m = 2 * p + t, min(P, rows[p] - t * P)
                        if i >= 2:
                            pe.wait_ge(v_done, ONE + b * KT + i - 1)
                        elif i == 0:
                            pe.wait_ge(h_done, ONE + b * TT)
                        three(bank(M0 + i % 2)[0:m, 0:W],
                              lambda l, c: (xh, xl)[l][:, c, t * P:t * P + m],
                              lambda r, c: (wkvh, wkvl)[r][:, c, W:2 * W]).then_inc(v_mm, 1)

                pe.wait_ge(o_done, ONE + b * KV1 * 2)
                for p in range(NP):
                    if p + 1 < NP:
                        turn(p + 1)
                    project(p)
                pe.wait_ge(klo, ONE + (b + 1) * NP * KV1)
                pe.wait_ge(v_done, ONE + (b + 1) * KT)

                def max_item(kv, i):
                    n = kv * NI + i
                    if i == 0:
                        pe.wait_ge(q_in[kv % 2], ONE + b * 64 + 32 * (kv // 2 + 1))
                    if i < 2:
                        pe.wait_ge(row_done, ONE + b * 2 * KV1 + 2 * kv)
                    if n >= 2:
                        pe.wait_ge(mx_done, ONE + b * KV1 * NI + n - 1)
                    j, (k0, _, k) = i // len(cuts), cuts[i % len(cuts)]
                    pe.matmul(bank(M0 + i % 2)[:, 0:k], qh[0:HD1, kv % 2, j * P:(j + 1) * P],
                              kh[0:HD1, kv, k0:k0 + k], start=True, stop=True).then_inc(mx_mm, 1)

                def max_rows(kv):
                    pe.wait_ge(mxr_done, ONE + b * KV1 + kv + 1)
                    for half in range(2):
                        for j in range(4):
                            mm = pe.matmul(bank(M0 + half)[HD1:HD1 + 1, j * P:(j + 1) * P],
                                           mx[:, 4 * half + j:4 * half + j + 1], ident[:, :], start=True, stop=True)
                        mm.then_inc(row_mm, 1)

                def scores(kv, kt):
                    n = kv * KT + kt
                    if kt == 0:
                        pe.wait_ge(row_done, ONE + b * 2 * KV1 + 2 * kv + 2)
                    if n >= 2:
                        pe.wait_ge(exp_done, ONE + b * KV1 * KT + n - 1)
                    k0, m = kt * P, keys[kt]
                    for half in range(2):
                        out = bank((n % 2) * 2 + half)[0:m, :]
                        cols = slice(half * BANK, (half + 1) * BANK)
                        pe.matmul(out, kh[:, kv, k0:k0 + m], qh[:, kv % 2, cols], start=True, stop=False)
                        pe.matmul(out, kl[:, kv, k0:k0 + m], qh[0:HD1, kv % 2, cols], start=False, stop=False)
                        mm = pe.matmul(out, kh[0:HD1, kv, k0:k0 + m], ql[:, kv % 2, cols], start=False, stop=True)
                    mm.then_inc(s_mm, 1)

                def values(kv, kt):
                    n = kv * KT + kt
                    if kt == 0:
                        pe.wait_ge(o_done, ONE + b * 2 * KV1 + 2 * kv)
                    pe.wait_ge(exp_done, ONE + b * KV1 * KT + n + 1)
                    for half in range(2):
                        mm = pe.matmul(bank(OB + half)[0:HD1 + 1, :], v[0:keys[kt], kt, kv, :],
                                       pr[0:keys[kt], n % 2, half * BANK:(half + 1) * BANK],
                                       start=(kt == 0), stop=(kt == KT - 1))
                    mm.then_inc(av_mm, 1)

                def wo_product(kv, items):
                    pe.wait_ge(on_done, ONE + b * KV1 + kv + 1)
                    pe.wait_ge(mx_done, ONE + b * KV1 * NI + items)
                    for t in range(TT):
                        for h in range(G):
                            mm = pe.matmul(bank(M0 + t), o[0:HD1, h * T + t * P:h * T + (t + 1) * P],
                                           woT[:, kv * G + h, :], start=(h == 0), stop=(h == G - 1))
                        mm.then_inc(wo_mm, 1)

                for i in range(NI):
                    max_item(0, i)
                max_rows(0)
                for kv in range(KV1):
                    scores(kv, 0)
                    for kt in range(KT):
                        if kt + 1 < KT:
                            scores(kv, kt + 1)
                        if kv + 1 < KV1:
                            for i in range(kt * per_step, min(NI, (kt + 1) * per_step)):
                                if kt == 4 and kv > 0 and i == kt * per_step:
                                    pe.wait_ge(post_done, ONE + b * KV1 * TT + kv * TT)
                                max_item(kv + 1, i)
                            if kt == KT - 2:
                                max_rows(kv + 1)
                        if kt == 3 and kv > 0:
                            last = kv + 1 < KV1
                            wo_product(kv - 1, (kv + 1) * NI + 4 * per_step if last else KV1 * NI)
                        values(kv, kt)
                wo_product(KV1 - 1, KV1 * NI)

                pe.wait_ge(n_done, ONE + b + 1)
                for half in range(2):
                    for c in range(2):
                        for t in range(TT):
                            mm = pe.transpose(bank(M0 + half)[:, c * T + t * P:c * T + (t + 1) * P],
                                              xn[:, t, (2 * half + c) * P:(2 * half + c + 1) * P], ident[:, :])
                    mm.then_inc(xT_tp, 1)
                pe.wait_ge(xT_a, ONE + b + 1)
                pe.wait_ge(xT_d, ONE + b + 1)
                for c in range(DC):
                    mm = pe.matmul(bank(OB)[0:R, 0:T], aw[:, c, :], xT[:, c, :], start=(c == 0), stop=(c == DC - 1))
                mm.then_inc(z_mm, 1)
                for c in range(DC):
                    mm = pe.matmul(bank(OB + 1)[:, 0:NE], xT[:, c, 1:T:2], w1T[:, c, 0:NE],
                                   start=(c == 0), stop=(c == DC - 1))
                mm.then_inc(h8_mm, 1)
                for t in range(TT):
                    for c in range(DC):
                        mm = pe.matmul(bank(M0 + t), xT[:, c, t * P:(t + 1) * P], w1T[:, c, :],
                                       start=(c == 0), stop=(c == DC - 1))
                    mm.then_inc(h_mm, 1)
                pe.wait_ge(z_done, ONE + b + 1)
                pe.wait_ge(exp_done, ONE + (b + 1) * KV1 * KT)
                pe.matmul(bank(0)[:, 0:NE], zb[:, 1:T:2], liT[:, :], start=True, stop=True).then_inc(dl_mm, 1)
                pe.wait_ge(h8_done, ONE + b + 1)
                pe.wait_ge(dl_done, ONE + b + 1)

        @block.scalar
        def _(act):
            with act.Fori(0, B) as b:
                def banks(n):
                    return ps[:, 0:DC * BANK].rearrange("p (c m) -> p c m", c=DC)[:, :, 0:n]

                for p in range(NP):
                    if p == 0:
                        act.wait_ge(piece_in, ONE + b * 16 * (NP + 1) + 16)
                        act.wait_ge(v_mm, ONE + b * KT)
                        act.copy(xh[:, :, 0:rows[p]], lt).then_inc(xh_done, 1)
                    for kv in range(KV1):
                        i = p * KV1 + kv
                        n = rows[p] + rows[p] % 2
                        c0 = p * T
                        act.wait_ge(k_mm, ONE + b * NP * KV1 + i + 1)
                        act.copy(kh[0:HD1, kv, c0:c0 + n], bank(OB + i % 2)[0:HD1, 0:n]).then_inc(khi, 1)
                    for t in range(-(-rows[p] // P)):
                        i, m = 2 * p + t, min(P, rows[p] - t * P)
                        act.wait_ge(v_mm, ONE + b * KT + i + 1)
                        act.copy(v[0:m, i, :, 0:HD1], bank(M0 + i % 2)[0:m, 0:W].rearrange("p (k e) -> p k e", e=HD1))\
                            .then_inc(v_done, 1)
                    if p + 1 < NP:
                        act.wait_ge(tp, ONE + b * 4 * (NP - 1) + 4 * (p + 1))
                        act.copy(xh[:, :, 0:rows[p + 1]], banks(rows[p + 1])).then_inc(xh_done, 1)

                def rows_of(kv):
                    for half in range(2):
                        act.wait_ge(row_mm, ONE + b * 2 * KV1 + 2 * kv + half + 1)
                        act.mul(qh[HD1:HD1 + 1, kv % 2, half * BANK:(half + 1) * BANK],
                                bank(M0 + half)[HD1:HD1 + 1, :], -1.0).then_inc(row_done, 1)

                rows_of(0)
                for kv in range(KV1):
                    for kt in range(KT):
                        n = kv * KT + kt
                        if kt == KT - 1 and kv + 1 < KV1:
                            rows_of(kv + 1)
                        act.wait_ge(s_mm, ONE + b * KV1 * KT + n + 1)
                        act.wait_ge(av_mm, ONE + b * KV1 * KT + max(n - 1, 0))
                        act.activation(pr[0:keys[kt], n % 2, :],
                                       ps[0:keys[kt], (n % 2) * 2 * BANK:((n % 2) * 2 + 2) * BANK],
                                       ACT.Exp, scale=S1).then_inc(exp_done, 1)
                    act.wait_ge(av_mm, ONE + b * KV1 * KT + (kv + 1) * KT)
                    act.wait_ge(wo_mm, ONE + b * KV1 * TT + kv * TT)
                    for half in range(2):
                        act.copy(o[0:HD1 + 1, half * BANK:(half + 1) * BANK], bank(OB + half)[0:HD1 + 1, :])\
                            .then_inc(o_done, 1)
                act.wait_ge(xT_tp, ONE + b * 2 + 1)
                act.copy(xT[:, 0:2, :], bank(M0).rearrange("p (c m) -> p c m", c=2)).then_inc(xT_a, 1)
                act.wait_ge(z_mm, ONE + b + 1)
                act.wait_ge(z_st, ONE + b * 16)
                act.copy(zb[:, :], bank(OB)[0:R, 0:T]).then_inc(z_done, 1)
                act.wait_ge(z_done, ONE + b + 1)
                act.dma_start(z_scr[ds(b, 1), :, :].rearrange("o p n -> p (o n)"), zb[:, :]).then_inc(z_st, 16)
                act.wait_ge(h_done, ONE + b * TT + TT)
                act.dma_start(y_scr[ds(b, 1), :, :].rearrange("o p n -> p (o n)"),
                              x[:, :, :].rearrange("p a b -> p (a b)")).then_inc(y_st, 16)

        @block.vector
        def _(dve):
            with dve.Fori(0, B) as b:
                chain = Chain(dve, step, DVE_STEPS, b)

                def banks(n):
                    return ps[:, 0:DC * BANK].rearrange("p (c m) -> p c m", c=DC)[:, :, 0:n]

                for p in range(NP):
                    if p == 0:
                        dve.wait_ge(xh_done, ONE + b * NP + 1)
                        dve.tensor_tensor(xl[:, :, 0:rows[p]], lt, xh[:, :, 0:rows[p]].bitcast(F32), ALU.subtract)\
                            .then_inc(xl_done, 1)
                    for kv in range(KV1):
                        i = p * KV1 + kv
                        n = rows[p] + rows[p] % 2
                        c0 = p * T
                        dve.wait_ge(khi, ONE + b * NP * KV1 + i + 1)
                        dve.tensor_tensor(kl[:, kv, c0:c0 + n], bank(OB + i % 2)[0:HD1, 0:n], kh[0:HD1, kv, c0:c0 + n],
                                          ALU.subtract).then_inc(klo, 1)
                    if p + 1 < NP:
                        dve.wait_ge(xh_done, ONE + b * NP + p + 2)
                        dve.tensor_tensor(xl[:, :, 0:rows[p + 1]], banks(rows[p + 1]), xh[:, :, 0:rows[p + 1]],
                                          ALU.subtract).then_inc(xl_done, 1)

                def max_part(kv, i):
                    n = kv * NI + i
                    if i == 0:
                        dve.wait_ge(mxr_done, ONE + b * KV1 + kv)
                    dve.wait_ge(mx_mm, ONE + b * KV1 * NI + n + 1)
                    j, ch = i // len(cuts), i % len(cuts)
                    dve.reduce_max(pm[:, j, ch:ch + 1], bank(M0 + i % 2)[:, 0:cuts[ch][1]], AX).then_inc(mx_done, 1)

                def max_all(kv):
                    dve.wait_ge(mx_done, ONE + b * KV1 * NI + (kv + 1) * NI)
                    dve.wait_ge(row_mm, ONE + b * 2 * KV1 + 2 * kv)
                    dve.reduce_max(mx[:, :], pm[:, :, :], AX).then_inc(mxr_done, 1)

                def invert(kv):
                    dve.wait_ge(o_done, ONE + b * 2 * KV1 + 2 * kv + 2)
                    dve.wait_ge(on_done, ONE + b * KV1 + kv)
                    dve.reciprocal(rb[HD1:HD1 + 1, :], o[HD1:HD1 + 1, :]).then_inc(rec_done, 1)

                def scale(kv):
                    dve.wait_ge(bc_done, ONE + b * KV1 + kv + 1)
                    dve.tensor_tensor(o[0:HD1, :], o[0:HD1, :], rb[0:HD1, :], ALU.mult).then_inc(on_done, 1)

                def add_wo(kv):
                    for t in range(TT):
                        dve.wait_ge(wo_mm, ONE + b * KV1 * TT + kv * TT + t + 1)
                        if kv == 0:
                            dve.wait_ge(x_in, ONE + b * 16 + 16)
                        else:
                            dve.wait_ge(post_done, ONE + b * KV1 * TT + kv * TT)
                        dve.tensor_tensor(x[:, t, :], bank(M0 + t), x[:, t, :], ALU.add).then_inc(post_done, 1)

                for i in range(NI):
                    max_part(0, i)
                max_all(0)
                for kv in range(KV1):
                    for kt in range(KT):
                        if kt == 0 and kv > 0:
                            invert(kv - 1)
                        if kv + 1 < KV1:
                            for i in range(kt * per_step, min(NI, (kt + 1) * per_step)):
                                max_part(kv + 1, i)
                            if kt == KT - 3:
                                max_all(kv + 1)
                        if kt == 1 and kv > 0:
                            scale(kv - 1)
                        if kt == 3 and kv > 0:
                            add_wo(kv - 1)
                invert(KV1 - 1)
                scale(KV1 - 1)
                add_wo(KV1 - 1)
                dve.wait_ge(post_done, ONE + (b + 1) * KV1 * TT)
                layernorm(dve, chain, xn, x, ln["st"], ln["mv"], ln["v"], ln["t"], ln["u"], ln["y"])\
                    .then_inc(n_done, 1)
                dve.wait_ge(xT_tp, ONE + b * 2 + 2)
                dve.tensor_copy(xT[:, 2:4, :], bank(M0 + 1).rearrange("p (c m) -> p c m", c=2)).then_inc(xT_d, 1)
                dve.wait_ge(h8_mm, ONE + b + 1)
                dve.tensor_tensor(h8all[:, ds(b, 1), :].rearrange("p o e -> p (o e)"), bank(OB + 1)[:, 0:NE],
                                  bias8[:, :], ALU.add).then_inc(h8_done, 1)
                for t in range(TT):
                    dve.wait_ge(h_mm, ONE + b * TT + t + 1)
                    dve.tensor_tensor(x[:, t, :], bank(M0 + t), x[:, t, :], ALU.add).then_inc(h_done, 1)
                dve.wait_ge(dl_mm, ONE + b + 1)
                dve.tensor_copy(dlall[:, ds(b, 1), :].rearrange("p o e -> p (o e)"), bank(0)[:, 0:NE])\
                    .then_inc(dl_done, 1)
                for _ in range(DVE_STEPS - chain.n):
                    chain.link(dve.memset(ln["t"][:, :], 0.0))


def mixture(nc, A, ident, ps, y_scr, z_scr, h8all, dlall, out):
    NA = B * NE
    with ExitStack() as ctx:
        def sb(name, shape, dt=F32):
            return ctx.enter_context(nc.sbuf_tensor(name, shape, dt))

        def sem(name):
            return ctx.enter_context(nc.semaphore(name))

        y = sb("y", [P, B, TT, D])
        z = sb("z", [R, B, T])
        zp = sb("zp", [R + 1, B, T])
        li = sb("li", [NE, R])
        bm = sb("bm", [R + 1, D])
        ones = sb("ones", [2, P])
        ab = sb("ab", [P, 2, NA])
        pmx = sb("pmx", [P, 2])
        rows2 = sb("rows2", [2, P])
        sc = sb("sc", [2, 4])
        dg = sb("dg", [2, 2])
        scl = sb("scl", [P, 2])
        lg = sb("lg", [P, B, NE])
        pb = sb("pb", [P, B, NE])
        top = sb("top", [P, B, NE])
        wt = sb("wt", [P, B, NE])
        r4 = sb("r4", [P, B])
        wT = sb("wT", [NE, B * P])
        y_in, z_in, w_in, const = sem("y_in"), sem("z_in"), sem("w_in"), sem("const2")
        step, a_in, a_out = sem("dve_step2"), sem("act_asked"), sem("act_done")
        to_pe, from_pe = sem("pe_asked"), sem("pe_done")
        zp_done, d_mm, y_done, o_st = sem("zp_ready"), sem("delta_product"), sem("y_ready"), sem("out_stored")
        block = ctx.enter_context(nc.Block())

        def bank(i, n=BANK):
            return ps[:, i * BANK:i * BANK + n]

        @block.sync
        def _(sp):
            sp.dma_start(bm[0:R, :], A["L1_ffn_Bmat"]).then_inc(w_in, 16)
            sp.dma_start(bm[R:R + 1, :], A["L1_ffn_b"].rearrange("(a n) -> a n", a=1)).then_inc(w_in, 16)
            sp.dma_start(li[:, :], A["L1_ffn_LiMEs"]).then_inc(w_in, 16)
            sp.dma_start(z[:, :, :], z_scr.rearrange("b r t -> r b t")).then_inc(z_in, 16)
            sp.dma_start(y[:, :, :, :].rearrange("p b t d -> p b (t d)"), y_scr.rearrange("b p n -> p b n"))\
                .then_inc(y_in, 16)
            for b in range(B):
                sp.wait_ge(y_done, (b + 1) * TT)
                sp.dma_start(out[b].rearrange("(t p) d -> p t d", p=P), y[:, b, :, :]).then_inc(o_st, 16)
            sp.wait_ge(o_st, 16 * B)

        @block.gpsimd
        def _(pool):
            pool.memset(ones[:, :], 1.0).then_inc(const, 1)
            pool.memset(zp[R:R + 1, :, :], 1.0).then_inc(const, 1)

        @block.tensor
        def _(pe):
            pe.wait_ge(const, 2)
            pe.wait_ge(to_pe, 1)
            pe.matmul(bank(0)[0:2, 0:P], pmx[:, :], ident[:, :], start=True, stop=True).then_inc(from_pe, 1)
            pe.wait_ge(to_pe, 2)
            pe.matmul(bank(1)[:, 0:2], ones[:, :], dg[:, :], start=True, stop=True).then_inc(from_pe, 1)
            pe.wait_ge(to_pe, 3)
            for b in range(B):
                mm = pe.matmul(bank(2)[0:NE, b * P:(b + 1) * P], wt[:, b, :], ident[:, :], start=True, stop=True)
            mm.then_inc(from_pe, 1)
            pe.wait_ge(to_pe, 4)
            pe.wait_ge(w_in, 48)
            pe.matmul(bank(3)[0:R, :], li[:, :], wT[:, :], start=True, stop=True).then_inc(from_pe, 1)
            pe.wait_ge(zp_done, 2)
            for n in range(B * TT):
                if n >= 4:
                    pe.wait_ge(y_done, n - 3)
                b, t = n // TT, n % TT
                pe.matmul(bank(4 + n % 4), zp[:, b, t * P:(t + 1) * P], bm[:, :], start=True, stop=True)\
                    .then_inc(d_mm, 1)

        @block.scalar
        def _(act):
            act.wait_ge(a_in, 1)
            act.activation(pb[:, :, :], lg[:, :, :], ACT.Exp).then_inc(a_out, 1)
            act.wait_ge(a_in, 2)
            act.activation(wt[:, :, :], lg[:, :, :], ACT.Exp, scale=-2.0).then_inc(a_out, 1)

        @block.vector
        def _(dve):
            chain = Chain(dve, step, 0)
            link = chain.link
            flat = "p b e -> p (b e)"
            for i, s in enumerate((h8all, dlall)):
                sf = s[:, :, :].rearrange(flat)
                link(dve.scalar_tensor_tensor(ab[:, i, :], sf, -1.0, sf, ALU.mult, ALU.max))
            dve.reduce_max(pmx[:, :], ab[:, :, :], AX).then_inc(to_pe, 1)
            dve.wait_ge(from_pe, 1)
            link(dve.reduce_max(sc[:, 0:1], bank(0)[0:2, 0:P], AX))
            link(dve.tensor_scalar(sc[:, 1:2], sc[:, 0:1], 1e-6, None, ALU.max))
            link(dve.reciprocal(sc[:, 2:3], sc[:, 1:2]))
            dve.tensor_scalar(dg[:, :], ident[0:2, 0:2], sc[:, 2:3], 0.5, ALU.mult, ALU.mult).then_inc(to_pe, 1)
            dve.wait_ge(from_pe, 2)
            link(dve.tensor_copy(scl[:, :], bank(1)[:, 0:2]))
            link(dve.tensor_scalar(pb[:, :, :], dlall[:, :, :], scl[:, 1:2], None, ALU.mult))
            link(dve.scalar_tensor_tensor(lg[:, :, :], h8all[:, :, :], scl[:, 0:1], pb[:, :, :], ALU.mult, ALU.add))

            def over(a):
                return a.rearrange("p (b o) -> p b o", o=1).broadcast_to([P, B, NE])

            link(dve.reduce_max(r4[:, :], lg[:, :, :], AX))
            dve.tensor_tensor(lg[:, :, :], lg[:, :, :], over(r4[:, :]), ALU.subtract).then_inc(a_in, 1)
            dve.wait_ge(a_out, 1)
            link(dve.reduce_sum(r4[:, :], pb[:, :, :], AX))
            link(dve.reciprocal(r4[:, :], r4[:, :]))
            link(dve.tensor_tensor(pb[:, :, :], pb[:, :, :], over(r4[:, :]), ALU.mult))
            for b in range(B):
                link(dve.max(top[:, b, :], pb[:, b, :]))
            dve.tensor_tensor(lg[:, :, :], pb[:, :, :], top[:, :, 1:2].broadcast_to([P, B, NE]), ALU.subtract)\
                .then_inc(a_in, 1)
            dve.wait_ge(a_out, 2)
            link(dve.tensor_scalar(wt[:, :, :], wt[:, :, :], 1.0, None, ALU.add))
            link(dve.reciprocal(wt[:, :, :], wt[:, :, :]))
            link(dve.tensor_tensor(wt[:, :, :], wt[:, :, :], pb[:, :, :], ALU.mult))
            link(dve.reduce_sum(r4[:, :], wt[:, :, :], AX))
            link(dve.tensor_scalar(r4[:, :], r4[:, :], 1e-9, None, ALU.add))
            link(dve.reciprocal(r4[:, :], r4[:, :]))
            dve.tensor_tensor(wt[:, :, :], wt[:, :, :], over(r4[:, :]), ALU.mult).then_inc(to_pe, 1)
            dve.wait_ge(from_pe, 3)
            dve.tensor_copy(wT[:, :], bank(2)[0:NE, :]).then_inc(to_pe, 1)
            dve.wait_ge(w_in, 48)
            dve.tensor_scalar(bm[0:R, :], bm[0:R, :], 16.0 / R, None, ALU.mult).then_inc(zp_done, 1)
            dve.wait_ge(from_pe, 4)
            dve.wait_ge(z_in, 16)
            dve.tensor_tensor(zp[0:R, :, :].rearrange("r b (a n) -> r (b a) n", n=2),
                              z[:, :, :].rearrange("r b (a n) -> r (b a) n", n=2),
                              bank(3)[0:R, :].rearrange("r (a o) -> r a o", o=1).broadcast_to([R, BANK, 2]), ALU.mult)\
                .then_inc(zp_done, 1)
            dve.wait_ge(y_in, 16)
            for n in range(B * TT):
                dve.wait_ge(d_mm, n + 1)
                dve.tensor_tensor(y[:, n // TT, n % TT, :], bank(4 + n % 4), y[:, n // TT, n % TT, :], ALU.add)\
                    .then_inc(y_done, 1)


_INS = ["x", "ctx_4096", "L0_xattn_Wq_d", "L0_xattn_W_qk", "L0_xattn_Wkv_d", "L0_xattn_Wv_u", "L0_ffn_weight_q",
        "L0_ffn_scale", "L0_ffn_zero_point", "L0_ffn_bias", "L1_xattn_Wq", "L1_xattn_Wk", "L1_xattn_Wv",
        "L1_xattn_Wo", "L1_ffn_W", "L1_ffn_b", "L1_ffn_A", "L1_ffn_Bmat", "L1_ffn_LiMEs"]


def kernel(**inputs):
    import numpy as _np
    import concourse.bacc as _bacc
    from concourse import mybir as _mybir
    from concourse.bass_utils import run_bass_kernel_spmd as _run

    nc = _bacc.Bacc("TRN2", target_bir_lowering=False, num_devices=1)
    arrays, args = {}, {}
    for name in _INS:
        a = _np.ascontiguousarray(inputs[name])
        arrays[f"in_{name}_dram"] = a
        args[name] = nc.dram_tensor(f"in_{name}_dram", a.shape, _mybir.dt.from_np(a.dtype), kind="ExternalInput").ap()
    out = nc.dram_tensor("out_0_dram", (B, T, D), F32, kind="ExternalOutput").ap()
    build(nc, args, out)
    r = _run(nc, [arrays], core_ids=[0])
    return r.results[0]["out_0_dram"]
```

```python
from contextlib import ExitStack

import concourse.bass as bass
from concourse import mybir

F32 = mybir.dt.float32
F32R = mybir.dt.float32r
I32 = mybir.dt.int32
ALU = mybir.AluOpType
ACT = mybir.ActivationFunctionType
AX = mybir.AxisListType.X
ds = bass.ds

P = 128
BANK = 512
B, T, D = 4, 256, 512
NC = 1601
DC = D // P
TT = T // P
EPS = 1e-5

H0, HD0, LQ = 16, 32, 64
S0 = float(HD0) ** -0.5
H1, KV1, HD1 = 16, 4, 96
S1 = float(HD1) ** -0.5
G = 4
NG = H0 // G
GC = G * T
QT = GC // P
R, NE = 32, 8
ONE = 1
RSQRT_GUESS = float(0x5F3759DF)


def widths(total, parts):
    w = total // parts
    cuts = [(i * w, w) for i in range(parts - 1)] + [((parts - 1) * w, total - (parts - 1) * w)]
    return [(s, n, n + n % 2) for s, n in cuts]


class Chain:

    def __init__(self, engine, sem, per, b=0):
        self.engine, self.sem, self.n = engine, sem, 0
        self.base = b * per + ONE if per else 0

    def mark(self, ins):
        self.n += 1
        ins.then_inc(self.sem, 1)

    def link(self, ins):
        self.mark(ins)
        self.engine.wait_ge(self.sem, self.base + self.n)


def layernorm(dve, chain, out, x, st, mv, v, t, u, y, pause=lambda: None):
    chain.link(dve.bn_stats(st[:, 0, :], x[:, 0, :]))
    chain.mark(dve.bn_stats(st[:, 1, :], x[:, 1, :]))
    chain.link(dve.bn_aggr(mv[:, 0, :], st[:, 0, :]))
    chain.mark(dve.tensor_scalar(v[:, 0:1], mv[:, 0, 1:2], EPS, None, ALU.add))
    chain.link(dve.bn_aggr(mv[:, 1, :], st[:, 1, :]))
    chain.link(dve.tensor_scalar(v[:, 1:2], mv[:, 1, 1:2], EPS, None, ALU.add))
    chain.link(dve.tensor_scalar(t[:, :].bitcast(I32), v[:, :].bitcast(I32), 1, None, ALU.logical_shift_right))
    chain.link(dve.tensor_scalar(y[:, :].bitcast(I32), t[:, :].bitcast(I32), -1.0, RSQRT_GUESS, ALU.mult, ALU.add))
    for _ in range(3):
        pause()
        chain.link(dve.tensor_tensor(t[:, :], y[:, :], y[:, :], ALU.mult))
        chain.link(dve.scalar_tensor_tensor(u[:, :], t[:, :], -0.5, v[:, :], ALU.mult, ALU.mult))
        chain.link(dve.scalar_tensor_tensor(y[:, :], u[:, :], 1.5, y[:, :], ALU.add, ALU.mult))
    last = None
    for i in range(TT):
        last = dve.tensor_scalar(out[:, i, :], x[:, i, :], mv[:, i, 0:1], y[:, i:i + 1], ALU.subtract, ALU.mult)
        if i < TT - 1:
            chain.link(last)
    return last


LN_STEPS = 6 + 2 + 9 + TT - 1


def build(nc, A, out):
    q_scr = nc.dram_tensor("q_scr", (B, NG, 2, HD1, GC), F32, kind="Internal").ap()
    x_scr = nc.dram_tensor("x_scr", (B, P, TT * D), F32, kind="Internal").ap()
    lt_scr = nc.dram_tensor("lt_scr", (B, P, DC * T), F32, kind="Internal").ap()
    y_scr = nc.dram_tensor("y_scr", (B, P, TT * D), F32, kind="Internal").ap()
    z_scr = nc.dram_tensor("z_scr", (B, R, T), F32, kind="Internal").ap()
    with ExitStack() as ctx:
        ident = ctx.enter_context(nc.sbuf_tensor("ident", [P, P], F32))
        ps = ctx.enter_context(nc.psum_tensor("ps", [P, 8 * BANK], F32))
        ln = {n: ctx.enter_context(nc.sbuf_tensor(f"ln_{n}", s, F32)) for n, s in
              (("st", [P, TT, 6]), ("mv", [P, TT, 2]), ("v", [P, TT]), ("t", [P, TT]), ("u", [P, TT]), ("y", [P, TT]))}
        wo_scr = nc.dram_tensor("wo_turned", (H1 // G, HD1, G * D), F32, kind="Internal").ap()
        latent_attention_and_ffn(nc, A, ident, ps, ln, q_scr, x_scr, lt_scr)
        wkvh = ctx.enter_context(nc.sbuf_tensor("wkvh", [P, DC, 2 * KV1 * HD1], F32R))
        wkvl = ctx.enter_context(nc.sbuf_tensor("wkvl", [P, DC, 2 * KV1 * HD1], F32R))
        w1T = ctx.enter_context(nc.sbuf_tensor("w1T", [P, DC, D], F32))
        h8all = ctx.enter_context(nc.sbuf_tensor("h8all", [P, B, NE], F32))
        dlall = ctx.enter_context(nc.sbuf_tensor("dlall", [P, B, NE], F32))
        turn_weights(nc, A, ident, ps, wkvh, wkvl, wo_scr, w1T)
        grouped_attention(nc, A, ident, ps, ln, q_scr, x_scr, lt_scr, y_scr, z_scr,
                          wkvh, wkvl, wo_scr, w1T, h8all, dlall)
        mixture(nc, A, ident, ps, y_scr, z_scr, h8all, dlall, out)


def latent_attention_and_ffn(nc, A, ident, ps, ln, q_scr, x_scr, lt_scr):
    NP = 4
    rows = [BANK, BANK, BANK, NC - 3 * BANK]
    KT = -(-NC // P)
    last_rows = NC - (KT - 1) * P
    keys = [P] * (KT - 1) + [last_rows]
    cuts = widths(NC, 4)
    NI = QT * len(cuts)
    per_step = -(-NI // (KT - 2))
    HW = HD0 + 1
    STEPS_F = 2 * LN_STEPS + NG * (1 + TT * 2 - 1) + 2

    with ExitStack() as ctx:
        def sb(name, shape, dt=F32):
            return ctx.enter_context(nc.sbuf_tensor(name, shape, dt))

        def sem(name):
            return ctx.enter_context(nc.semaphore(name))

        in_loop = []

        def counted(name):
            in_loop.append(sem(name))
            return in_loop[-1]

        wqn = sb("wqn", [P, H1 * HD1 // P, D])
        w0i = sb("w0i", [P, DC, D], I32)
        w0n = sb("w0n", [P, DC, D])
        w0s = sb("w0s", [P, DC, D // P])
        w0z = sb("w0z", [P, DC, D // P])
        bias0 = sb("bias0", [P, D])
        wqd = sb("wqd", [P, DC, LQ])
        wqk = sb("wqk", [LQ, H0, 3 * HD0])
        wkv = sb("wkv", [P, DC, 3 * HD0])
        wvu = sb("wvu", [P, NG * 2, 2, HW])
        w0T = sb("w0T", [P, DC, D])
        wqT = sb("wqT", [P, DC, H1 * HD1])
        xa = sb("xa", [P, TT, D])
        xah = sb("xah", [P, TT, D])
        xaT = sb("xaT", [P, DC, T])
        x = sb("x", [P, TT, D])
        xh = sb("xh", [P, TT, D])
        xT = sb("xT", [P, DC, T])
        cnat = sb("cnat", [P, 2, 4, D])
        cT = sb("cT", [P, DC, BANK])
        cst = sb("cst", [HD1 + 1, NC + 1], F32R)
        cf = sb("cf", [HD0, BANK])
        cv = sb("cv", [P, KT, 64])
        cq = sb("cq", [LQ, T])
        ast = sb("ast", [HD1 + 1, H0 * T], F32R)
        pr = sb("pr", [P, 2, GC])
        osb = sb("osb", [P, BANK])
        pm = sb("pm", [P, QT, len(cuts)])
        mx = sb("mx", [P, QT])
        rec = sb("rec", [P, TT * G])
        tmp = sb("tmp", [P, TT, G * HD0])
        qst = sb("qst", [HD1, 2, 2, BANK], F32R)

        const = sem("const")
        w_q, w_0, w_small = sem("w_q_loaded"), sem("w_0_loaded"), sem("w_small_loaded")
        w_deq, w_tp, w_ev = sem("w_dequantised"), sem("w_turned"), sem("w_copied")
        xa_in, x_in = counted("xa_in"), counted("x_in")
        ctx_in = [counted("ctx_in0"), counted("ctx_in1")]
        ctx_tp, c_mm, cnat_tp = counted("ctx_turned"), counted("c_product"), counted("c_turned")
        ctxT_a, ctxT_d = counted("ctxT_by_act"), counted("ctxT_by_dve")
        cf_done, cst_done, cv_done = counted("c_copied"), counted("c_split"), counted("cv_copied")
        xah_done, xaT_tp, xaT_a, xaT_d = counted("xa_ready"), counted("xa_turned"), counted("xaT_by_act"), counted("xaT_by_dve")
        xh_done, xT_tp, xT_a, xT_d = counted("xh_ready"), counted("x_turned"), counted("xT_by_act"), counted("xT_by_dve")
        cq_mm, cq_done, a_mm = counted("cq_product"), counted("cq_copied"), counted("a_product")
        ahi, alo = counted("a_hi"), counted("a_lo")
        mx_mm, mx_done, mxr_done = counted("max_scores"), counted("max_part"), counted("max_ready")
        row_mm, row_done = counted("max_turned"), counted("max_row")
        s_mm, exp_done, av_mm, o_done = counted("scores"), counted("probs"), counted("values"), counted("o_copied")
        bd_mm, post_done = counted("o_turned"), counted("x_attended")
        ffn_mm, ffn_done = counted("ffn_product"), counted("ffn_added")
        q_mm, qhi, qlo = counted("q_product"), counted("q_hi"), counted("q_lo")
        q_st = [counted("q_stored0"), counted("q_stored1")]
        x1_st = counted("x1_stored")
        step_a, step_f = counted("dve_step_a"), counted("dve_step_f")
        block = ctx.enter_context(nc.Block())

        def bank(i, n=BANK):
            return ps[:, i * BANK:i * BANK + n]

        OB, M0, M2 = 4, 5, 7
        first_cuts = [(p * BANK, rows[p], rows[p] + rows[p] % 2) for p in range(NP)]

        THIRD = 12
        max_bank = [i % 2 if i < THIRD else (i - THIRD) % 3 for i in range(NI)]

        def max_cut(g, i):
            if g == 0:
                return i % QT, i // QT, first_cuts[i // QT], i % 4
            return i // len(cuts), i % len(cuts), cuts[i % len(cuts)], M0 + max_bank[i]


        @block.sync
        def _(sp):
            sp.dma_start(w0i[:, :, :], A["L0_ffn_weight_q"].rearrange("(a p) i -> p a i", p=P)).then_inc(w_0, 16)
            sp.dma_start(w0s[:, :, :], A["L0_ffn_scale"].rearrange("(a p) i -> p a i", p=P)).then_inc(w_0, 16)
            sp.dma_start(w0z[:, :, :], A["L0_ffn_zero_point"].rearrange("(a p) i -> p a i", p=P)).then_inc(w_0, 16)
            sp.dma_start(wqn[:, :, :], A["L1_xattn_Wq"].rearrange("(a p) i -> p a i", p=P)).then_inc(w_q, 16)
            sp.wait_ge(const, 3)
            sp.dma_start(bias0[:, :], A["L0_ffn_bias"].rearrange("(a n) -> a n", a=1).to_broadcast([P, D]))\
                .then_inc(w_small, 16)
            sp.dma_start(wqd[:, :, :], A["L0_xattn_Wq_d"].rearrange("(c p) n -> p c n", p=P)).then_inc(w_small, 16)
            for r in range(3):
                sp.dma_start(wqk[:, :, r * HD0:(r + 1) * HD0],
                             A["L0_xattn_W_qk"].rearrange("l (h e) -> l h e", e=HD0)).then_inc(w_small, 16)
                sp.dma_start(wkv[:, :, r * HD0:(r + 1) * HD0],
                             A["L0_xattn_Wkv_d"].rearrange("(c p) n -> p c n", p=P)).then_inc(w_small, 16)
            up = A["L0_xattn_Wv_u"].rearrange("l (g h c e) -> l h g c e", g=NG, h=2, c=2)
            for h in range(2):
                for c in range(2):
                    sp.dma_start(wvu[64 * h:64 * h + HD0, c:2 * NG:2, h, 0:HD0], up[:, h, :, c, :])\
                        .then_inc(w_small, 16)
            with sp.Fori(0, B) as b:
                for p in range(NP):
                    sp.wait_ge(ctx_tp, ONE + b * 16 + 4 * max(p - 1, 0))
                    r0 = p * BANK
                    if rows[p] == BANK:
                        src = A["ctx_4096"][ds(b, 1), r0:r0 + BANK, :].rearrange("o (a p) d -> p (o a) d", p=P)
                        sp.dma_start(cnat[:, p % 2, :, :], src).then_inc(ctx_in[p % 2], 16)
                    else:
                        src = A["ctx_4096"][ds(b, 1), r0:r0 + rows[p], :].rearrange("o p d -> p (o d)")
                        sp.dma_start(cnat[0:rows[p], p % 2, 0, :], src).then_inc(ctx_in[p % 2], 16)
                    if p in (0, 3):
                        sp.wait_ge(*((xah_done, ONE + b) if p == 0 else (x1_st, ONE + b * 32)))
                        sp.dma_start((xa if p == 0 else x)[:, :, :],
                                     A["x"][ds(b, 1), :, :].rearrange("o (t p) d -> p (o t) d", p=P))\
                            .then_inc(xa_in if p == 0 else x_in, 16)
            sp.wait_ge(x1_st, ONE + B * 32)
            sp.wait_ge(q_st[0], ONE + B * 128)
            sp.wait_ge(q_st[1], ONE + B * 128)

        @block.gpsimd
        def _(pool):
            for s in in_loop:
                pool.sem_inc(s, ONE)
            ready = Chain(pool, const, 0)
            ready.link(pool.memset(ident[:, :], 0.0))
            ready.link(pool.affine_select(out=ident[:, :], in_=ident[:, :], compare_op=ALU.not_equal, fill=1.0,
                                          base=0, pattern=[[-1, P]], channel_multiplier=1))
            ready.link(pool.memset(wvu[:, :, :, :], 0.0))
            for h in range(2):
                ready.link(pool.memset(wvu[64 * h + HD0:64 * h + HW, :, h, HD0:HW], 1.0))
            ready.link(pool.memset(cst[HD1:HD1 + 1, :].bitcast(F32), 1.0))
            ready.link(pool.memset(cst[0:HD1, NC:NC + 1].bitcast(F32), 0.0))
            ready.link(pool.memset(cv[:, :, HD0:64], 0.0))
            ready.link(pool.memset(cv[:, :, HD0:HW], 1.0))

        @block.tensor
        def _(pe):
            pe.wait_ge(const, 9)
            pe.wait_ge(w_deq, 1)
            for n in range(4 + 12):
                if n == 4:
                    pe.wait_ge(w_q, 16)
                if n >= 2:
                    pe.wait_ge(w_ev, n - 1)
                for c in range(DC):
                    src = w0n[:, n, c * P:(c + 1) * P] if n < 4 else wqn[:, n - 4, c * P:(c + 1) * P]
                    tp = pe.transpose(ps[:, (n % 2) * BANK + c * P:(n % 2) * BANK + (c + 1) * P], src, ident[:, :])
                tp.then_inc(w_tp, 1)
            pe.wait_ge(w_ev, 16)
            pe.wait_ge(w_small, 16 * 12)

            def turn_ctx(e, p):
                pe.wait_ge(ctx_in[p % 2], ONE + e * 32 + 16 * (p // 2 + 1))
                if p == 0:
                    pe.wait_ge(exp_done, ONE + e * NG * KT)
                pe.wait_ge(ctxT_a, ONE + e * 8 + 2 * p)
                pe.wait_ge(ctxT_d, ONE + e * 8 + 2 * p)
                for c in range(DC):
                    for t in range(-(-rows[p] // P)):
                        m = min(P, rows[p] - t * P)
                        tp = pe.transpose(ps[:, c * BANK + t * P:c * BANK + t * P + m],
                                          cnat[0:m, p % 2, t, c * P:(c + 1) * P], ident[0:m, 0:m])
                    tp.then_inc(ctx_tp, 1)

            def c_product(e, p):
                pe.wait_ge(ctxT_a, ONE + e * 8 + 2 * p + 2)
                pe.wait_ge(ctxT_d, ONE + e * 8 + 2 * p + 2)
                if p == 0:
                    pe.wait_ge(o_done, ONE + e * NG)
                pe.wait_ge(cst_done, ONE + e * 4 + p)
                for c in range(DC):
                    mm = pe.matmul(bank(OB)[0:HD1, 0:rows[p]], wkv[:, c, :], cT[:, c, 0:rows[p]],
                                   start=(c == 0), stop=(c == DC - 1))
                mm.then_inc(c_mm, 1)

            def turn_c(e, p):
                pe.wait_ge(cf_done, ONE + e * 4 + p + 1)
                pe.wait_ge(cv_done, ONE + e * 4 + p)
                if p == 0:
                    pe.wait_ge(post_done, ONE + e * NG)
                if p == 2:
                    pe.wait_ge(cq_done, ONE + e + 1)
                for t in range(-(-rows[p] // P)):
                    m = min(P, rows[p] - t * P)
                    tp = pe.matmul(bank(M2)[0:m, t * HD0:(t + 1) * HD0], cf[:, t * P:t * P + m],
                                   ident[0:HD0, 0:HD0], start=True, stop=True)
                tp.then_inc(cnat_tp, 1)

            def turn_rows(src, turned):
                for half in range(2):
                    for c in range(2):
                        for t in range(TT):
                            tp = pe.transpose(bank(M0 + half)[:, c * T + t * P:c * T + (t + 1) * P],
                                              src[:, t, (2 * half + c) * P:(2 * half + c + 1) * P], ident[:, :])
                    tp.then_inc(turned, 1)

            def turn_xa(e):
                pe.wait_ge(xah_done, ONE + e + 1)
                pe.wait_ge(ffn_done, ONE + e * TT)
                turn_rows(xah, xaT_tp)

            def turn_x(e, k, more):
                pe.wait_ge(xh_done, ONE + e * 2 + k + 1)
                if k == 0:
                    pe.wait_ge(mx_done, ONE + (e + 1) * NG * NI)
                    pe.wait_ge(row_done, ONE + (e + 1) * 8)
                elif more:
                    pe.wait_ge(alo, ONE + (e + 2) * 8)
                else:
                    pe.wait_ge(ffn_done, ONE + (e + 1) * TT)
                turn_rows(xh, xT_tp)

            def latent_queries(e):
                pe.wait_ge(xaT_a, ONE + e + 1)
                pe.wait_ge(xaT_d, ONE + e + 1)
                pe.wait_ge(cv_done, ONE + e * 4 + 2)
                for c in range(DC):
                    mm = pe.matmul(bank(M2)[0:LQ, 0:T], wqd[:, c, :], xaT[:, c, :],
                                   start=(c == 0), stop=(c == DC - 1))
                mm.then_inc(cq_mm, 1)

            def queries(e, hp):
                if hp == 0:
                    pe.wait_ge(cq_done, ONE + e + 1)
                else:
                    pe.wait_ge(alo, ONE + e * 8 + hp - 1)
                for j in range(2):
                    mm = pe.matmul(bank(M0 + hp % 2)[0:HD1, j * T:(j + 1) * T], wqk[:, 2 * hp + j, :], cq[:, :],
                                   start=True, stop=True)
                mm.then_inc(a_mm, 1)

            def max_item(e, g, i):
                n = g * NI + i
                j, ch, (k0, _, k), at = max_cut(g, i)
                if g == 0:
                    if i == 0:
                        pe.wait_ge(alo, ONE + e * 8 + 8)
                        pe.wait_ge(ctxT_a, ONE + e * 8 + 8)
                        pe.wait_ge(ctxT_d, ONE + e * 8 + 8)
                    if j == 0:
                        pe.wait_ge(cst_done, ONE + e * 4 + ch + 1)
                    if i >= 4:
                        pe.wait_ge(mx_done, ONE + e * NG * NI + i - 3)
                elif i < 2:
                    pe.wait_ge(row_done, ONE + e * 8 + 2 * g)
                elif i == THIRD + 2:
                    pe.wait_ge(post_done, ONE + e * NG + g - 1)
                else:
                    before = max(k for k in range(i) if max_bank[k] == max_bank[i])
                    pe.wait_ge(mx_done, ONE + e * NG * NI + g * NI + before + 1)
                pe.matmul(bank(at)[:, 0:k], ast[0:HD1, g * GC + j * P:g * GC + (j + 1) * P],
                          cst[0:HD1, k0:k0 + k], start=True, stop=True).then_inc(mx_mm, 1)

            def max_rows(e, g):
                pe.wait_ge(mxr_done, ONE + e * NG + g + 1)
                if g == 0:
                    pe.wait_ge(qlo, ONE + e * 8)
                for half in range(2):
                    for j in range(4):
                        mm = pe.matmul(bank(M0 + half)[HD1:HD1 + 1, j * P:(j + 1) * P],
                                       mx[:, 4 * half + j:4 * half + j + 1], ident[:, :], start=True, stop=True)
                    mm.then_inc(row_mm, 1)

            def scores(e, g, kt, fill):
                n = g * KT + kt
                if kt == 0:
                    pe.wait_ge(row_done, ONE + e * 8 + 2 * g + 2)
                if n >= 2:
                    pe.wait_ge(exp_done, ONE + e * NG * KT + n - 1)
                else:
                    pe.wait_ge(mx_done, ONE + e * NG * NI + NI)
                for half in range(2):
                    mm = pe.matmul(ps[0:keys[kt], ((n % 2) * 2 + half) * BANK:((n % 2) * 2 + half + 1) * BANK],
                                   cst[0:HD1 + 1, kt * P:kt * P + keys[kt]],
                                   ast[:, g * GC + half * BANK:g * GC + (half + 1) * BANK], start=True, stop=True)
                    if half == 0:
                        fill()
                mm.then_inc(s_mm, 1)

            def values(e, g, kt):
                n = g * KT + kt
                if kt == 0:
                    pe.wait_ge(o_done, ONE + e * NG + g)
                pe.wait_ge(exp_done, ONE + e * NG * KT + n + 1)
                for half in range(2):
                    mm = pe.matmul(bank(OB)[64 * half:64 * half + 64, :], cv[0:keys[kt], kt, :],
                                   pr[0:keys[kt], n % 2, half * BANK:(half + 1) * BANK],
                                   start=(kt == 0), stop=(kt == KT - 1))
                mm.then_inc(av_mm, 1)

            def raise_values(e, g):
                pe.wait_ge(o_done, ONE + e * NG + g + 1)
                pe.wait_ge(post_done, ONE + e * NG + g)
                if g == 0:
                    pe.wait_ge(cv_done, ONE + e * 4 + 4)
                for t in range(TT):
                    for c in range(2):
                        mm = pe.matmul(bank(M2)[:, (t * 2 + c) * 2 * HW:(t * 2 + c + 1) * 2 * HW],
                                       osb[:, c * T + t * P:c * T + (t + 1) * P],
                                       wvu[:, 2 * g + c, :, :].rearrange("p h e -> p (h e)"),
                                       start=True, stop=True)
                mm.then_inc(bd_mm, 1)

            def attend(e):
                pe.wait_ge(cst_done, ONE + e * 4 + 4)
                pe.wait_ge(cv_done, ONE + e * 4 + 4)
                for g in range(NG):
                    items = iter(range(NI if g + 1 < NG else 0))

                    def fill():
                        i = next(items, None)
                        if i is not None:
                            max_item(e, g + 1, i)

                    scores(e, g, 0, lambda: None)
                    for kt in range(KT):
                        if kt + 1 < KT:
                            scores(e, g, kt + 1, fill)
                            fill()
                        if g + 1 < NG and kt == KT - 2:
                            max_rows(e, g + 1)
                        if kt == 2 and g > 0:
                            raise_values(e, g - 1)
                        values(e, g, kt)
                        if kt < KT - 2:
                            fill()

            def between(e, f):
                if e is not None:
                    raise_values(e, NG - 1)
                if f is not None:
                    turn_ctx(f, 0)
                    c_product(f, 0)
                    turn_ctx(f, 1)
                    turn_c(f, 0)
                if e is not None:
                    turn_x(e, 0, False)
                    pe.wait_ge(xT_a, ONE + e * 2 + 1)
                    pe.wait_ge(xT_d, ONE + e * 2 + 1)
                    for t in range(TT):
                        for c in range(DC):
                            mm = pe.matmul(bank(M0 + t), xT[:, c, t * P:(t + 1) * P], w0T[:, c, :],
                                           start=(c == 0), stop=(c == DC - 1))
                        mm.then_inc(ffn_mm, 1)
                if f is not None:
                    c_product(f, 1)
                    turn_ctx(f, 2)
                    turn_c(f, 1)
                    turn_xa(f)
                    latent_queries(f)
                    for hp in range(4):
                        queries(f, hp)
                    c_product(f, 2)
                    for hp in range(4, 8):
                        queries(f, hp)
                    turn_ctx(f, 3)
                    turn_c(f, 2)
                if e is not None:
                    turn_x(e, 1, f is not None)
                if f is not None:
                    c_product(f, 3)
                    turn_c(f, 3)
                if e is not None:
                    pe.wait_ge(xT_a, ONE + e * 2 + 2)
                    pe.wait_ge(xT_d, ONE + e * 2 + 2)
                for hp in range(8):
                    if e is not None:
                        if hp >= 2:
                            pe.wait_ge(qlo, ONE + e * 8 + hp - 1)
                        for j in range(2):
                            h = 2 * hp + j
                            for c in range(DC):
                                mm = pe.matmul(bank(M0 + hp % 2)[0:HD1, j * T:(j + 1) * T],
                                               wqT[:, c, h * HD1:(h + 1) * HD1], xT[:, c, :],
                                               start=(c == 0), stop=(c == DC - 1))
                                if c % 2 and f is not None:
                                    max_item(f, 0, 4 * hp + 2 * j + c // 2)
                        mm.then_inc(q_mm, 1)
                    elif f is not None:
                        for i in range(4 * hp, 4 * hp + 4):
                            max_item(f, 0, i)
                if f is not None:
                    max_rows(f, 0)

            between(None, 0)
            with pe.Fori(0, B - 1) as b:
                attend(b)
                between(b, b + 1)
            attend(B - 1)
            between(B - 1, None)

        @block.scalar
        def _(act):
            for n in range(0, 16, 2):
                act.wait_ge(w_tp, n + 1)
                if n:
                    act.wait_ge(w_ev, n)
                dst = w0T[:, :, n * P:(n + 1) * P] if n < 4 else wqT[:, :, (n - 4) * P:(n - 3) * P]
                act.copy(dst, bank(0).rearrange("p (c m) -> p c m", c=DC)).then_inc(w_ev, 1)

            def turned_ctx(e, p):
                for c in (0, 2):
                    act.wait_ge(ctx_tp, ONE + e * 16 + 4 * p + c + 1)
                    act.wait_ge(c_mm, ONE + e * 4 + p)
                    act.copy(cT[:, c, 0:rows[p]], bank(c, rows[p])).then_inc(ctxT_a, 1)

            def copy_c(e, p):
                act.wait_ge(c_mm, ONE + e * 4 + p + 1)
                act.copy(cst[0:HD1, p * BANK:p * BANK + rows[p]], bank(OB)[0:HD1, 0:rows[p]])
                act.wait_ge(cnat_tp, ONE + e * 4 + p)
                act.copy(cf[:, 0:rows[p]], bank(OB)[0:HD0, 0:rows[p]]).then_inc(cf_done, 1)

            def turned_xa(e):
                act.wait_ge(xaT_tp, ONE + e * 2 + 1)
                act.wait_ge(cq_mm, ONE + e)
                act.copy(xaT[:, 0:2, :], bank(M0).rearrange("p (c m) -> p c m", c=2)).then_inc(xaT_a, 1)

            def turned_x(e, k):
                act.wait_ge(xT_tp, ONE + e * 4 + 2 * k + 1)
                if k == 0:
                    act.wait_ge(x1_st, ONE + e * 32)
                else:
                    act.wait_ge(ffn_mm, ONE + e * TT + TT)
                act.copy(xT[:, 0:2, :], bank(M0).rearrange("p (c m) -> p c m", c=2)).then_inc(xT_a, 1)

            def copy_queries(e, hp):
                act.wait_ge(a_mm, ONE + e * 8 + hp + 1)
                act.copy(ast[0:HD1, hp * BANK:(hp + 1) * BANK], bank(M0 + hp % 2)[0:HD1, :]).then_inc(ahi, 1)

            def rows_of(e, g):
                for half in range(2):
                    act.wait_ge(row_mm, ONE + e * 8 + 2 * g + half + 1)
                    act.mul(ast[HD1:HD1 + 1, g * GC + half * BANK:g * GC + (half + 1) * BANK],
                            bank(M0 + half)[HD1:HD1 + 1, :], -1.0).then_inc(row_done, 1)

            def store_q(e, hp):
                act.wait_ge(qhi, ONE + e * 8 + hp + 1)
                act.wait_ge(qlo, ONE + e * 8 + hp + 1)
                for part in range(2):
                    dst = q_scr[ds(e, 1), hp // 2, part, :, (hp % 2) * BANK:(hp % 2 + 1) * BANK]
                    act.dma_start(dst.rearrange("o p n -> p (o n)"), qst[:, hp % 2, part, :].bitcast(F32))\
                        .then_inc(q_st[hp % 2], 16)

            def attend(e):
                for g in range(NG):
                    for kt in range(KT):
                        n = g * KT + kt
                        act.wait_ge(s_mm, ONE + e * NG * KT + n + 1)
                        act.wait_ge(av_mm, ONE + e * NG * KT + max(n - 1, 0))
                        act.activation(pr[0:keys[kt], n % 2, :],
                                       ps[0:keys[kt], (n % 2) * 2 * BANK:((n % 2) * 2 + 2) * BANK],
                                       ACT.Exp, scale=S0).then_inc(exp_done, 1)
                    if g + 1 < NG:
                        rows_of(e, g + 1)
                    act.wait_ge(av_mm, ONE + e * NG * KT + (g + 1) * KT)
                    act.wait_ge(bd_mm, ONE + e * NG + g)
                    act.copy(osb[:, :], bank(OB)).then_inc(o_done, 1)

            def between(e, f):
                if f is not None:
                    turned_ctx(f, 0)
                    copy_c(f, 0)
                    turned_ctx(f, 1)
                if e is not None:
                    turned_x(e, 0)
                if f is not None:
                    copy_c(f, 1)
                    turned_ctx(f, 2)
                    turned_xa(f)
                    act.wait_ge(cq_mm, ONE + f + 1)
                    act.copy(cq[:, :], bank(M2)[0:LQ, 0:T]).then_inc(cq_done, 1)
                    for hp in range(4):
                        copy_queries(f, hp)
                    copy_c(f, 2)
                    for hp in range(4, 8):
                        copy_queries(f, hp)
                    turned_ctx(f, 3)
                if e is not None:
                    turned_x(e, 1)
                if f is not None:
                    copy_c(f, 3)
                if e is not None:
                    for hp in range(8):
                        act.wait_ge(q_mm, ONE + e * 8 + hp + 1)
                        act.wait_ge(q_st[hp % 2], ONE + e * 128 + 32 * (hp // 2))
                        act.copy(qst[:, hp % 2, 0, :], bank(M0 + hp % 2)[0:HD1, :]).then_inc(qhi, 1)
                        if hp:
                            store_q(e, hp - 1)
                    store_q(e, 7)
                if f is not None:
                    rows_of(f, 0)
                if e is not None:
                    act.wait_ge(xT_d, ONE + e * 2 + 2)
                    act.wait_ge(xT_a, ONE + e * 2 + 2)
                    act.wait_ge(step_f, ONE + (e + 1) * STEPS_F)
                    act.dma_start(x_scr[ds(e, 1), :, :].rearrange("o p n -> p (o n)"),
                                  x[:, :, :].rearrange("p a b -> p (a b)")).then_inc(x1_st, 16)
                    act.dma_start(lt_scr[ds(e, 1), :, :].rearrange("o p n -> p (o n)"),
                                  xT[:, :, :].rearrange("p a b -> p (a b)")).then_inc(x1_st, 16)

            between(None, 0)
            with act.Fori(0, B - 1) as b:
                attend(b)
                between(b, b + 1)
            attend(B - 1)
            between(B - 1, None)

        @block.vector
        def _(dve):
            dve.wait_ge(w_0, 48)
            for o in range(DC):
                for i in range(DC):
                    last = dve.tensor_scalar(w0n[:, o, i * P:(i + 1) * P], w0i[:, o, i * P:(i + 1) * P],
                                             w0z[:, o, i:i + 1], w0s[:, o, i:i + 1], ALU.subtract, ALU.mult)
            last.then_inc(w_deq, 1)
            for n in range(1, 16, 2):
                dve.wait_ge(w_tp, n + 1)
                dve.wait_ge(w_ev, n)
                dst = w0T[:, :, n * P:(n + 1) * P] if n < 4 else wqT[:, :, (n - 4) * P:(n - 3) * P]
                dve.tensor_copy(dst, bank(1).rearrange("p (c m) -> p c m", c=DC)).then_inc(w_ev, 1)
            dve.wait_ge(const, 9)
            dve.wait_ge(w_small, 192)

            def turned_ctx(e, p):
                for c in (1, 3):
                    dve.wait_ge(ctx_tp, ONE + e * 16 + 4 * p + c + 1)
                    dve.wait_ge(c_mm, ONE + e * 4 + p)
                    dve.tensor_copy(cT[:, c, 0:rows[p]], bank(c, rows[p])).then_inc(ctxT_d, 1)

            def split_c(e, p):
                lo = cst[HD0:2 * HD0, p * BANK:p * BANK + rows[p]]
                dve.wait_ge(cf_done, ONE + e * 4 + p + 1)
                dve.tensor_tensor(lo, bank(OB)[HD0:2 * HD0, 0:rows[p]], lo, ALU.subtract).then_inc(cst_done, 1)

            def turned_c(e, p):
                dve.wait_ge(cnat_tp, ONE + e * 4 + p + 1)
                nt, m = -(-rows[p] // P), min(P, rows[p])
                dve.tensor_copy(cv[0:m, 4 * p:4 * p + nt, 0:HD0],
                                bank(M2)[0:m, 0:nt * HD0].rearrange("p (t e) -> p t e", e=HD0)).then_inc(cv_done, 1)

            def normalise_xa(e):
                dve.wait_ge(xa_in, ONE + e * 16 + 16)
                dve.wait_ge(xaT_tp, ONE + e * 2)
                chain = Chain(dve, step_a, LN_STEPS, e)
                layernorm(dve, chain, xah, xa, ln["st"], ln["mv"], ln["v"], ln["t"], ln["u"], ln["y"])\
                    .then_inc(xah_done, 1)

            def normalise(chain, e, k):
                dve.wait_ge(xT_tp, ONE + e * 4 + 2 * k)
                layernorm(dve, chain, xh, x, ln["st"], ln["mv"], ln["v"], ln["t"], ln["u"], ln["y"])\
                    .then_inc(xh_done, 1)

            def turned_xa(e):
                dve.wait_ge(xaT_tp, ONE + e * 2 + 2)
                dve.wait_ge(cq_mm, ONE + e)
                dve.tensor_copy(xaT[:, 2:4, :], bank(M0 + 1).rearrange("p (c m) -> p c m", c=2)).then_inc(xaT_d, 1)

            def turned_x(e, k):
                dve.wait_ge(xT_tp, ONE + e * 4 + 2 * k + 2)
                if k == 0:
                    dve.wait_ge(x1_st, ONE + e * 32)
                else:
                    dve.wait_ge(ffn_mm, ONE + e * TT + TT)
                dve.tensor_copy(xT[:, 2:4, :], bank(M0 + 1).rearrange("p (c m) -> p c m", c=2)).then_inc(xT_d, 1)

            def split_queries(e, hp):
                lo = ast[2 * HD0:3 * HD0, hp * BANK:(hp + 1) * BANK]
                dve.wait_ge(ahi, ONE + e * 8 + hp + 1)
                dve.tensor_tensor(lo, bank(M0 + hp % 2)[2 * HD0:3 * HD0, :], lo, ALU.subtract).then_inc(alo, 1)

            def max_part(e, g, i):
                n = g * NI + i
                if i == 0:
                    dve.wait_ge(mxr_done, ONE + e * NG + g)
                dve.wait_ge(mx_mm, ONE + e * NG * NI + n + 1)
                j, ch, (_, k, _), at = max_cut(g, i)
                dve.reduce_max(pm[:, j, ch:ch + 1], bank(at)[:, 0:k], AX).then_inc(mx_done, 1)

            def max_all(e, g):
                dve.wait_ge(mx_done, ONE + e * NG * NI + (g + 1) * NI)
                dve.wait_ge(row_mm, ONE + e * 8 + 2 * g)
                dve.reduce_max(mx[:, :], pm[:, :, :], AX).then_inc(mxr_done, 1)

            def attended(chain, e, g):
                dve.wait_ge(bd_mm, ONE + e * NG + g + 1)
                if g == 0:
                    dve.wait_ge(x_in, ONE + e * 16 + 16)
                o = bank(M2)[:, 0:TT * G * HW].rearrange("p (t c h e) -> p t c h e", t=TT, c=2, h=2)
                r = rec[:, :].rearrange("p (t c h e) -> p t c h e", t=TT, c=2, e=1)
                chain.link(dve.reciprocal(rec[:, :], bank(M2)[:, 0:TT * G * HW]
                                          .rearrange("p (n e) -> p n e", e=HW)[:, :, HD0]))
                for t in range(TT):
                    xs = x[:, t, g * P:(g + 1) * P].rearrange("p (h c e) -> p c h e", h=2, c=2)
                    tm = tmp[:, t, :].rearrange("p (c h e) -> p c h e", c=2, h=2)
                    chain.link(dve.tensor_tensor(tm, o[:, t, :, :, 0:HD0],
                                                 r[:, t].broadcast_to([P, 2, 2, HD0]), ALU.mult))
                    last = dve.tensor_tensor(xs, xs, tm, ALU.add)
                    if t < TT - 1:
                        chain.link(last)
                last.then_inc(post_done, 1)
                dve.wait_ge(post_done, ONE + e * NG + g + 1)

            def attend(chain, e):
                for g in range(NG):
                    items = iter(range(NI if g + 1 < NG else 0))

                    def fill(n):
                        for _ in range(n):
                            i = next(items, None)
                            if i is not None:
                                max_part(e, g + 1, i)

                    for kt in range(KT):
                        if kt + 1 < KT:
                            fill(2)
                        if kt == 2 and g > 0:
                            attended(chain, e, g - 1)
                        if kt < KT - 2:
                            fill(1)
                        if g + 1 < NG and kt == KT - 2:
                            max_all(e, g + 1)

            def between(chain, e, f):
                if e is not None:
                    attended(chain, e, NG - 1)
                    normalise(chain, e, 0)
                if f is not None:
                    turned_ctx(f, 0)
                    split_c(f, 0)
                    turned_ctx(f, 1)
                    turned_c(f, 0)
                if e is not None:
                    turned_x(e, 0)
                if f is not None:
                    normalise_xa(f)
                if e is not None:
                    for t in range(TT):
                        dve.wait_ge(ffn_mm, ONE + e * TT + t + 1)
                        dve.tensor_tensor(x[:, t, :], bank(M0 + t), x[:, t, :], ALU.add).then_inc(ffn_done, 1)
                        dve.wait_ge(ffn_done, ONE + e * TT + t + 1)
                        chain.link(dve.tensor_tensor(x[:, t, :], x[:, t, :], bias0[:, :], ALU.add))
                if f is not None:
                    split_c(f, 1)
                    turned_ctx(f, 2)
                    turned_c(f, 1)
                    turned_xa(f)
                    for hp in range(4):
                        split_queries(f, hp)
                    split_c(f, 2)
                if e is not None:
                    normalise(chain, e, 1)
                if f is not None:
                    for hp in range(4, 8):
                        split_queries(f, hp)
                    turned_ctx(f, 3)
                    turned_c(f, 2)
                if e is not None:
                    turned_x(e, 1)
                if f is not None:
                    split_c(f, 3)
                    turned_c(f, 3)
                for hp in range(8):
                    if f is not None:
                        for i in range(4 * hp, 4 * hp + 4):
                            max_part(f, 0, i)
                    if e is not None:
                        dve.wait_ge(qhi, ONE + e * 8 + hp + 1)
                        dve.tensor_tensor(qst[:, hp % 2, 1, :], bank(M0 + hp % 2)[0:HD1, :], qst[:, hp % 2, 0, :],
                                          ALU.subtract).then_inc(qlo, 1)
                if f is not None:
                    max_all(f, 0)
                if e is not None:
                    assert chain.n == STEPS_F, (chain.n, STEPS_F)

            between(None, None, 0)
            with dve.Fori(0, B - 1) as b:
                chain = Chain(dve, step_f, STEPS_F, b)
                attend(chain, b)
                between(chain, b, b + 1)
            chain = Chain(dve, step_f, STEPS_F, B - 1)
            attend(chain, B - 1)
            between(chain, B - 1, None)


def turn_weights(nc, A, ident, ps, wkvh, wkvl, wo_scr, w1T):
    with ExitStack() as ctx:
        def sem(name):
            return ctx.enter_context(nc.semaphore(name))

        W = KV1 * HD1
        wk = ctx.enter_context(nc.sbuf_tensor("wk_rows", [P, 2, W // P, D], F32))
        wo = ctx.enter_context(nc.sbuf_tensor("wo_rows", [P, DC, H1 * HD1], F32))
        w1 = ctx.enter_context(nc.sbuf_tensor("w1_rows", [P, DC, D], F32))
        woT = ctx.enter_context(nc.sbuf_tensor("woT_all", [HD1, H1, D], F32))
        kv_in, w1_in, wo_in = sem("kv_rows_in"), sem("w1_rows_in"), sem("wo_rows_in")
        tp, hi, done, wo_st = sem("rows_turned"), sem("rows_hi"), sem("rows_copied"), sem("wo_stored")
        NKV = 2 * W // P
        block = ctx.enter_context(nc.Block())

        def bank(i):
            return ps[:, i * BANK:(i + 1) * BANK]

        N = NKV + DC + H1

        @block.sync
        def _(sp):
            for i, name in enumerate(("L1_xattn_Wk", "L1_xattn_Wv")):
                sp.dma_start(wk[:, i, :, :], A[name].rearrange("(a p) i -> p a i", p=P)).then_inc(kv_in, 16)
            sp.dma_start(w1[:, :, :], A["L1_ffn_W"].rearrange("(a p) i -> p a i", p=P)).then_inc(w1_in, 16)
            sp.dma_start(wo[:, :, :], A["L1_xattn_Wo"].rearrange("(a p) i -> p a i", p=P)).then_inc(wo_in, 16)
            for g in range(H1 // G):
                sp.wait_ge(done, NKV + DC + G * (g + 1))
                sp.dma_start(wo_scr[g], woT[:, g * G:(g + 1) * G, :].rearrange("p h d -> p (h d)"))\
                    .then_inc(wo_st, 16)
            sp.wait_ge(wo_st, 16 * (H1 // G))

        @block.tensor
        def _(pe):
            for n in range(N):
                if n in (0, NKV, NKV + DC):
                    s, v = {0: (kv_in, 32), NKV: (w1_in, 16), NKV + DC: (wo_in, 16)}[n]
                    pe.wait_ge(s, v)
                if n >= 2:
                    pe.wait_ge(done, n - 1)
                for c in range(DC):
                    if n < NKV:
                        src = wk[:, n // 3, n % 3, c * P:(c + 1) * P]
                    elif n < NKV + DC:
                        src = w1[:, n - NKV, c * P:(c + 1) * P]
                    else:
                        h = n - NKV - DC
                        src = wo[:, c, h * HD1:(h + 1) * HD1]
                    m = pe.transpose(bank(n % 2)[0:src.shape[1], c * P:(c + 1) * P], src, ident[:, :])
                m.then_inc(tp, 1)

        @block.scalar
        def _(act):
            for n in range(N):
                act.wait_ge(tp, n + 1)
                src = bank(n % 2).rearrange("p (c m) -> p c m", c=DC)
                if n < NKV:
                    act.copy(wkvh[:, :, n * P:(n + 1) * P], src).then_inc(hi, 1)
                elif n % 2:
                    act.wait_ge(done, n)
                    dst = w1T[:, :, (n - NKV) * P:(n - NKV + 1) * P] if n < NKV + DC else woT[:, n - NKV - DC, :]
                    if n >= NKV + DC:
                        src = bank(n % 2)[0:HD1, :]
                    act.copy(dst, src).then_inc(done, 1)

        @block.vector
        def _(dve):
            for n in range(N):
                src = bank(n % 2).rearrange("p (c m) -> p c m", c=DC)
                if n < NKV:
                    dve.wait_ge(hi, n + 1)
                    dve.tensor_tensor(wkvl[:, :, n * P:(n + 1) * P], src, wkvh[:, :, n * P:(n + 1) * P], ALU.subtract)\
                        .then_inc(done, 1)
                elif n % 2 == 0:
                    dve.wait_ge(tp, n + 1)
                    dve.wait_ge(done, n)
                    dst = w1T[:, :, (n - NKV) * P:(n - NKV + 1) * P] if n < NKV + DC else woT[:, n - NKV - DC, :]
                    if n >= NKV + DC:
                        src = bank(n % 2)[0:HD1, :]
                    dve.tensor_copy(dst, src).then_inc(done, 1)


def grouped_attention(nc, A, ident, ps, ln, q_scr, x_scr, lt_scr, y_scr, z_scr, wkvh, wkvl, wo_scr, w1T, h8all,
                      dlall):
    W = KV1 * HD1
    NP = 7
    LAT = 5
    rows = [T] * 6 + [NC - 5 * T]
    NK = T + NC
    KT = -(-NK // P)
    keys = [P] * (KT - 1) + [NK - (KT - 1) * P]
    cuts = widths(NK, 4)
    NI = QT * len(cuts)
    RING = (KV1 - 1) * NI + KV1 * (1 + TT * G)
    XW = rows[-1] + 1

    with ExitStack() as ctx:
        def sb(name, shape, dt=F32):
            return ctx.enter_context(nc.sbuf_tensor(name, shape, dt))

        def sem(name):
            return ctx.enter_context(nc.semaphore(name))

        in_loop = []

        def counted(name):
            in_loop.append(sem(name))
            return in_loop[-1]

        kh = sb("kh", [HD1 + 1, KV1, NK + 1], F32R)
        kl = sb("kl", [HD1, KV1, NK + 1], F32R)
        vh = sb("vh", [P, KT, KV1, HD1 + 1], F32R)
        vl = sb("vl", [P, KT, KV1, HD1 + 1], F32R)
        qh = sb("qh", [HD1 + 1, 2, GC], F32R)
        ql = sb("ql", [HD1, 2, GC], F32R)
        woT = sb("woT", [HD1, G, D])
        nat = sb("nat", [P, 2, 3, D])
        parts = sb("parts", [P, 2, 2, DC * XW], F32R)
        xT = sb("xT1", [P, DC, T])
        x = sb("x1", [P, TT, D])
        o = sb("o1", [P, GC])
        rec = sb("rec1", [P, G * TT])
        pm = sb("pm1", [P, QT, NP])
        mx = sb("mx1", [P, QT])
        aw = sb("aw", [P, DC, R])
        liT = sb("liT", [R, NE])
        bias8 = sb("bias8", [P, NE])
        zb = sb("zb", [R, T])
        one = sb("one", [HD1 + 1, 2])

        w_small, const = sem("w_small1"), sem("const1")
        wo_in = counted("wo_in")
        x_in, piece_in = counted("x1_in"), [counted("piece_in0"), counted("piece_in1")]
        q_in = [counted("q_in0"), counted("q_in1")]
        tp, xh_done, xl_done = counted("piece_turned"), counted("piece_hi"), counted("piece_lo")
        k_mm, khi, klo, v_mm, vhi, v_done = counted("k_product"), counted("k_hi"), counted("k_lo"), counted("v_product"), counted("v_hi"), counted("v_lo")
        mx_mm, mx_done = counted("first_max_scores1"), counted("first_max_part1")
        ring_mm, ring_done, mxr_done = counted("ring_product"), counted("ring_read"), counted("max_ready1")
        row_mm, row_done = counted("max_turned1"), counted("max_row1")
        s_mm, phi, exp_done = counted("scores1"), counted("probs_hi"), counted("probs1")
        plo_d, plo_p = counted("probs_lo_by_dve"), counted("probs_lo_by_pool")
        av_mm, o_done = counted("values1"), counted("o_copied1")
        n_done, xT_tp, xT_a, xT_d = counted("x_normal"), counted("x_turned1"), counted("xT1_by_act"), counted("xT1_by_dve")
        z_mm, z_done, h8_mm, h8_done = counted("z_product"), counted("z_copied"), counted("h8_product"), counted("h8_kept")
        dl_mm, dl_done, h_mm, h_done = counted("dl_product"), counted("dl_kept"), counted("h_product"), counted("h_added")
        y_st, z_st = counted("y_stored"), counted("z_stored")
        step = counted("dve_step1")
        block = ctx.enter_context(nc.Block())
        OB, M0 = 4, 6

        def bank(i, n=BANK):
            return ps[:, i * BANK:i * BANK + n]

        lt = nat[:, LAT % 2, :, :].rearrange("p a d -> p (a d)")[:, 0:DC * T].rearrange("p (c m) -> p c m", c=DC)
        xn = o[:, :].rearrange("p (t d) -> p t d", t=TT)
        xh = parts[:, 0, :, :].rearrange("p i (c m) -> p i c m", c=DC)
        xl = parts[:, 1, :, :].rearrange("p i (c m) -> p i c m", c=DC)
        ph, pl = parts[:, 0, :, 0:GC], parts[:, 1, :, 0:GC]
        pf = xT[:, :, :].rearrange("p (h c) m -> p h (c m)", h=2)

        def beside(kv):
            maxima = [("max", kv + 1, i) for i in range(NI)] if kv + 1 < KV1 else []
            if kv < 1:
                return maxima
            order, maxima = maxima[:6] + [("sum", kv - 1, 0)], maxima[6:]
            for i in range(TT * G):
                order += maxima[:2] + [("out", kv - 1, i)]
                maxima = maxima[2:]
            return order + maxima

        ring = {}
        for kv in range(KV1 + 1):
            for item in beside(kv):
                ring[item] = len(ring)
        assert len(ring) == RING


        def piece_loaded(e, p):
            return ONE + e * 16 * (NP // 2, NP // 2 + 2)[p % 2 == 0] + 16 * (p // 2 + 1) + 16 * (p == NP - 1)

        @block.sync
        def _(sp):
            sp.dma_start(aw[:, :, :], A["L1_ffn_A"].rearrange("(c p) r -> p c r", p=P)).then_inc(w_small, 16)
            with nc.allow_non_contiguous_dma(reason="256 values"):
                sp.dma_start(liT[:, :], A["L1_ffn_LiMEs"].rearrange("e r -> r e")).then_inc(w_small, 16)
            sp.dma_start(bias8[:, :], A["L1_ffn_b"][0:NE].rearrange("(a n) -> a n", a=1).to_broadcast([P, NE]))\
                .then_inc(w_small, 16)
            with sp.Fori(0, B) as b:
                def load_q(kv):
                    for part, q in ((0, qh[0:HD1, kv % 2, :]), (1, ql[:, kv % 2, :])):
                        sp.dma_start(q.bitcast(F32), q_scr[ds(b, 1), kv, part, :, :].rearrange("o p n -> p (o n)"))\
                            .then_inc(q_in[kv % 2], 16)

                def load_wo(kv):
                    used = ring["out", kv - 1, TT * G - 1] + 1 if kv else 0
                    sp.wait_ge(ring_mm, ONE + b * RING + used)
                    sp.dma_start(woT[:, :, :].rearrange("p h d -> p (h d)"), wo_scr[kv]).then_inc(wo_in, 16)

                for p in range(NP):
                    if p == LAT + 2:
                        sp.wait_ge(xl_done, ONE + b * NP + LAT + 1)
                    else:
                        sp.wait_ge(tp, ONE + b * 4 * (NP - 1) + 4 * max(p - 1, 0))
                    if p == LAT % 2:
                        sp.wait_ge(xl_done, ONE + b * NP)
                    n2 = 2 * P
                    if p == LAT:
                        sp.dma_start(lt, lt_scr[ds(b, 1), :, :].rearrange("o p (c m) -> p (o c) m", c=DC))\
                            .then_inc(piece_in[p % 2], 16)
                    else:
                        r0 = (p if p < LAT else p - 1) * T
                        src = A["ctx_4096"][ds(b, 1), r0:r0 + n2, :].rearrange("o (a p) d -> p (o a) d", p=P)
                        sp.dma_start(nat[:, p % 2, 0:2, :], src).then_inc(piece_in[p % 2], 16)
                        if rows[p] > n2:
                            src = A["ctx_4096"][ds(b, 1), r0 + n2:r0 + rows[p], :].rearrange("o p d -> p (o d)")
                            sp.dma_start(nat[0:rows[p] - n2, p % 2, 2, :], src).then_inc(piece_in[p % 2], 16)
                    if p == 1:
                        sp.wait_ge(s_mm, ONE + b * KV1 * KT * 2)
                        load_q(0)
                        load_q(1)
                    if p == 3:
                        load_wo(0)
                sp.wait_ge(y_st, ONE + b * 16)
                sp.dma_start(x[:, :, :].rearrange("p a b -> p (a b)"),
                             x_scr[ds(b, 1), :, :].rearrange("o p n -> p (o n)")).then_inc(x_in, 16)
                for kv in range(1, KV1):
                    if kv + 1 < KV1:
                        sp.wait_ge(s_mm, ONE + b * KV1 * KT * 2 + kv * KT * 2)
                        load_q(kv + 1)
                    load_wo(kv)
            sp.wait_ge(y_st, ONE + B * 16)
            sp.wait_ge(z_st, ONE + B * 16)

        @block.gpsimd
        def _(pool):
            for s in in_loop:
                pool.sem_inc(s, ONE)
            ready = Chain(pool, const, 0)
            ready.link(pool.memset(one[:, :], 1.0))
            ready.link(pool.memset(kh[HD1:HD1 + 1, :, :].bitcast(F32), 1.0))
            ready.link(pool.memset(parts[:, :, :, XW - 1:DC * XW:XW].bitcast(F32), 0.0))
            ready.link(pool.memset(vh[:, :, :, HD1:HD1 + 1].bitcast(F32), 1.0))
            ready.link(pool.memset(vl[:, :, :, HD1:HD1 + 1].bitcast(F32), 0.0))
            with pool.Fori(0, B) as b:
                for n in range(KV1 * KT):
                    m = keys[n % KT]
                    pool.wait_ge(exp_done, ONE + b * KV1 * KT * 2 + 2 * n + 2)
                    pool.tensor_tensor(pl[0:m, n % 2, BANK:GC], pf[0:m, 1, :],
                                       ph[0:m, n % 2, BANK:GC].bitcast(F32), ALU.subtract).then_inc(plo_p, 1)

        @block.tensor
        def _(pe):
            pe.wait_ge(w_small, 48)
            pe.wait_ge(const, 5)

            def turn(e, p):
                pe.wait_ge(piece_in[p % 2], piece_loaded(e, p))
                if p == 0:
                    pe.wait_ge(exp_done, ONE + e * KV1 * KT * 2)
                elif p == 1:
                    pe.wait_ge(xl_done, ONE + e * NP + 1)
                else:
                    pe.wait_ge(mx_done, ONE + e * NP * QT + (p - 1) * QT)
                for c in range(DC):
                    for t in range(-(-rows[p] // P)):
                        m = min(P, rows[p] - t * P)
                        mm = pe.transpose(bank(c)[:, t * P:t * P + m], nat[0:m, p % 2, t, c * P:(c + 1) * P],
                                          ident[0:m, 0:m])
                    mm.then_inc(tp, 1)

            def three(out, lhs, rhs, fill):
                n = 0
                for l, r in ((0, 0), (1, 0), (0, 1)):
                    for c in range(DC):
                        mm = pe.matmul(out, lhs(l, c), rhs(r, c), start=(n == 0), stop=(n == 3 * DC - 1))
                        n += 1
                        if n % 3 == 0:
                            fill()
                return mm

            def keys_of(e, p, kv):
                if kv == 0:
                    pe.wait_ge(xl_done, ONE + e * NP + p + 1)
                n, i = rows[p] + rows[p] % 2, p * KV1 + kv
                if i >= 2:
                    pe.wait_ge(klo, ONE + e * NP * KV1 + i - 1)
                else:
                    pe.wait_ge(o_done, ONE + e * KV1 * 2)
                three(bank(OB + i % 2)[0:HD1, 0:n],
                      lambda l, c: (wkvh, wkvl)[l][:, c, kv * HD1:(kv + 1) * HD1],
                      lambda r, c: (xh, xl)[r][:, p % 2, c, 0:n], lambda: None).then_inc(k_mm, 1)

            def first_max(e, p, j):
                n = p * QT + j
                if j == 0:
                    pe.wait_ge(khi, ONE + e * NP * KV1 + p * KV1 + 1)
                    if p == 0:
                        pe.wait_ge(q_in[0], ONE + e * 64 + 32)
                    if p + 1 < NP:
                        pe.wait_ge(xl_done, ONE + e * NP + p + 2)
                if n >= 4:
                    pe.wait_ge(mx_done, ONE + e * NP * QT + n - 3)
                k = rows[p] + rows[p] % 2
                pe.matmul(bank(j % 4)[:, 0:k], qh[0:HD1, 0, j * P:(j + 1) * P], kh[0:HD1, 0, p * T:p * T + k],
                          start=True, stop=True).then_inc(mx_mm, 1)

            def values_of(e, p):
                items = iter(range(QT))

                def fill():
                    j = next(items, None)
                    if j is not None:
                        first_max(e, p, j)

                for t in range(-(-rows[p] // P)):
                    i, m = 2 * p + t, min(P, rows[p] - t * P)
                    if i >= 2:
                        pe.wait_ge(v_done, ONE + e * KT + i - 1)
                    else:
                        pe.wait_ge(ring_done, ONE + e * RING)
                    if p == 2:
                        pe.wait_ge(h_done, ONE + e * TT)
                    if p == 3:
                        pe.wait_ge(z_done, ONE + e)
                        pe.wait_ge(h8_done, ONE + e)
                    if p == 4:
                        pe.wait_ge(dl_done, ONE + e)
                    three(bank(M0 + i % 2)[0:m, 0:W],
                          lambda l, c: (xh, xl)[l][:, p % 2, c, t * P:t * P + m],
                          lambda r, c: (wkvh, wkvl)[r][:, c, W:2 * W], fill).then_inc(v_mm, 1)
                for _ in range(QT):
                    fill()

            def ring_item(e, kind, kv, i):
                n = ring[kind, kv, i]
                at = bank(M0 + n % 2)
                if n >= 2:
                    pe.wait_ge(ring_done, ONE + e * RING + n - 1)
                if kind == "max":
                    if i == 0:
                        pe.wait_ge(q_in[kv % 2], ONE + e * 64 + 32 * (kv // 2 + 1))
                    if i < 2:
                        pe.wait_ge(row_done, ONE + e * 2 * KV1 + 2 * kv)
                    j, (k0, _, k) = i // len(cuts), cuts[i % len(cuts)]
                    mm = pe.matmul(at[:, 0:k], qh[0:HD1, kv % 2, j * P:(j + 1) * P],
                                   kh[0:HD1, kv, k0:k0 + k], start=True, stop=True)
                elif kind == "sum":
                    pe.wait_ge(row_done, ONE + e * 2 * KV1 + 2 * min(kv + 2, KV1))
                    pe.wait_ge(o_done, ONE + e * 2 * KV1 + 2 * kv + 2)
                    for j in range(QT):
                        mm = pe.matmul(at[:, j:j + 1], o[HD1:HD1 + 1, j * P:(j + 1) * P], one[HD1:HD1 + 1, 0:1],
                                       start=True, stop=True)
                else:
                    if i == 0:
                        pe.wait_ge(wo_in, ONE + e * 16 * KV1 + 16 * (kv + 1))
                    h, t = i // TT, i % TT
                    mm = pe.matmul(at, o[0:HD1, h * T + t * P:h * T + (t + 1) * P], woT[:, h, :],
                                   start=True, stop=True)
                mm.then_inc(ring_mm, 1)

            def max_rows(e, kv):
                pe.wait_ge(mxr_done, ONE + e * KV1 + kv + 1)
                if kv == 0:
                    pe.wait_ge(v_done, ONE + (e + 1) * KT)
                for half in range(2):
                    for j in range(4):
                        mm = pe.matmul(bank(M0 + half)[HD1:HD1 + 1, j * P:(j + 1) * P],
                                       mx[:, 4 * half + j:4 * half + j + 1], ident[:, :], start=True, stop=True)
                    mm.then_inc(row_mm, 1)

            def scores(e, kv, kt, fill):
                n = kv * KT + kt
                if kt == 0:
                    pe.wait_ge(row_done, ONE + e * 2 * KV1 + 2 * kv + 2)
                if n >= 2:
                    pe.wait_ge(exp_done, ONE + e * KV1 * KT * 2 + 2 * (n - 1))
                k0, m = kt * P, keys[kt]
                for half in range(2):
                    out = bank((n % 2) * 2 + half)[0:m, :]
                    cols = slice(half * BANK, (half + 1) * BANK)
                    pe.matmul(out, kh[:, kv, k0:k0 + m], qh[:, kv % 2, cols], start=True, stop=False)
                    pe.matmul(out, kl[:, kv, k0:k0 + m], qh[0:HD1, kv % 2, cols], start=False, stop=False)
                    mm = pe.matmul(out, kh[0:HD1, kv, k0:k0 + m], ql[:, kv % 2, cols], start=False, stop=True)
                    mm.then_inc(s_mm, 1)
                    if half == 0:
                        fill()

            def values(e, kv, kt, fill):
                n = kv * KT + kt
                if kt == 0:
                    pe.wait_ge(o_done, ONE + e * 2 * KV1 + 2 * kv)
                m = keys[kt]
                for half in range(2):
                    out, cols = bank(OB + half)[0:HD1 + 1, :], slice(half * BANK, (half + 1) * BANK)
                    pe.wait_ge(phi, ONE + e * KV1 * KT * 2 + 2 * n + half + 1)
                    pe.matmul(out, vh[0:m, kt, kv, :], ph[0:m, n % 2, cols], start=(kt == 0), stop=False)
                    pe.matmul(out, vl[0:m, kt, kv, :], ph[0:m, n % 2, cols], start=False, stop=False)
                    pe.wait_ge((plo_d, plo_p)[half], ONE + e * KV1 * KT + n + 1)
                    mm = pe.matmul(out, vh[0:m, kt, kv, :], pl[0:m, n % 2, cols], start=False, stop=(kt == KT - 1))
                    if half == 0:
                        fill()
                mm.then_inc(av_mm, 1)

            def attend(e):
                pe.wait_ge(klo, ONE + (e + 1) * NP * KV1)
                pe.wait_ge(mx_done, ONE + (e + 1) * NP * QT)
                for kv in range(KV1):
                    items = iter(beside(kv))

                    def fill():
                        item = next(items, None)
                        if item:
                            ring_item(e, *item)

                    scores(e, kv, 0, lambda: None)
                    for kt in range(KT):
                        if kt + 1 < KT:
                            scores(e, kv, kt + 1, fill)
                            fill()
                        if kv + 1 < KV1 and kt == KT - 2:
                            max_rows(e, kv + 1)
                        late = kt > KT - 4
                        values(e, kv, kt, (lambda: None) if late else fill)
                        if not late:
                            fill()

            def turn_x(e, f):
                pe.wait_ge(n_done, ONE + e + 1)
                if f is not None:
                    pe.wait_ge(v_done, ONE + f * KT + 4)
                for half in range(2):
                    for c in range(2):
                        for t in range(TT):
                            mm = pe.transpose(bank(M0 + half)[:, c * T + t * P:c * T + (t + 1) * P],
                                              xn[:, t, (2 * half + c) * P:(2 * half + c + 1) * P], ident[:, :])
                    mm.then_inc(xT_tp, 1)

            def forward(e, f, step):
                if f is not None:
                    pe.wait_ge(v_done, ONE + f * KT + 4 + 2 * step)
                if step == 0:
                    pe.wait_ge(xT_a, ONE + e + 1)
                    pe.wait_ge(xT_d, ONE + e + 1)
                    for t in range(TT):
                        for c in range(DC):
                            mm = pe.matmul(bank(M0 + t), xT[:, c, t * P:(t + 1) * P], w1T[:, c, :],
                                           start=(c == 0), stop=(c == DC - 1))
                        mm.then_inc(h_mm, 1)
                if step == 1:
                    pe.wait_ge(h_done, ONE + e * TT + TT)
                    for c in range(DC):
                        mm = pe.matmul(bank(M0)[0:R, 0:T], aw[:, c, :], xT[:, c, :],
                                       start=(c == 0), stop=(c == DC - 1))
                    mm.then_inc(z_mm, 1)
                    for c in range(DC):
                        mm = pe.matmul(bank(M0 + 1)[:, 0:NE], xT[:, c, 1:T:2], w1T[:, c, 0:NE],
                                       start=(c == 0), stop=(c == DC - 1))
                    mm.then_inc(h8_mm, 1)
                if step == 2:
                    pe.wait_ge(z_done, ONE + e + 1)
                    pe.matmul(bank(M0)[:, 0:NE], zb[:, 1:T:2], liT[:, :], start=True, stop=True).then_inc(dl_mm, 1)

            def between(e, f):
                outs = iter(beside(KV1) if e is not None else [])

                def out(n):
                    for _ in range(n):
                        item = next(outs, None)
                        if item:
                            ring_item(e, *item)

                for p in range(NP):
                    if p == 0:
                        if f is not None:
                            turn(f, 0)
                        out(4)
                    for kv in range(KV1):
                        if f is not None:
                            if kv == (2 if p == 0 else 0) and p + 1 < NP and p + 1 != LAT:
                                turn(f, p + 1)
                            keys_of(f, p, kv)
                        if p == 0:
                            out(1 if kv < KV1 - 1 else 2)
                        if kv == 1 and e is not None and 2 <= p < 5:
                            forward(e, f, p - 2)
                    if f is not None:
                        values_of(f, p)
                    if p == 1 and e is not None:
                        turn_x(e, f)
                if f is not None:
                    max_rows(f, 0)

            between(None, 0)
            with pe.Fori(0, B - 1) as b:
                attend(b)
                between(b, b + 1)
            attend(B - 1)
            between(B - 1, None)

        def turned(n):
            return ps[:, 0:DC * BANK].rearrange("p (c m) -> p c m", c=DC)[:, :, 0:n]

        @block.scalar
        def _(act):
            def piece_hi(e, p):
                act.wait_ge(v_mm, ONE + e * KT + 2 * max(p - 1, 0))
                if p == LAT:
                    act.wait_ge(piece_in[p % 2], piece_loaded(e, p))
                else:
                    act.wait_ge(tp, ONE + e * 4 * (NP - 1) + 4 * (p + 1 if p < LAT else p))
                act.copy(xh[:, p % 2, :, 0:rows[p]], lt if p == LAT else turned(rows[p])).then_inc(xh_done, 1)

            def keys_hi(e, p, kv):
                i, n, c0 = p * KV1 + kv, rows[p] + rows[p] % 2, p * T
                act.wait_ge(k_mm, ONE + e * NP * KV1 + i + 1)
                act.copy(kh[0:HD1, kv, c0:c0 + n], bank(OB + i % 2)[0:HD1, 0:n]).then_inc(khi, 1)

            def copy_values(e, p):
                for t in range(-(-rows[p] // P)):
                    i, m = 2 * p + t, min(P, rows[p] - t * P)
                    act.wait_ge(v_mm, ONE + e * KT + i + 1)
                    act.copy(vh[0:m, i, :, 0:HD1], bank(M0 + i % 2)[0:m, 0:W].rearrange("p (k e) -> p k e", e=HD1))\
                        .then_inc(vhi, 1)

            def rows_of(e, kv):
                for half in range(2):
                    act.wait_ge(row_mm, ONE + e * 2 * KV1 + 2 * kv + half + 1)
                    act.mul(qh[HD1:HD1 + 1, kv % 2, half * BANK:(half + 1) * BANK],
                            bank(M0 + half)[HD1:HD1 + 1, :], -1.0).then_inc(row_done, 1)

            def attend(e):
                act.wait_ge(v_mm, ONE + (e + 1) * KT)
                act.wait_ge(h_mm, ONE + e * TT)
                act.wait_ge(h8_mm, ONE + e)
                act.wait_ge(xT_tp, ONE + e * 2)
                for kv in range(KV1):
                    for kt in range(KT):
                        n = kv * KT + kt
                        act.wait_ge(av_mm, ONE + e * KV1 * KT + max(n - 1, 0))
                        for half in range(2):
                            src = bank((n % 2) * 2 + half)[0:keys[kt], :]
                            cols = slice(half * BANK, (half + 1) * BANK)
                            act.wait_ge(s_mm, ONE + e * KV1 * KT * 2 + 2 * n + half + 1)
                            act.activation(ph[0:keys[kt], n % 2, cols], src, ACT.Exp, scale=S1).then_inc(phi, 1)
                            act.wait_ge((plo_d, plo_p)[half], ONE + e * KV1 * KT + n)
                            act.activation(pf[0:keys[kt], half, :], src, ACT.Exp, scale=S1)\
                                .then_inc(exp_done, 1)
                    if kv + 1 < KV1:
                        rows_of(e, kv + 1)
                    act.wait_ge(av_mm, ONE + e * KV1 * KT + (kv + 1) * KT)
                    if kv:
                        act.wait_ge(ring_mm, ONE + e * RING + ring["out", kv - 1, TT * G - 1] + 1)
                    for half in range(2):
                        act.copy(o[0:HD1 + 1, half * BANK:(half + 1) * BANK], bank(OB + half)[0:HD1 + 1, :])\
                            .then_inc(o_done, 1)

            def forward(e, step):
                if step == 1:
                    act.wait_ge(z_mm, ONE + e + 1)
                    act.wait_ge(z_st, ONE + e * 16)
                    act.copy(zb[:, :], bank(M0)[0:R, 0:T]).then_inc(z_done, 1)
                    act.wait_ge(z_done, ONE + e + 1)
                    act.dma_start(z_scr[ds(e, 1), :, :].rearrange("o p n -> p (o n)"), zb[:, :]).then_inc(z_st, 16)
                    act.wait_ge(h_done, ONE + e * TT + TT)
                    act.dma_start(y_scr[ds(e, 1), :, :].rearrange("o p n -> p (o n)"),
                                  x[:, :, :].rearrange("p a b -> p (a b)")).then_inc(y_st, 16)

            def between(e, f):
                if f is not None:
                    piece_hi(f, 0)
                for p in range(NP):
                    for kv in range(KV1):
                        if f is not None:
                            if kv == (2 if p == 0 else 0) and p + 1 < NP:
                                piece_hi(f, p + 1)
                            keys_hi(f, p, kv)
                        if kv == 1 and e is not None and 2 <= p < 5:
                            forward(e, p - 2)
                    if f is not None:
                        copy_values(f, p)
                    if p == 1 and e is not None:
                        act.wait_ge(xT_tp, ONE + e * 2 + 1)
                        act.copy(xT[:, 0:2, :], bank(M0).rearrange("p (c m) -> p c m", c=2)).then_inc(xT_a, 1)
                if f is not None:
                    rows_of(f, 0)

            between(None, 0)
            with act.Fori(0, B - 1) as b:
                attend(b)
                between(b, b + 1)
            attend(B - 1)
            between(B - 1, None)

        @block.vector
        def _(dve):
            def piece_lo(e, p):
                dve.wait_ge(xh_done, ONE + e * NP + p + 1)
                whole, hi = (lt if p == LAT else turned(rows[p])), xh[:, p % 2, :, 0:rows[p]]
                dve.tensor_tensor(xl[:, p % 2, :, 0:rows[p]], whole, hi.bitcast(F32) if p == LAT else hi,
                                  ALU.subtract).then_inc(xl_done, 1)

            def keys_lo(e, p, kv):
                i, n, c0 = p * KV1 + kv, rows[p] + rows[p] % 2, p * T
                dve.wait_ge(khi, ONE + e * NP * KV1 + i + 1)
                dve.tensor_tensor(kl[:, kv, c0:c0 + n], bank(OB + i % 2)[0:HD1, 0:n], kh[0:HD1, kv, c0:c0 + n],
                                  ALU.subtract).then_inc(klo, 1)

            def values_lo(e, p, t):
                i, m = 2 * p + t, min(P, rows[p] - t * P)
                hi, lo = (a[0:m, i, :, 0:HD1] for a in (vh, vl))
                dve.wait_ge(vhi, ONE + e * KT + i + 1)
                dve.tensor_tensor(lo, bank(M0 + i % 2)[0:m, 0:W].rearrange("p (k e) -> p k e", e=HD1), hi,
                                  ALU.subtract).then_inc(v_done, 1)

            def first_max(e, p):
                for j in range(QT):
                    if j % 4 == 0 and j:
                        values_lo(e, p, j // 4 - 1)
                    if p == 0 and j == 0:
                        dve.wait_ge(mxr_done, ONE + e * KV1)
                    dve.wait_ge(mx_mm, ONE + e * NP * QT + p * QT + j + 1)
                    dve.reduce_max(pm[:, j, p:p + 1], bank(j % 4)[:, 0:rows[p]], AX).then_inc(mx_done, 1)
                for t in range(1, -(-rows[p] // P)):
                    values_lo(e, p, t)

            def max_all(e, kv):
                if kv == 0:
                    dve.wait_ge(mx_done, ONE + (e + 1) * NP * QT)
                else:
                    dve.wait_ge(ring_done, ONE + e * RING + ring["max", kv, NI - 1] + 1)
                dve.wait_ge(row_mm, ONE + e * 2 * KV1 + 2 * kv)
                dve.reduce_max(mx[:, :], pm[:, :, 0:(NP if kv == 0 else len(cuts))], AX).then_inc(mxr_done, 1)

            def ring_item(e, kind, kv, i):
                n = ring[kind, kv, i]
                at = bank(M0 + n % 2)
                if kind == "max" and i == 0:
                    dve.wait_ge(mxr_done, ONE + e * KV1 + kv)
                if kind == "sum" and kv:
                    dve.wait_ge(ring_done, ONE + e * RING + ring["out", kv - 1, TT * G - 1] + 1)
                if kind == "sum" and not kv:
                    dve.wait_ge(ring_done, ONE + e * RING)
                if kind == "out":
                    before = ring["out", kv, i - TT] if i >= TT else ring["sum", kv, 0]
                    dve.wait_ge(ring_done, ONE + e * RING + before + 1)
                    if kv == 0 and i == 0:
                        dve.wait_ge(x_in, ONE + e * 16 + 16)
                dve.wait_ge(ring_mm, ONE + e * RING + n + 1)
                if kind == "max":
                    j, ch = i // len(cuts), i % len(cuts)
                    ins = dve.reduce_max(pm[:, j, ch:ch + 1], at[:, 0:cuts[ch][1]], AX)
                elif kind == "sum":
                    ins = dve.reciprocal(rec[:, :], at[:, 0:QT])
                else:
                    h, t = i // TT, i % TT
                    ins = dve.scalar_tensor_tensor(x[:, t, :], at, rec[:, i:i + 1], x[:, t, :], ALU.mult, ALU.add)
                ins.then_inc(ring_done, 1)

            def attend(e):
                for kv in range(KV1):
                    items = iter(beside(kv))

                    def fill(n):
                        for _ in range(n):
                            item = next(items, None)
                            if item:
                                ring_item(e, *item)

                    for kt in range(KT):
                        n, m = kv * KT + kt, keys[kt]
                        late = kt > KT - 4
                        if kt + 1 < KT:
                            fill(1)
                        dve.wait_ge(exp_done, ONE + e * KV1 * KT * 2 + 2 * n + 1)
                        dve.tensor_tensor(pl[0:m, n % 2, 0:BANK], pf[0:m, 0, :],
                                          ph[0:m, n % 2, 0:BANK].bitcast(F32), ALU.subtract).then_inc(plo_d, 1)
                        if kt + 1 < KT:
                            fill(1)
                        if not late:
                            fill(2)
                        if kv + 1 < KV1 and kt == KT - 3:
                            max_all(e, kv + 1)

            def normalise(chain, e, pause):
                dve.wait_ge(ring_done, ONE + (e + 1) * RING)
                layernorm(dve, chain, xn, x, ln["st"], ln["mv"], ln["v"], ln["t"], ln["u"], ln["y"], pause)\
                    .then_inc(n_done, 1)

            def forward(e, step):
                if step == 0:
                    for t in range(TT):
                        dve.wait_ge(h_mm, ONE + e * TT + t + 1)
                        dve.tensor_tensor(x[:, t, :], bank(M0 + t), x[:, t, :], ALU.add).then_inc(h_done, 1)
                if step == 1:
                    dve.wait_ge(h8_mm, ONE + e + 1)
                    dve.tensor_tensor(h8all[:, ds(e, 1), :].rearrange("p o e -> p (o e)"), bank(M0 + 1)[:, 0:NE],
                                      bias8[:, :], ALU.add).then_inc(h8_done, 1)
                if step == 2:
                    dve.wait_ge(dl_mm, ONE + e + 1)
                    dve.tensor_copy(dlall[:, ds(e, 1), :].rearrange("p o e -> p (o e)"), bank(M0)[:, 0:NE])\
                        .then_inc(dl_done, 1)

            def between(chain, e, f):
                outs = iter(beside(KV1) if e is not None else [])

                def out(n):
                    for _ in range(n):
                        item = next(outs, None)
                        if item:
                            ring_item(e, *item)

                if f is not None:
                    piece_lo(f, 0)
                out(4)
                for p in range(NP):
                    kvs = iter(range(KV1))

                    def next_keys():
                        kv = next(kvs, None)
                        if kv is not None and f is not None:
                            if kv == 2 and p == 0:
                                piece_lo(f, 1)
                            keys_lo(f, p, kv)
                            if kv == 0 and 0 < p < NP - 1:
                                piece_lo(f, p + 1)

                    for kv in range(KV1):
                        next_keys()
                        if p == 0:
                            out(1 if kv < KV1 - 1 else 2)
                        if kv == 0 and p == 1 and e is not None:
                            normalise(chain, e, next_keys)
                        if kv == 1 and e is not None and 2 <= p < 5:
                            forward(e, p - 2)
                    if f is not None:
                        first_max(f, p)
                    if p == 1 and e is not None:
                        dve.wait_ge(xT_tp, ONE + e * 2 + 2)
                        dve.tensor_copy(xT[:, 2:4, :], bank(M0 + 1).rearrange("p (c m) -> p c m", c=2)).then_inc(xT_d, 1)
                if f is not None:
                    max_all(f, 0)

            between(None, None, 0)
            with dve.Fori(0, B - 1) as b:
                attend(b)
                between(Chain(dve, step, LN_STEPS, b), b, b + 1)
            attend(B - 1)
            between(Chain(dve, step, LN_STEPS, B - 1), B - 1, None)


def mixture(nc, A, ident, ps, y_scr, z_scr, h8all, dlall, out):
    NA = B * NE
    with ExitStack() as ctx:
        def sb(name, shape, dt=F32):
            return ctx.enter_context(nc.sbuf_tensor(name, shape, dt))

        def sem(name):
            return ctx.enter_context(nc.semaphore(name))

        y = sb("y", [P, B, TT, D])
        z = sb("z", [R, B, T])
        zp = sb("zp", [R + 1, B, T])
        li = sb("li", [NE, R])
        bm = sb("bm", [R + 1, D])
        ones = sb("ones", [2, P])
        ab = sb("ab", [P, 2, NA])
        pmx = sb("pmx", [P, 2])
        rows2 = sb("rows2", [2, P])
        sc = sb("sc", [2, 4])
        dg = sb("dg", [2, 2])
        scl = sb("scl", [P, 2])
        lg = sb("lg", [P, B, NE])
        pb = sb("pb", [P, B, NE])
        top = sb("top", [P, B, NE])
        wt = sb("wt", [P, B, NE])
        r4 = sb("r4", [P, B])
        wT = sb("wT", [NE, B * P])
        y_in, z_in, w_in, const = sem("y_in"), sem("z_in"), sem("w_in"), sem("const2")
        step, a_in, a_out = sem("dve_step2"), sem("act_asked"), sem("act_done")
        to_pe, from_pe = sem("pe_asked"), sem("pe_done")
        zp_done, d_mm, y_done, o_st = sem("zp_ready"), sem("delta_product"), sem("y_ready"), sem("out_stored")
        block = ctx.enter_context(nc.Block())

        def bank(i, n=BANK):
            return ps[:, i * BANK:i * BANK + n]

        @block.sync
        def _(sp):
            sp.dma_start(bm[0:R, :], A["L1_ffn_Bmat"]).then_inc(w_in, 16)
            sp.dma_start(bm[R:R + 1, :], A["L1_ffn_b"].rearrange("(a n) -> a n", a=1)).then_inc(w_in, 16)
            sp.dma_start(li[:, :], A["L1_ffn_LiMEs"]).then_inc(w_in, 16)
            sp.dma_start(z[:, :, :], z_scr.rearrange("b r t -> r b t")).then_inc(z_in, 16)
            sp.dma_start(y[:, :, :, :].rearrange("p b t d -> p b (t d)"), y_scr.rearrange("b p n -> p b n"))\
                .then_inc(y_in, 16)
            for b in range(B):
                sp.wait_ge(y_done, (b + 1) * TT)
                sp.dma_start(out[b].rearrange("(t p) d -> p t d", p=P), y[:, b, :, :]).then_inc(o_st, 16)
            sp.wait_ge(o_st, 16 * B)

        @block.gpsimd
        def _(pool):
            pool.memset(ones[:, :], 1.0).then_inc(const, 1)
            pool.memset(zp[R:R + 1, :, :], 1.0).then_inc(const, 1)

        @block.tensor
        def _(pe):
            pe.wait_ge(const, 2)
            pe.wait_ge(to_pe, 1)
            pe.matmul(bank(0)[0:2, 0:P], pmx[:, :], ident[:, :], start=True, stop=True).then_inc(from_pe, 1)
            pe.wait_ge(to_pe, 2)
            pe.matmul(bank(1)[:, 0:2], ones[:, :], dg[:, :], start=True, stop=True).then_inc(from_pe, 1)
            pe.wait_ge(to_pe, 3)
            for b in range(B):
                mm = pe.matmul(bank(2)[0:NE, b * P:(b + 1) * P], wt[:, b, :], ident[:, :], start=True, stop=True)
            mm.then_inc(from_pe, 1)
            pe.wait_ge(to_pe, 4)
            pe.wait_ge(w_in, 48)
            pe.matmul(bank(3)[0:R, :], li[:, :], wT[:, :], start=True, stop=True).then_inc(from_pe, 1)
            pe.wait_ge(zp_done, 2)
            for n in range(B * TT):
                if n >= 4:
                    pe.wait_ge(y_done, n - 3)
                b, t = n // TT, n % TT
                pe.matmul(bank(4 + n % 4), zp[:, b, t * P:(t + 1) * P], bm[:, :], start=True, stop=True)\
                    .then_inc(d_mm, 1)

        @block.scalar
        def _(act):
            act.wait_ge(a_in, 1)
            act.activation(pb[:, :, :], lg[:, :, :], ACT.Exp).then_inc(a_out, 1)
            act.wait_ge(a_in, 2)
            act.activation(wt[:, :, :], lg[:, :, :], ACT.Exp, scale=-2.0).then_inc(a_out, 1)

        @block.vector
        def _(dve):
            chain = Chain(dve, step, 0)
            link = chain.link
            flat = "p b e -> p (b e)"
            for i, s in enumerate((h8all, dlall)):
                sf = s[:, :, :].rearrange(flat)
                link(dve.scalar_tensor_tensor(ab[:, i, :], sf, -1.0, sf, ALU.mult, ALU.max))
            dve.reduce_max(pmx[:, :], ab[:, :, :], AX).then_inc(to_pe, 1)
            dve.wait_ge(from_pe, 1)
            link(dve.reduce_max(sc[:, 0:1], bank(0)[0:2, 0:P], AX))
            link(dve.tensor_scalar(sc[:, 1:2], sc[:, 0:1], 1e-6, None, ALU.max))
            link(dve.reciprocal(sc[:, 2:3], sc[:, 1:2]))
            dve.tensor_scalar(dg[:, :], ident[0:2, 0:2], sc[:, 2:3], 0.5, ALU.mult, ALU.mult).then_inc(to_pe, 1)
            dve.wait_ge(from_pe, 2)
            link(dve.tensor_copy(scl[:, :], bank(1)[:, 0:2]))
            link(dve.tensor_scalar(pb[:, :, :], dlall[:, :, :], scl[:, 1:2], None, ALU.mult))
            link(dve.scalar_tensor_tensor(lg[:, :, :], h8all[:, :, :], scl[:, 0:1], pb[:, :, :], ALU.mult, ALU.add))

            def over(a):
                return a.rearrange("p (b o) -> p b o", o=1).broadcast_to([P, B, NE])

            link(dve.reduce_max(r4[:, :], lg[:, :, :], AX))
            dve.tensor_tensor(lg[:, :, :], lg[:, :, :], over(r4[:, :]), ALU.subtract).then_inc(a_in, 1)
            dve.wait_ge(a_out, 1)
            link(dve.reduce_sum(r4[:, :], pb[:, :, :], AX))
            link(dve.reciprocal(r4[:, :], r4[:, :]))
            link(dve.tensor_tensor(pb[:, :, :], pb[:, :, :], over(r4[:, :]), ALU.mult))
            for b in range(B):
                link(dve.max(top[:, b, :], pb[:, b, :]))
            dve.tensor_tensor(lg[:, :, :], pb[:, :, :], top[:, :, 1:2].broadcast_to([P, B, NE]), ALU.subtract)\
                .then_inc(a_in, 1)
            dve.wait_ge(a_out, 2)
            link(dve.tensor_scalar(wt[:, :, :], wt[:, :, :], 1.0, None, ALU.add))
            link(dve.reciprocal(wt[:, :, :], wt[:, :, :]))
            link(dve.tensor_tensor(wt[:, :, :], wt[:, :, :], pb[:, :, :], ALU.mult))
            link(dve.reduce_sum(r4[:, :], wt[:, :, :], AX))
            link(dve.tensor_scalar(r4[:, :], r4[:, :], 1e-9, None, ALU.add))
            link(dve.reciprocal(r4[:, :], r4[:, :]))
            dve.tensor_tensor(wt[:, :, :], wt[:, :, :], over(r4[:, :]), ALU.mult).then_inc(to_pe, 1)
            dve.wait_ge(from_pe, 3)
            dve.tensor_copy(wT[:, :], bank(2)[0:NE, :]).then_inc(to_pe, 1)
            dve.wait_ge(w_in, 48)
            dve.tensor_scalar(bm[0:R, :], bm[0:R, :], 16.0 / R, None, ALU.mult).then_inc(zp_done, 1)
            dve.wait_ge(from_pe, 4)
            dve.wait_ge(z_in, 16)
            dve.tensor_tensor(zp[0:R, :, :].rearrange("r b (a n) -> r (b a) n", n=2),
                              z[:, :, :].rearrange("r b (a n) -> r (b a) n", n=2),
                              bank(3)[0:R, :].rearrange("r (a o) -> r a o", o=1).broadcast_to([R, BANK, 2]), ALU.mult)\
                .then_inc(zp_done, 1)
            dve.wait_ge(y_in, 16)
            for n in range(B * TT):
                dve.wait_ge(d_mm, n + 1)
                dve.tensor_tensor(y[:, n // TT, n % TT, :], bank(4 + n % 4), y[:, n // TT, n % TT, :], ALU.add)\
                    .then_inc(y_done, 1)


_INS = ["x", "ctx_4096", "L0_xattn_Wq_d", "L0_xattn_W_qk", "L0_xattn_Wkv_d", "L0_xattn_Wv_u", "L0_ffn_weight_q",
        "L0_ffn_scale", "L0_ffn_zero_point", "L0_ffn_bias", "L1_xattn_Wq", "L1_xattn_Wk", "L1_xattn_Wv",
        "L1_xattn_Wo", "L1_ffn_W", "L1_ffn_b", "L1_ffn_A", "L1_ffn_Bmat", "L1_ffn_LiMEs"]


def kernel(**inputs):
    import numpy as _np
    import concourse.bacc as _bacc
    from concourse import mybir as _mybir
    from concourse.bass_utils import run_bass_kernel_spmd as _run

    nc = _bacc.Bacc("TRN2", target_bir_lowering=False, num_devices=1)
    arrays, args = {}, {}
    for name in _INS:
        a = _np.ascontiguousarray(inputs[name])
        arrays[f"in_{name}_dram"] = a
        args[name] = nc.dram_tensor(f"in_{name}_dram", a.shape, _mybir.dt.from_np(a.dtype), kind="ExternalInput").ap()
    out = nc.dram_tensor("out_0_dram", (B, T, D), F32, kind="ExternalOutput").ap()
    build(nc, args, out)
    r = _run(nc, [arrays], core_ids=[0])
    return r.results[0]["out_0_dram"]
```

```python
from contextlib import ExitStack

import concourse.bass as bass
from concourse import mybir

F32 = mybir.dt.float32
F32R = mybir.dt.float32r
I32 = mybir.dt.int32
ALU = mybir.AluOpType
ACT = mybir.ActivationFunctionType
AX = mybir.AxisListType.X
ds = bass.ds

P = 128
BANK = 512
B, T, D = 4, 256, 512
NC = 1601
DC = D // P
TT = T // P
EPS = 1e-5

H0, HD0, LQ = 16, 32, 64
S0 = float(HD0) ** -0.5
H1, KV1, HD1 = 16, 4, 96
S1 = float(HD1) ** -0.5
G = 4
NG = H0 // G
GC = G * T
QT = GC // P
R, NE = 32, 8
ONE = 1
RSQRT_GUESS = float(0x5F3759DF)


def widths(total, parts):
    w = total // parts
    cuts = [(i * w, w) for i in range(parts - 1)] + [((parts - 1) * w, total - (parts - 1) * w)]
    return [(s, n, n + n % 2) for s, n in cuts]


class Chain:

    def __init__(self, engine, sem, per, b=0):
        self.engine, self.sem, self.n = engine, sem, 0
        self.base = b * per + ONE if per else 0

    def mark(self, ins):
        self.n += 1
        ins.then_inc(self.sem, 1)

    def link(self, ins):
        self.mark(ins)
        self.engine.wait_ge(self.sem, self.base + self.n)


def layernorm(dve, chain, out, x, st, mv, v, t, u, y, pause=lambda: None):
    chain.link(dve.bn_stats(st[:, 0, :], x[:, 0, :]))
    chain.mark(dve.bn_stats(st[:, 1, :], x[:, 1, :]))
    chain.link(dve.bn_aggr(mv[:, 0, :], st[:, 0, :]))
    chain.mark(dve.tensor_scalar(v[:, 0:1], mv[:, 0, 1:2], EPS, None, ALU.add))
    chain.link(dve.bn_aggr(mv[:, 1, :], st[:, 1, :]))
    chain.link(dve.tensor_scalar(v[:, 1:2], mv[:, 1, 1:2], EPS, None, ALU.add))
    chain.link(dve.tensor_scalar(t[:, :].bitcast(I32), v[:, :].bitcast(I32), 1, None, ALU.logical_shift_right))
    chain.link(dve.tensor_scalar(y[:, :].bitcast(I32), t[:, :].bitcast(I32), -1.0, RSQRT_GUESS, ALU.mult, ALU.add))
    for _ in range(3):
        pause()
        chain.link(dve.tensor_tensor(t[:, :], y[:, :], y[:, :], ALU.mult))
        chain.link(dve.scalar_tensor_tensor(u[:, :], t[:, :], -0.5, v[:, :], ALU.mult, ALU.mult))
        chain.link(dve.scalar_tensor_tensor(y[:, :], u[:, :], 1.5, y[:, :], ALU.add, ALU.mult))
    last = None
    for i in range(TT):
        last = dve.tensor_scalar(out[:, i, :], x[:, i, :], mv[:, i, 0:1], y[:, i:i + 1], ALU.subtract, ALU.mult)
        if i < TT - 1:
            chain.link(last)
    return last


LN_STEPS = 6 + 2 + 9 + TT - 1


def build(nc, A, out):
    q_scr = nc.dram_tensor("q_scr", (B, NG, 2, HD1, GC), F32, kind="Internal").ap()
    x_scr = nc.dram_tensor("x_scr", (B, P, TT * D), F32, kind="Internal").ap()
    lt_scr = nc.dram_tensor("lt_scr", (B, P, DC * T), F32, kind="Internal").ap()
    y_scr = nc.dram_tensor("y_scr", (B, P, TT * D), F32, kind="Internal").ap()
    z_scr = nc.dram_tensor("z_scr", (B, R, T), F32, kind="Internal").ap()
    with ExitStack() as ctx:
        ident = ctx.enter_context(nc.sbuf_tensor("ident", [P, P], F32))
        ps = ctx.enter_context(nc.psum_tensor("ps", [P, 8 * BANK], F32))
        ln = {n: ctx.enter_context(nc.sbuf_tensor(f"ln_{n}", s, F32)) for n, s in
              (("st", [P, TT, 6]), ("mv", [P, TT, 2]), ("v", [P, TT]), ("t", [P, TT]), ("u", [P, TT]), ("y", [P, TT]))}
        wo_scr = nc.dram_tensor("wo_turned", (H1 // G, HD1, G * D), F32, kind="Internal").ap()
        w1_scr = nc.dram_tensor("w1_turned", (P, DC * D), F32, kind="Internal").ap()
        wkvh = ctx.enter_context(nc.sbuf_tensor("wkvh", [P, DC, 2 * KV1 * HD1], F32R))
        wkvl = ctx.enter_context(nc.sbuf_tensor("wkvl", [P, DC, 2 * KV1 * HD1], F32R))
        h8all = ctx.enter_context(nc.sbuf_tensor("h8all", [P, B, NE], F32))
        dlall = ctx.enter_context(nc.sbuf_tensor("dlall", [P, B, NE], F32))
        latent_attention_and_ffn(nc, A, ident, ps, ln, q_scr, x_scr, lt_scr, wkvh, wkvl, wo_scr, w1_scr)
        grouped_attention(nc, A, ident, ps, ln, q_scr, x_scr, lt_scr, y_scr, z_scr,
                          wkvh, wkvl, wo_scr, w1_scr, h8all, dlall)
        mixture(nc, A, ident, ps, y_scr, z_scr, h8all, dlall, out)


def latent_attention_and_ffn(nc, A, ident, ps, ln, q_scr, x_scr, lt_scr, wkvh, wkvl, wo_scr, w1_scr):
    NP = 4
    rows = [BANK, BANK, BANK, NC - 3 * BANK]
    KT = -(-NC // P)
    last_rows = NC - (KT - 1) * P
    keys = [P] * (KT - 1) + [last_rows]
    cuts = widths(NC, 4)
    NI = QT * len(cuts)
    HW = HD0 + 1
    STEPS_F = 2 * LN_STEPS + NG * (1 + TT * 2 - 1) + 2

    with ExitStack() as ctx:
        def sb(name, shape, dt=F32):
            return ctx.enter_context(nc.sbuf_tensor(name, shape, dt))

        def sem(name):
            return ctx.enter_context(nc.semaphore(name))

        in_loop = []

        def counted(name):
            in_loop.append(sem(name))
            return in_loop[-1]

        wqn = sb("wqn", [P, H1 * HD1 // P, D])
        w0i = sb("w0i", [P, DC, D], I32)
        w0n = sb("w0n", [P, DC, D])
        w0s = sb("w0s", [P, DC, D // P])
        w0z = sb("w0z", [P, DC, D // P])
        bias0 = sb("bias0", [P, D])
        wqd = sb("wqd", [P, DC, LQ])
        wqk = sb("wqk", [LQ, H0, 3 * HD0])
        wkv = sb("wkv", [P, DC, 3 * HD0])
        wvu = sb("wvu", [P, NG * 2, 2, HW])
        w0T = sb("w0T", [P, DC, D])
        wqT = sb("wqT", [P, DC, H1 * HD1])
        xa = sb("xa", [P, TT, D])
        xah = sb("xah", [P, TT, D])
        xaT = sb("xaT", [P, DC, T])
        x = sb("x", [P, TT, D])
        xh = sb("xh", [P, TT, D])
        xT = sb("xT", [P, DC, T])
        cnat = sb("cnat", [P, 2, 4, D])
        cT = sb("cT", [P, DC, BANK])
        cst = sb("cst", [HD1 + 1, NC + 1], F32R)
        cf = sb("cf", [HD0, BANK])
        cv = sb("cv", [P, KT, 64])
        cq = sb("cq", [LQ, T])
        ast = sb("ast", [HD1 + 1, H0 * T], F32R)
        pr = sb("pr", [P, 2, GC])
        osb = sb("osb", [P, BANK])
        pm = sb("pm", [P, QT, len(cuts)])
        mx = sb("mx", [P, QT])
        rec = sb("rec", [P, TT * G])
        tmp = sb("tmp", [P, TT, G * HD0])
        qst = sb("qst", [HD1, 2, 2, BANK], F32R)

        const = sem("const")
        w_q, w_0, w_small = sem("w_q_loaded"), sem("w_0_loaded"), sem("w_small_loaded")
        w_lat = sem("w_latent_keys_loaded")
        w_deq, w_tp, w_ev, w_hi = sem("w_dequantised"), sem("w_turned"), sem("w_copied"), sem("w_hi")
        w_kv, w_1, w_o = sem("w_kv_loaded"), sem("w_1_loaded"), sem("w_o_loaded")
        w1_st, wo_st = sem("w_1_stored"), [sem("w_o_stored0"), sem("w_o_stored1")]
        xa_in, x_in = counted("xa_in"), counted("x_in")
        ctx_in = [counted("ctx_in0"), counted("ctx_in1")]
        ctx_tp, c_mm, cnat_tp = counted("ctx_turned"), counted("c_product"), counted("c_turned")
        ctxT_a, ctxT_d = counted("ctxT_by_act"), counted("ctxT_by_dve")
        cf_done, cst_done, cv_done = counted("c_copied"), counted("c_split"), counted("cv_copied")
        xah_done, xaT_tp, xaT_a, xaT_d = counted("xa_ready"), counted("xa_turned"), counted("xaT_by_act"), counted("xaT_by_dve")
        xh_done, xT_tp, xT_a, xT_d = counted("xh_ready"), counted("x_turned"), counted("xT_by_act"), counted("xT_by_dve")
        cq_mm, cq_done, a_mm = counted("cq_product"), counted("cq_copied"), counted("a_product")
        ahi, alo = counted("a_hi"), counted("a_lo")
        mx_mm, mx_done, mxr_done = counted("max_scores"), counted("max_part"), counted("max_ready")
        row_mm, row_done = counted("max_turned"), counted("max_row")
        s_mm, exp_done, av_mm, o_done = counted("scores"), counted("probs"), counted("values"), counted("o_copied")
        bd_mm, post_done = counted("o_turned"), counted("x_attended")
        ffn_mm, ffn_done = counted("ffn_product"), counted("ffn_added")
        q_mm, qhi, qlo = counted("q_product"), counted("q_hi"), counted("q_lo")
        q_st = [counted("q_stored0"), counted("q_stored1")]
        x1_st = counted("x1_stored")
        step_a, step_f = counted("dve_step_a"), counted("dve_step_f")
        block = ctx.enter_context(nc.Block())

        T_0 = H1 * HD1 // P
        T_KV = T_0 + DC
        T_1 = T_KV + 2 * KV1 * HD1 // P
        T_O = T_1 + DC
        wv_rows = [xh[:, 0, :], xh[:, 1, :], osb[:, :]]
        wk_rows = pr[:, :, :].rearrange("p a n -> p (a n)").rearrange("p (a n) -> p a n", n=D)
        w1_rows, w1_out = w0i[:, :, :].bitcast(F32), w0n
        wo_rows = wqn[:, :, :].rearrange("p a n -> p (a n)").rearrange("p (a n) -> p a n", n=H1 * HD1)
        wo_out = qst[:, :, :, :].rearrange("p j a n -> p j (a n)").bitcast(F32)

        def bank(i, n=BANK):
            return ps[:, i * BANK:i * BANK + n]

        OB, M0, M2 = 4, 5, 7
        first_cuts = [(p * BANK, rows[p], rows[p] + rows[p] % 2) for p in range(NP)]

        THIRD = 5
        max_bank = [i % 2 if i < THIRD else (i - THIRD) % 3 for i in range(NI)]

        def row_bank(g, half):
            return (OB, M2)[half] if g == 0 else M0 + half

        def max_cut(g, i):
            if g == 0:
                return i % QT, i // QT, first_cuts[i // QT], i % 4
            return i // len(cuts), i % len(cuts), cuts[i % len(cuts)], M0 + max_bank[i]


        def turned_to(n):
            out, k = (wqT, n) if n < T_0 else (w0T, n - T_0) if n < T_KV else (w1_out, n - T_1)
            return out[:, :, k * P:(k + 1) * P]

        @block.sync
        def _(sp):
            for r in range(3):
                sp.dma_start(wkv[:, :, r * HD0:(r + 1) * HD0],
                             A["L0_xattn_Wkv_d"].rearrange("(c p) n -> p c n", p=P)).then_inc(w_lat, 16)

            def load(b):
                for p in range(NP):
                    sp.wait_ge(ctx_tp, ONE + b * 16 + 4 * max(p - 1, 0))
                    r0 = p * BANK
                    if rows[p] == BANK:
                        src = A["ctx_4096"][ds(b, 1), r0:r0 + BANK, :].rearrange("o (a p) d -> p (o a) d", p=P)
                        sp.dma_start(cnat[:, p % 2, :, :], src).then_inc(ctx_in[p % 2], 16)
                    else:
                        src = A["ctx_4096"][ds(b, 1), r0:r0 + rows[p], :].rearrange("o p d -> p (o d)")
                        sp.dma_start(cnat[0:rows[p], p % 2, 0, :], src).then_inc(ctx_in[p % 2], 16)
                    if p in (0, 3):
                        sp.wait_ge(*((xah_done, ONE + b) if p == 0 else (x1_st, ONE + b * 32)))
                        sp.dma_start((xa if p == 0 else x)[:, :, :],
                                     A["x"][ds(b, 1), :, :].rearrange("o (t p) d -> p (o t) d", p=P))\
                            .then_inc(xa_in if p == 0 else x_in, 16)

            def store_q(e):
                for hp in range(8):
                    sp.wait_ge(qhi, ONE + e * 8 + hp + 1)
                    sp.wait_ge(qlo, ONE + e * 8 + hp + 1)
                    for part in range(2):
                        dst = q_scr[ds(e, 1), hp // 2, part, :, (hp % 2) * BANK:(hp % 2 + 1) * BANK]
                        sp.dma_start(dst.rearrange("o p n -> p (o n)"), qst[:, hp % 2, part, :].bitcast(F32))\
                            .then_inc(q_st[hp % 2], 16)

            load(0)
            sp.dma_start(w0i[:, :, :], A["L0_ffn_weight_q"].rearrange("(a p) i -> p a i", p=P)).then_inc(w_0, 16)
            sp.dma_start(w0s[:, :, :], A["L0_ffn_scale"].rearrange("(a p) i -> p a i", p=P)).then_inc(w_0, 16)
            sp.dma_start(w0z[:, :, :], A["L0_ffn_zero_point"].rearrange("(a p) i -> p a i", p=P)).then_inc(w_0, 16)
            sp.dma_start(wk_rows[:, 0:3, :], A["L1_xattn_Wk"].rearrange("(a p) i -> p a i", p=P)).then_inc(w_kv, 16)
            sp.dma_start(xh[:, :, :], A["L1_xattn_Wv"][0:2 * P].rearrange("(a p) i -> p a i", p=P)).then_inc(w_kv, 16)
            sp.dma_start(osb[:, :], A["L1_xattn_Wv"][2 * P:3 * P]).then_inc(w_kv, 16)
            sp.wait_ge(w_deq, 1)
            sp.dma_start(w1_rows, A["L1_ffn_W"].rearrange("(a p) i -> p a i", p=P)).then_inc(w_1, 16)
            with sp.Fori(0, B - 1) as b:
                load(b + 1)
                store_q(b)
            store_q(B - 1)
            sp.wait_ge(x1_st, ONE + B * 32)
            sp.wait_ge(q_st[0], ONE + B * 128)
            sp.wait_ge(q_st[1], ONE + B * 128)
            sp.wait_ge(w1_st, 16)
            sp.wait_ge(wo_st[0], 16 * H1 // 4)
            sp.wait_ge(wo_st[1], 16 * H1 // 4)

        @block.gpsimd
        def _(pool):
            for s in in_loop:
                pool.sem_inc(s, ONE)
            ready = Chain(pool, const, 0)
            ready.link(pool.memset(ident[:, :], 0.0))
            ready.link(pool.affine_select(out=ident[:, :], in_=ident[:, :], compare_op=ALU.not_equal, fill=1.0,
                                          base=0, pattern=[[-1, P]], channel_multiplier=1))
            ready.link(pool.memset(wvu[:, :, :, :], 0.0))
            for h in range(2):
                ready.link(pool.memset(wvu[64 * h + HD0:64 * h + HW, :, h, HD0:HW], 1.0))
            ready.link(pool.memset(cst[HD1:HD1 + 1, :].bitcast(F32), 1.0))
            ready.link(pool.memset(cst[0:HD1, NC:NC + 1].bitcast(F32), 0.0))
            ready.link(pool.memset(cv[:, :, HD0:64], 0.0))
            ready.link(pool.memset(cv[:, :, HD0:HW], 1.0))

        @block.tensor
        def _(pe):
            pe.wait_ge(const, 9)

            def turn_weight(n):
                if n in (0, T_0, T_KV, T_1, T_O):
                    pe.wait_ge(*{0: (w_q, 16), T_0: (w_deq, 1), T_KV: (w_kv, 48), T_1: (w_1, 16), T_O: (w_o, 64)}[n])
                if n >= 2:
                    pe.wait_ge(w_ev, n - 1)
                for c in range(DC):
                    if n < T_0:
                        src = wqn[:, n, c * P:(c + 1) * P]
                    elif n < T_KV:
                        src = w0n[:, n - T_0, c * P:(c + 1) * P]
                    elif n < T_1:
                        k = n - T_KV
                        src = (wk_rows[:, k, :] if k < 3 else wv_rows[k - 3])[:, c * P:(c + 1) * P]
                    elif n < T_O:
                        src = w1_rows[:, n - T_1, c * P:(c + 1) * P]
                    else:
                        src = wo_rows[:, c, (n - T_O) * HD1:(n - T_O + 1) * HD1]
                    tp = pe.transpose(bank(M0 + n % 2)[0:src.shape[1], c * P:(c + 1) * P], src, ident[:, :])
                tp.then_inc(w_tp, 1)

            def turn_ctx(e, p):
                pe.wait_ge(ctx_in[p % 2], ONE + e * 32 + 16 * (p // 2 + 1))
                if p == 0:
                    pe.wait_ge(exp_done, ONE + e * NG * KT)
                pe.wait_ge(ctxT_a, ONE + e * 8 + 2 * p)
                pe.wait_ge(ctxT_d, ONE + e * 8 + 2 * p)
                for c in range(DC):
                    for t in range(-(-rows[p] // P)):
                        m = min(P, rows[p] - t * P)
                        tp = pe.transpose(ps[:, c * BANK + t * P:c * BANK + t * P + m],
                                          cnat[0:m, p % 2, t, c * P:(c + 1) * P], ident[0:m, 0:m])
                    tp.then_inc(ctx_tp, 1)

            def c_product(e, p):
                pe.wait_ge(ctxT_a, ONE + e * 8 + 2 * p + 2)
                pe.wait_ge(ctxT_d, ONE + e * 8 + 2 * p + 2)
                if p == 0:
                    pe.wait_ge(o_done, ONE + e * NG)
                pe.wait_ge(cst_done, ONE + e * 4 + p)
                for c in range(DC):
                    mm = pe.matmul(bank(OB)[0:HD1, 0:rows[p]], wkv[:, c, :], cT[:, c, 0:rows[p]],
                                   start=(c == 0), stop=(c == DC - 1))
                mm.then_inc(c_mm, 1)

            def turn_c(e, p):
                pe.wait_ge(cf_done, ONE + e * 4 + p + 1)
                pe.wait_ge(cv_done, ONE + e * 4 + p)
                if p == 0:
                    pe.wait_ge(post_done, ONE + e * NG)
                if p == 2:
                    pe.wait_ge(cq_done, ONE + e + 1)
                for t in range(-(-rows[p] // P)):
                    m = min(P, rows[p] - t * P)
                    tp = pe.matmul(bank(M2)[0:m, t * HD0:(t + 1) * HD0], cf[:, t * P:t * P + m],
                                   ident[0:HD0, 0:HD0], start=True, stop=True)
                tp.then_inc(cnat_tp, 1)

            def turn_rows(src, turned):
                for half in range(2):
                    for c in range(2):
                        for t in range(TT):
                            tp = pe.transpose(bank(M0 + half)[:, c * T + t * P:c * T + (t + 1) * P],
                                              src[:, t, (2 * half + c) * P:(2 * half + c + 1) * P], ident[:, :])
                    tp.then_inc(turned, 1)

            def turn_xa(e):
                pe.wait_ge(xah_done, ONE + e + 1)
                pe.wait_ge(ffn_done, ONE + e * TT)
                turn_rows(xah, xaT_tp)

            def turn_x(e, k, more):
                pe.wait_ge(xh_done, ONE + e * 2 + k + 1)
                if k == 0:
                    pe.wait_ge(mx_done, ONE + (e + 1) * NG * NI)
                    pe.wait_ge(row_done, ONE + (e + 1) * 8)
                elif more:
                    pe.wait_ge(alo, ONE + (e + 2) * 8)
                else:
                    pe.wait_ge(ffn_done, ONE + (e + 1) * TT)
                turn_rows(xh, xT_tp)

            def latent_queries(e):
                pe.wait_ge(xaT_a, ONE + e + 1)
                pe.wait_ge(xaT_d, ONE + e + 1)
                pe.wait_ge(cv_done, ONE + e * 4 + 2)
                for c in range(DC):
                    mm = pe.matmul(bank(M2)[0:LQ, 0:T], wqd[:, c, :], xaT[:, c, :],
                                   start=(c == 0), stop=(c == DC - 1))
                mm.then_inc(cq_mm, 1)

            def queries(e, hp):
                if hp == 0:
                    pe.wait_ge(cq_done, ONE + e + 1)
                else:
                    pe.wait_ge(alo, ONE + e * 8 + hp - 1)
                for j in range(2):
                    mm = pe.matmul(bank(M0 + hp % 2)[0:HD1, j * T:(j + 1) * T], wqk[:, 2 * hp + j, :], cq[:, :],
                                   start=True, stop=True)
                mm.then_inc(a_mm, 1)

            def max_item(e, g, i):
                n = g * NI + i
                j, ch, (k0, _, k), at = max_cut(g, i)
                if g == 0:
                    if i == 0:
                        pe.wait_ge(alo, ONE + e * 8 + 8)
                        pe.wait_ge(ctxT_a, ONE + e * 8 + 8)
                        pe.wait_ge(ctxT_d, ONE + e * 8 + 8)
                    if j == 0:
                        pe.wait_ge(cst_done, ONE + e * 4 + ch + 1)
                    if i >= 4:
                        pe.wait_ge(mx_done, ONE + e * NG * NI + i - 3)
                elif i < 2:
                    pe.wait_ge(*((row_done, ONE + e * 8 + 2 * g) if g > 1 else (qlo, ONE + e * 8)))
                elif i == THIRD + 2:
                    pe.wait_ge(post_done, ONE + e * NG + g - 1)
                else:
                    before = max(k for k in range(i) if max_bank[k] == max_bank[i])
                    pe.wait_ge(mx_done, ONE + e * NG * NI + g * NI + before + 1)
                pe.matmul(bank(at)[:, 0:k], ast[0:HD1, g * GC + j * P:g * GC + (j + 1) * P],
                          cst[0:HD1, k0:k0 + k], start=True, stop=True).then_inc(mx_mm, 1)

            def max_rows(e, g):
                pe.wait_ge(mxr_done, ONE + e * NG + g + 1)
                if g == 0:
                    pe.wait_ge(cst_done, ONE + e * 4 + 4)
                    pe.wait_ge(cv_done, ONE + e * 4 + 4)
                for half in range(2):
                    for j in range(4):
                        mm = pe.matmul(bank(row_bank(g, half))[HD1:HD1 + 1, j * P:(j + 1) * P],
                                       mx[:, 4 * half + j:4 * half + j + 1], ident[:, :], start=True, stop=True)
                    mm.then_inc(row_mm, 1)

            def scores(e, g, kt, fill):
                n = g * KT + kt
                if kt == 0:
                    pe.wait_ge(row_done, ONE + e * 8 + 2 * g + 2)
                if n >= 2:
                    pe.wait_ge(exp_done, ONE + e * NG * KT + n - 1)
                else:
                    pe.wait_ge(mx_done, ONE + e * NG * NI + NI)
                for half in range(2):
                    mm = pe.matmul(ps[0:keys[kt], ((n % 2) * 2 + half) * BANK:((n % 2) * 2 + half + 1) * BANK],
                                   cst[0:HD1 + 1, kt * P:kt * P + keys[kt]],
                                   ast[:, g * GC + half * BANK:g * GC + (half + 1) * BANK], start=True, stop=True)
                    if half == 0:
                        fill()
                mm.then_inc(s_mm, 1)

            def values(e, g, kt):
                n = g * KT + kt
                if kt == 0:
                    pe.wait_ge(o_done, ONE + e * NG + g)
                pe.wait_ge(exp_done, ONE + e * NG * KT + n + 1)
                for half in range(2):
                    mm = pe.matmul(bank(OB)[64 * half:64 * half + 64, :], cv[0:keys[kt], kt, :],
                                   pr[0:keys[kt], n % 2, half * BANK:(half + 1) * BANK],
                                   start=(kt == 0), stop=(kt == KT - 1))
                mm.then_inc(av_mm, 1)

            def raise_values(e, g):
                pe.wait_ge(o_done, ONE + e * NG + g + 1)
                pe.wait_ge(post_done, ONE + e * NG + g)
                if g == 0:
                    pe.wait_ge(cv_done, ONE + e * 4 + 4)
                for t in range(TT):
                    for c in range(2):
                        mm = pe.matmul(bank(M2)[:, (t * 2 + c) * 2 * HW:(t * 2 + c + 1) * 2 * HW],
                                       osb[:, c * T + t * P:c * T + (t + 1) * P],
                                       wvu[:, 2 * g + c, :, :].rearrange("p h e -> p (h e)"),
                                       start=True, stop=True)
                mm.then_inc(bd_mm, 1)

            def attend(e):
                pe.wait_ge(cst_done, ONE + e * 4 + 4)
                pe.wait_ge(cv_done, ONE + e * 4 + 4)
                for g in range(NG):
                    items = iter(range(NI if g + 1 < NG else 0))

                    def fill():
                        i = next(items, None)
                        if i is not None:
                            max_item(e, g + 1, i)

                    scores(e, g, 0, lambda: None)
                    for kt in range(KT):
                        if kt + 1 < KT:
                            scores(e, g, kt + 1, fill)
                            fill()
                        if g + 1 < NG and kt == KT - 2:
                            max_rows(e, g + 1)
                        if kt == 1 and g > 0:
                            raise_values(e, g - 1)
                        values(e, g, kt)
                        if kt < KT - 2:
                            fill()

            def between(e, f):
                if f is not None:
                    turn_ctx(f, 0)
                if e is not None:
                    raise_values(e, NG - 1)
                if e is None:
                    pe.wait_ge(w_lat, 48)
                if f is not None:
                    c_product(f, 0)
                    turn_ctx(f, 1)
                    turn_c(f, 0)
                    c_product(f, 1)
                if e is not None:
                    turn_x(e, 0, False)
                    pe.wait_ge(xT_a, ONE + e * 2 + 1)
                    pe.wait_ge(xT_d, ONE + e * 2 + 1)
                    for t in range(TT):
                        for c in range(DC):
                            mm = pe.matmul(bank(M0 + t), xT[:, c, t * P:(t + 1) * P], w0T[:, c, :],
                                           start=(c == 0), stop=(c == DC - 1))
                        mm.then_inc(ffn_mm, 1)
                if f is not None:
                    turn_ctx(f, 2)
                    turn_c(f, 1)
                    turn_xa(f)
                    if e is None:
                        pe.wait_ge(w_small, 16 * 9)
                    latent_queries(f)
                    for hp in range(4):
                        queries(f, hp)
                    c_product(f, 2)
                    for hp in range(4, 8):
                        queries(f, hp)
                    turn_ctx(f, 3)
                    turn_c(f, 2)
                if e is not None:
                    turn_x(e, 1, f is not None)
                if f is not None:
                    c_product(f, 3)
                    turn_c(f, 3)
                if e is not None:
                    pe.wait_ge(xT_a, ONE + e * 2 + 2)
                    pe.wait_ge(xT_d, ONE + e * 2 + 2)
                items = iter(range(NI if f is not None else 0))

                def fill():
                    i = next(items, None)
                    if i is not None:
                        max_item(f, 0, i)

                if e is None:
                    for n in range(T_O):
                        turn_weight(n)
                        for _ in range(2 if n < NI - T_O else 1):
                            fill()
                for hp in range(8):
                    if hp == 7 and f is not None:
                        max_rows(f, 0)
                    if e is not None:
                        if hp >= 2:
                            pe.wait_ge(qlo, ONE + e * 8 + hp - 1)
                        for j in range(2):
                            h = 2 * hp + j
                            for c in range(DC):
                                mm = pe.matmul(bank(M0 + hp % 2)[0:HD1, j * T:(j + 1) * T],
                                               wqT[:, c, h * HD1:(h + 1) * HD1], xT[:, c, :],
                                               start=(c == 0), stop=(c == DC - 1))
                                if c != 1:
                                    fill()
                        mm.then_inc(q_mm, 1)

            between(None, 0)
            for n in range(T_O, T_O + H1):
                turn_weight(n)
            pe.wait_ge(w_ev, T_O + H1)
            with pe.Fori(0, B - 1) as b:
                attend(b)
                between(b, b + 1)
            attend(B - 1)
            between(B - 1, None)

        @block.scalar
        def _(act):
            def copy_weights(first, end):
                for n in range(first, end):
                    src = bank(M0 + n % 2).rearrange("p (c m) -> p c m", c=DC)
                    if T_KV <= n < T_1:
                        act.wait_ge(w_tp, n + 1)
                        act.copy(wkvh[:, :, (n - T_KV) * P:(n - T_KV + 1) * P], src).then_inc(w_hi, 1)
                    elif n % 2 == 0:
                        act.wait_ge(w_tp, n + 1)
                        if n:
                            act.wait_ge(w_ev, n)
                        if n >= T_O:
                            pair = (n - T_O) // 2
                            if pair >= 2:
                                act.wait_ge(wo_st[pair % 2], 16 * (pair // 2))
                            act.copy(wo_out[:, pair % 2, 0:D], bank(M0)[0:HD1, :]).then_inc(w_ev, 1)
                            act.wait_ge(w_ev, n + 2)
                            act.dma_start(wo_scr[pair // 2, :, (pair % 2) * 2 * D:(pair % 2 + 1) * 2 * D],
                                          wo_out[:, pair % 2, :]).then_inc(wo_st[pair % 2], 16)
                        else:
                            act.copy(turned_to(n), src).then_inc(w_ev, 1)
                    if n < T_0 and n % 3 == 2:
                        act.wait_ge(w_tp, n + 1)
                        act.dma_start(wo_rows[:, n // 3, :], A["L1_xattn_Wo"][n // 3 * P:(n // 3 + 1) * P])\
                            .then_inc(w_o, 16)

            act.dma_start(wqd[:, :, :], A["L0_xattn_Wq_d"].rearrange("(c p) n -> p c n", p=P)).then_inc(w_small, 16)
            for r in range(3):
                act.dma_start(wqk[:, :, r * HD0:(r + 1) * HD0],
                              A["L0_xattn_W_qk"].rearrange("l (h e) -> l h e", e=HD0)).then_inc(w_small, 16)
            act.wait_ge(const, 3)
            up = A["L0_xattn_Wv_u"].rearrange("l (g h c e) -> l h g c e", g=NG, h=2, c=2)
            for h in range(2):
                for c in range(2):
                    act.dma_start(wvu[64 * h:64 * h + HD0, c:2 * NG:2, h, 0:HD0], up[:, h, :, c, :])\
                        .then_inc(w_small, 16)
            act.dma_start(bias0[:, :], A["L0_ffn_bias"].rearrange("(a n) -> a n", a=1).to_broadcast([P, D]))\
                .then_inc(w_small, 16)

            def turned_ctx(e, p):
                for c in (0, 2):
                    act.wait_ge(ctx_tp, ONE + e * 16 + 4 * p + c + 1)
                    act.wait_ge(c_mm, ONE + e * 4 + p)
                    act.copy(cT[:, c, 0:rows[p]], bank(c, rows[p])).then_inc(ctxT_a, 1)

            def copy_c(e, p):
                act.wait_ge(c_mm, ONE + e * 4 + p + 1)
                act.copy(cst[0:HD1, p * BANK:p * BANK + rows[p]], bank(OB)[0:HD1, 0:rows[p]])
                act.wait_ge(cnat_tp, ONE + e * 4 + p)
                act.copy(cf[:, 0:rows[p]], bank(OB)[0:HD0, 0:rows[p]]).then_inc(cf_done, 1)

            def turned_xa(e):
                act.wait_ge(xaT_tp, ONE + e * 2 + 1)
                act.wait_ge(cq_mm, ONE + e)
                act.copy(xaT[:, 0:2, :], bank(M0).rearrange("p (c m) -> p c m", c=2)).then_inc(xaT_a, 1)

            def turned_x(e, k):
                act.wait_ge(xT_tp, ONE + e * 4 + 2 * k + 1)
                if k == 0:
                    act.wait_ge(x1_st, ONE + e * 32)
                else:
                    act.wait_ge(ffn_mm, ONE + e * TT + TT)
                act.copy(xT[:, 0:2, :], bank(M0).rearrange("p (c m) -> p c m", c=2)).then_inc(xT_a, 1)

            def copy_queries(e, hp):
                act.wait_ge(a_mm, ONE + e * 8 + hp + 1)
                act.copy(ast[0:HD1, hp * BANK:(hp + 1) * BANK], bank(M0 + hp % 2)[0:HD1, :]).then_inc(ahi, 1)

            def rows_of(e, g):
                for half in range(2):
                    act.wait_ge(row_mm, ONE + e * 8 + 2 * g + half + 1)
                    act.mul(ast[HD1:HD1 + 1, g * GC + half * BANK:g * GC + (half + 1) * BANK],
                            bank(row_bank(g, half))[HD1:HD1 + 1, :], -1.0).then_inc(row_done, 1)

            def attend(e):
                for g in range(NG):
                    for kt in range(KT):
                        n = g * KT + kt
                        act.wait_ge(s_mm, ONE + e * NG * KT + n + 1)
                        act.wait_ge(av_mm, ONE + e * NG * KT + max(n - 1, 0))
                        act.activation(pr[0:keys[kt], n % 2, :],
                                       ps[0:keys[kt], (n % 2) * 2 * BANK:((n % 2) * 2 + 2) * BANK],
                                       ACT.Exp, scale=S0).then_inc(exp_done, 1)
                    if g + 1 < NG:
                        rows_of(e, g + 1)
                    act.wait_ge(av_mm, ONE + e * NG * KT + (g + 1) * KT)
                    act.wait_ge(bd_mm, ONE + e * NG + g)
                    act.copy(osb[:, :], bank(OB)).then_inc(o_done, 1)

            def between(e, f):
                if f is not None:
                    turned_ctx(f, 0)
                    copy_c(f, 0)
                    if e is None:
                        act.dma_start(wqn[:, :, :], A["L1_xattn_Wq"].rearrange("(a p) i -> p a i", p=P)).then_inc(w_q, 16)
                    turned_ctx(f, 1)
                if e is not None:
                    turned_x(e, 0)
                if f is not None:
                    copy_c(f, 1)
                    turned_ctx(f, 2)
                    turned_xa(f)
                    act.wait_ge(cq_mm, ONE + f + 1)
                    act.copy(cq[:, :], bank(M2)[0:LQ, 0:T]).then_inc(cq_done, 1)
                    for hp in range(4):
                        copy_queries(f, hp)
                    copy_c(f, 2)
                    for hp in range(4, 8):
                        copy_queries(f, hp)
                    turned_ctx(f, 3)
                if e is not None:
                    turned_x(e, 1)
                if f is not None:
                    copy_c(f, 3)
                if e is not None:
                    act.wait_ge(xT_d, ONE + e * 2 + 2)
                    act.wait_ge(xT_a, ONE + e * 2 + 2)
                    act.wait_ge(step_f, ONE + (e + 1) * STEPS_F)
                    act.dma_start(x_scr[ds(e, 1), :, :].rearrange("o p n -> p (o n)"),
                                  x[:, :, :].rearrange("p a b -> p (a b)")).then_inc(x1_st, 16)
                    act.dma_start(lt_scr[ds(e, 1), :, :].rearrange("o p n -> p (o n)"),
                                  xT[:, :, :].rearrange("p a b -> p (a b)")).then_inc(x1_st, 16)
                if e is not None:
                    for hp in range(8):
                        if hp == 7 and f is not None:
                            rows_of(f, 0)
                        act.wait_ge(q_mm, ONE + e * 8 + hp + 1)
                        act.wait_ge(q_st[hp % 2], ONE + e * 128 + 32 * (hp // 2))
                        act.copy(qst[:, hp % 2, 0, :], bank(M0 + hp % 2)[0:HD1, :]).then_inc(qhi, 1)
                elif f is not None:
                    copy_weights(0, T_O)
                    rows_of(f, 0)

            between(None, 0)
            act.wait_ge(w_ev, T_O)
            act.dma_start(w1_scr, w1_out[:, :, :].rearrange("p a b -> p (a b)")).then_inc(w1_st, 16)
            copy_weights(T_O, T_O + H1)
            act.wait_ge(wo_st[0], 16 * H1 // 4)
            act.wait_ge(wo_st[1], 16 * H1 // 4)
            with act.Fori(0, B - 1) as b:
                attend(b)
                between(b, b + 1)
            attend(B - 1)
            between(B - 1, None)

        @block.vector
        def _(dve):
            def copy_weights(first, end):
                for n in range(first, end):
                    src = bank(M0 + n % 2).rearrange("p (c m) -> p c m", c=DC)
                    if T_KV <= n < T_1:
                        cols = slice((n - T_KV) * P, (n - T_KV + 1) * P)
                        dve.wait_ge(w_hi, n - T_KV + 1)
                        dve.wait_ge(w_ev, n)
                        dve.tensor_tensor(wkvl[:, :, cols], src, wkvh[:, :, cols], ALU.subtract).then_inc(w_ev, 1)
                    elif n % 2:
                        dve.wait_ge(w_tp, n + 1)
                        dve.wait_ge(w_ev, n)
                        if n >= T_O:
                            pair = (n - T_O) // 2
                            if pair >= 2:
                                dve.wait_ge(wo_st[pair % 2], 16 * (pair // 2))
                            dve.tensor_copy(wo_out[:, pair % 2, D:2 * D], bank(M0 + 1)[0:HD1, :]).then_inc(w_ev, 1)
                        else:
                            dve.tensor_copy(turned_to(n), src).then_inc(w_ev, 1)

            dve.wait_ge(const, 9)

            def dequantise(o):
                if o == 0:
                    dve.wait_ge(w_0, 48)
                for i in range(DC):
                    last = dve.tensor_scalar(w0n[:, o, i * P:(i + 1) * P], w0i[:, o, i * P:(i + 1) * P],
                                             w0z[:, o, i:i + 1], w0s[:, o, i:i + 1], ALU.subtract, ALU.mult)
                if o == DC - 1:
                    last.then_inc(w_deq, 1)

            def turned_ctx(e, p):
                for c in (1, 3):
                    dve.wait_ge(ctx_tp, ONE + e * 16 + 4 * p + c + 1)
                    dve.wait_ge(c_mm, ONE + e * 4 + p)
                    dve.tensor_copy(cT[:, c, 0:rows[p]], bank(c, rows[p])).then_inc(ctxT_d, 1)

            def split_c(e, p):
                lo = cst[HD0:2 * HD0, p * BANK:p * BANK + rows[p]]
                dve.wait_ge(cf_done, ONE + e * 4 + p + 1)
                dve.tensor_tensor(lo, bank(OB)[HD0:2 * HD0, 0:rows[p]], lo, ALU.subtract).then_inc(cst_done, 1)

            def turned_c(e, p):
                dve.wait_ge(cnat_tp, ONE + e * 4 + p + 1)
                nt, m = -(-rows[p] // P), min(P, rows[p])
                dve.tensor_copy(cv[0:m, 4 * p:4 * p + nt, 0:HD0],
                                bank(M2)[0:m, 0:nt * HD0].rearrange("p (t e) -> p t e", e=HD0)).then_inc(cv_done, 1)

            def normalise_xa(e):
                dve.wait_ge(xa_in, ONE + e * 16 + 16)
                dve.wait_ge(xaT_tp, ONE + e * 2)
                chain = Chain(dve, step_a, LN_STEPS, e)
                layernorm(dve, chain, xah, xa, ln["st"], ln["mv"], ln["v"], ln["t"], ln["u"], ln["y"])\
                    .then_inc(xah_done, 1)

            def normalise(chain, e, k, pause):
                dve.wait_ge(xT_tp, ONE + e * 4 + 2 * k)
                layernorm(dve, chain, xh, x, ln["st"], ln["mv"], ln["v"], ln["t"], ln["u"], ln["y"], pause)\
                    .then_inc(xh_done, 1)

            def turned_xa(e):
                dve.wait_ge(xaT_tp, ONE + e * 2 + 2)
                dve.wait_ge(cq_mm, ONE + e)
                dve.tensor_copy(xaT[:, 2:4, :], bank(M0 + 1).rearrange("p (c m) -> p c m", c=2)).then_inc(xaT_d, 1)

            def turned_x(e, k):
                dve.wait_ge(xT_tp, ONE + e * 4 + 2 * k + 2)
                if k == 0:
                    dve.wait_ge(x1_st, ONE + e * 32)
                else:
                    dve.wait_ge(ffn_mm, ONE + e * TT + TT)
                dve.tensor_copy(xT[:, 2:4, :], bank(M0 + 1).rearrange("p (c m) -> p c m", c=2)).then_inc(xT_d, 1)

            def split_queries(e, hp):
                lo = ast[2 * HD0:3 * HD0, hp * BANK:(hp + 1) * BANK]
                dve.wait_ge(ahi, ONE + e * 8 + hp + 1)
                dve.tensor_tensor(lo, bank(M0 + hp % 2)[2 * HD0:3 * HD0, :], lo, ALU.subtract).then_inc(alo, 1)

            def max_part(e, g, i):
                n = g * NI + i
                if i == 0:
                    dve.wait_ge(mxr_done, ONE + e * NG + g)
                dve.wait_ge(mx_mm, ONE + e * NG * NI + n + 1)
                j, ch, (_, k, _), at = max_cut(g, i)
                dve.reduce_max(pm[:, j, ch:ch + 1], bank(at)[:, 0:k], AX).then_inc(mx_done, 1)

            def max_all(e, g):
                dve.wait_ge(mx_done, ONE + e * NG * NI + (g + 1) * NI)
                dve.wait_ge(row_mm, ONE + e * 8 + 2 * g)
                dve.reduce_max(mx[:, :], pm[:, :, :], AX).then_inc(mxr_done, 1)

            def attended(chain, e, g):
                dve.wait_ge(bd_mm, ONE + e * NG + g + 1)
                if g == 0:
                    dve.wait_ge(x_in, ONE + e * 16 + 16)
                o = bank(M2)[:, 0:TT * G * HW].rearrange("p (t c h e) -> p t c h e", t=TT, c=2, h=2)
                r = rec[:, :].rearrange("p (t c h e) -> p t c h e", t=TT, c=2, e=1)
                chain.link(dve.reciprocal(rec[:, :], bank(M2)[:, 0:TT * G * HW]
                                          .rearrange("p (n e) -> p n e", e=HW)[:, :, HD0]))
                for t in range(TT):
                    xs = x[:, t, g * P:(g + 1) * P].rearrange("p (h c e) -> p c h e", h=2, c=2)
                    tm = tmp[:, t, :].rearrange("p (c h e) -> p c h e", c=2, h=2)
                    chain.link(dve.tensor_tensor(tm, o[:, t, :, :, 0:HD0],
                                                 r[:, t].broadcast_to([P, 2, 2, HD0]), ALU.mult))
                    last = dve.tensor_tensor(xs, xs, tm, ALU.add)
                    if t < TT - 1:
                        chain.link(last)
                last.then_inc(post_done, 1)
                dve.wait_ge(post_done, ONE + e * NG + g + 1)

            def attend(chain, e):
                for g in range(NG):
                    items = iter(range(NI if g + 1 < NG else 0))

                    def fill(n):
                        for _ in range(n):
                            i = next(items, None)
                            if i is not None:
                                max_part(e, g + 1, i)

                    for kt in range(KT):
                        if kt + 1 < KT:
                            fill(2)
                        if kt == 1 and g > 0:
                            attended(chain, e, g - 1)
                        if kt < KT - 2:
                            fill(1)
                        if g + 1 < NG and kt == KT - 2:
                            max_all(e, g + 1)

            def between(chain, e, f):
                parts = iter(range(3))

                def latent_keys():
                    part = next(parts, None) if f is not None else None
                    if part == 0:
                        split_c(f, 0)
                    if part == 1:
                        turned_ctx(f, 1)
                    if part == 2:
                        turned_c(f, 0)

                if f is not None:
                    turned_ctx(f, 0)
                if e is not None:
                    attended(chain, e, NG - 1)
                    normalise(chain, e, 0, latent_keys)
                for _ in range(3):
                    latent_keys()
                if e is not None:
                    turned_x(e, 0)
                if f is not None:
                    normalise_xa(f)
                    split_c(f, 1)
                if e is not None:
                    for t in range(TT):
                        dve.wait_ge(ffn_mm, ONE + e * TT + t + 1)
                        dve.tensor_tensor(x[:, t, :], bank(M0 + t), x[:, t, :], ALU.add).then_inc(ffn_done, 1)
                        dve.wait_ge(ffn_done, ONE + e * TT + t + 1)
                        chain.link(dve.tensor_tensor(x[:, t, :], x[:, t, :], bias0[:, :], ALU.add))
                pairs = iter(range(4))

                def next_queries():
                    hp = next(pairs, None)
                    if hp is not None and f is not None:
                        split_queries(f, hp)

                if f is not None:
                    turned_ctx(f, 2)
                    turned_c(f, 1)
                    turned_xa(f)
                if e is not None:
                    normalise(chain, e, 1, next_queries)
                for _ in range(4):
                    next_queries()
                if f is not None:
                    split_c(f, 2)
                    for hp in range(4, 8):
                        split_queries(f, hp)
                if f is not None:
                    turned_ctx(f, 3)
                    turned_c(f, 2)
                if e is not None:
                    turned_x(e, 1)
                if f is not None:
                    split_c(f, 3)
                    turned_c(f, 3)
                items = iter(range(NI if f is not None else 0))

                def fill(n):
                    for _ in range(n):
                        i = next(items, None)
                        if i is not None:
                            max_part(f, 0, i)

                if e is None:
                    for n in range(T_O):
                        copy_weights(n, n + 1)
                        fill(2 if n < NI - T_O else 1)
                        if n < T_0 and n % 3 == 1:
                            dequantise(n // 3)
                for hp in range(8):
                    fill(6)
                    if hp == 6 and f is not None:
                        max_all(f, 0)
                    if e is not None:
                        dve.wait_ge(qhi, ONE + e * 8 + hp + 1)
                        dve.tensor_tensor(qst[:, hp % 2, 1, :], bank(M0 + hp % 2)[0:HD1, :], qst[:, hp % 2, 0, :],
                                          ALU.subtract).then_inc(qlo, 1)
                if e is not None:
                    assert chain.n == STEPS_F, (chain.n, STEPS_F)

            between(None, None, 0)
            dve.wait_ge(w_small, 16 * 9)
            copy_weights(T_O, T_O + H1)
            with dve.Fori(0, B - 1) as b:
                chain = Chain(dve, step_f, STEPS_F, b)
                attend(chain, b)
                between(chain, b, b + 1)
            chain = Chain(dve, step_f, STEPS_F, B - 1)
            attend(chain, B - 1)
            between(chain, B - 1, None)


def grouped_attention(nc, A, ident, ps, ln, q_scr, x_scr, lt_scr, y_scr, z_scr, wkvh, wkvl, wo_scr, w1_scr, h8all,
                      dlall):
    W = KV1 * HD1
    NP = 7
    LAT = 5
    rows = [T] * 6 + [NC - 5 * T]
    NK = T + NC
    KT = -(-NK // P)
    keys = [P] * (KT - 1) + [NK - (KT - 1) * P]
    cuts = widths(NK, 4)
    NI = QT * len(cuts)
    RING = (KV1 - 1) * NI + KV1 * (1 + TT * G)
    XW = rows[-1] + 1

    with ExitStack() as ctx:
        def sb(name, shape, dt=F32):
            return ctx.enter_context(nc.sbuf_tensor(name, shape, dt))

        def sem(name):
            return ctx.enter_context(nc.semaphore(name))

        in_loop = []

        def counted(name):
            in_loop.append(sem(name))
            return in_loop[-1]

        kh = sb("kh", [HD1 + 1, KV1, NK + 1], F32R)
        kl = sb("kl", [HD1, KV1, NK + 1], F32R)
        vh = sb("vh", [P, KT, KV1, HD1 + 1], F32R)
        vl = sb("vl", [P, KT, KV1, HD1 + 1], F32R)
        qh = sb("qh", [HD1 + 1, 2, GC], F32R)
        ql = sb("ql", [HD1, 2, GC], F32R)
        woT = sb("woT", [HD1, G, D])
        nat = sb("nat", [P, 2, 3, D])
        parts = sb("parts", [P, 2, 2, DC * XW], F32R)
        xT = sb("xT1", [P, DC, T])
        x = sb("x1", [P, TT, D])
        o = sb("o1", [P, GC])
        rec = sb("rec1", [P, G * TT])
        pm = sb("pm1", [P, QT, NP])
        mx = sb("mx1", [P, QT])
        aw = sb("aw", [P, DC, R])
        w1T = sb("w1T", [P, DC, D])
        liT = sb("liT", [R, NE])
        bias8 = sb("bias8", [P, NE])
        zb = sb("zb", [R, T])
        one = sb("one", [HD1 + 1, 2])

        w_small, const = sem("w_small1"), sem("const1")
        wo_in = counted("wo_in")
        x_in, piece_in = counted("x1_in"), [counted("piece_in0"), counted("piece_in1")]
        q_in = [counted("q_in0"), counted("q_in1")]
        tp, xh_done, xl_done = counted("piece_turned"), counted("piece_hi"), counted("piece_lo")
        k_mm, khi, klo, v_mm, vhi, v_done = counted("k_product"), counted("k_hi"), counted("k_lo"), counted("v_product"), counted("v_hi"), counted("v_lo")
        mx_mm, mx_done = counted("first_max_scores1"), counted("first_max_part1")
        ring_mm, ring_done, mxr_done = counted("ring_product"), counted("ring_read"), counted("max_ready1")
        row_mm, row_done = counted("max_turned1"), counted("max_row1")
        s_mm, phi, exp_done = counted("scores1"), counted("probs_hi"), counted("probs1")
        plo = counted("probs_lo")
        av_mm, o_done = counted("values1"), counted("o_copied1")
        n_done, xT_tp, xT_a, xT_d = counted("x_normal"), counted("x_turned1"), counted("xT1_by_act"), counted("xT1_by_dve")
        z_mm, z_done, h8_mm, h8_done = counted("z_product"), counted("z_copied"), counted("h8_product"), counted("h8_kept")
        dl_mm, dl_done, h_mm, h_done = counted("dl_product"), counted("dl_kept"), counted("h_product"), counted("h_added")
        y_st, z_st = counted("y_stored"), counted("z_stored")
        step = counted("dve_step1")
        block = ctx.enter_context(nc.Block())
        OB, M0 = 4, 6

        def bank(i, n=BANK):
            return ps[:, i * BANK:i * BANK + n]

        lt = nat[:, LAT % 2, :, :].rearrange("p a d -> p (a d)")[:, 0:DC * T].rearrange("p (c m) -> p c m", c=DC)
        xn = o[:, :].rearrange("p (t d) -> p t d", t=TT)
        xh = parts[:, 0, :, :].rearrange("p i (c m) -> p i c m", c=DC)
        xl = parts[:, 1, :, :].rearrange("p i (c m) -> p i c m", c=DC)
        ph, pl = parts[:, 0, :, 0:GC], parts[:, 1, :, 0:GC]
        pf = xT[:, :, :].rearrange("p (h c) m -> p h (c m)", h=2)

        def beside(kv):
            maxima = [("max", kv + 1, i) for i in range(NI)] if kv + 1 < KV1 else []
            if kv < 1:
                return maxima
            order, maxima = maxima[:6] + [("sum", kv - 1, 0)], maxima[6:]
            for i in range(TT * G):
                order += maxima[:2] + [("out", kv - 1, i)]
                maxima = maxima[2:]
            return order + maxima

        ring = {}
        for kv in range(KV1 + 1):
            for item in beside(kv):
                ring[item] = len(ring)
        assert len(ring) == RING


        def row_bank(kv, half):
            return (OB if kv == 0 else M0) + half

        def piece_loaded(e, p):
            return ONE + e * 16 * (NP // 2, NP // 2 + 2)[p % 2 == 0] + 16 * (p // 2 + 1) + 16 * (p == NP - 1)

        @block.sync
        def _(sp):
            with sp.Fori(0, B) as b:
                def load_q(kv):
                    for part, q in ((0, qh[0:HD1, kv % 2, :]), (1, ql[:, kv % 2, :])):
                        sp.dma_start(q.bitcast(F32), q_scr[ds(b, 1), kv, part, :, :].rearrange("o p n -> p (o n)"))\
                            .then_inc(q_in[kv % 2], 16)

                def load_wo(kv):
                    used = ring["out", kv - 1, TT * G - 1] + 1 if kv else 0
                    sp.wait_ge(ring_mm, ONE + b * RING + used)
                    sp.dma_start(woT[:, :, :].rearrange("p h d -> p (h d)"), wo_scr[kv]).then_inc(wo_in, 16)

                for p in range(NP):
                    if p == LAT + 2:
                        sp.wait_ge(xl_done, ONE + b * NP + LAT + 1)
                    else:
                        sp.wait_ge(tp, ONE + b * 4 * (NP - 1) + 4 * max(p - 1, 0))
                    if p == LAT % 2:
                        sp.wait_ge(xl_done, ONE + b * NP)
                    n2 = 2 * P
                    if p == LAT:
                        sp.dma_start(lt, lt_scr[ds(b, 1), :, :].rearrange("o p (c m) -> p (o c) m", c=DC))\
                            .then_inc(piece_in[p % 2], 16)
                    else:
                        r0 = (p if p < LAT else p - 1) * T
                        src = A["ctx_4096"][ds(b, 1), r0:r0 + n2, :].rearrange("o (a p) d -> p (o a) d", p=P)
                        sp.dma_start(nat[:, p % 2, 0:2, :], src).then_inc(piece_in[p % 2], 16)
                        if rows[p] > n2:
                            src = A["ctx_4096"][ds(b, 1), r0 + n2:r0 + rows[p], :].rearrange("o p d -> p (o d)")
                            sp.dma_start(nat[0:rows[p] - n2, p % 2, 2, :], src).then_inc(piece_in[p % 2], 16)
                    if p == 1:
                        sp.wait_ge(s_mm, ONE + b * KV1 * KT * 2)
                        load_q(0)
                        load_q(1)
                    if p == 3:
                        load_wo(0)
                sp.wait_ge(y_st, ONE + b * 16)
                sp.dma_start(x[:, :, :].rearrange("p a b -> p (a b)"),
                             x_scr[ds(b, 1), :, :].rearrange("o p n -> p (o n)")).then_inc(x_in, 16)
                for kv in range(1, KV1):
                    if kv + 1 < KV1:
                        sp.wait_ge(s_mm, ONE + b * KV1 * KT * 2 + kv * KT * 2)
                        load_q(kv + 1)
                    load_wo(kv)
            sp.wait_ge(y_st, ONE + B * 16)
            sp.wait_ge(z_st, ONE + B * 16)

        @block.gpsimd
        def _(pool):
            for s in in_loop:
                pool.sem_inc(s, ONE)
            ready = Chain(pool, const, 0)
            ready.link(pool.memset(one[:, :], 1.0))
            ready.link(pool.memset(parts[:, :, :, XW - 1:DC * XW:XW].bitcast(F32), 0.0))
            ready.link(pool.memset(vh[:, :, :, HD1:HD1 + 1].bitcast(F32), 1.0))
            ready.link(pool.memset(vl[:, :, :, HD1:HD1 + 1].bitcast(F32), 0.0))
            ready.link(pool.memset(kh[HD1:HD1 + 1, :, :].bitcast(F32), 1.0))
            with pool.Fori(0, B) as b:
                for n in range(KV1 * KT):
                    m = keys[n % KT]
                    for half in range(2):
                        cols = slice(half * BANK, (half + 1) * BANK)
                        pool.wait_ge(exp_done, ONE + b * KV1 * KT * 2 + 2 * n + half + 1)
                        pool.tensor_tensor(pl[0:m, n % 2, cols], pf[0:m, half, :],
                                           ph[0:m, n % 2, cols].bitcast(F32), ALU.subtract).then_inc(plo, 1)

        @block.tensor
        def _(pe):

            def turn(e, p):
                pe.wait_ge(piece_in[p % 2], piece_loaded(e, p))
                if p == 0:
                    pe.wait_ge(exp_done, ONE + e * KV1 * KT * 2)
                elif p == 1:
                    pe.wait_ge(xl_done, ONE + e * NP + 1)
                else:
                    pe.wait_ge(mx_done, ONE + e * NP * QT + (p - 1) * QT)
                for c in range(DC):
                    for t in range(-(-rows[p] // P)):
                        m = min(P, rows[p] - t * P)
                        mm = pe.transpose(bank(c)[:, t * P:t * P + m], nat[0:m, p % 2, t, c * P:(c + 1) * P],
                                          ident[0:m, 0:m])
                    mm.then_inc(tp, 1)

            def three(out, lhs, rhs, fill):
                n = 0
                for l, r in ((0, 0), (1, 0), (0, 1)):
                    for c in range(DC):
                        mm = pe.matmul(out, lhs(l, c), rhs(r, c), start=(n == 0), stop=(n == 3 * DC - 1))
                        n += 1
                        if n % 3 == 0:
                            fill()
                return mm

            def keys_of(e, p, kv):
                if kv == 0:
                    pe.wait_ge(xl_done, ONE + e * NP + p + 1)
                n, i = rows[p] + rows[p] % 2, p * KV1 + kv
                if i >= 2:
                    pe.wait_ge(klo, ONE + e * NP * KV1 + i - 1)
                else:
                    pe.wait_ge(o_done, ONE + e * KV1 * 2)
                three(bank(OB + i % 2)[0:HD1, 0:n],
                      lambda l, c: (wkvh, wkvl)[l][:, c, kv * HD1:(kv + 1) * HD1],
                      lambda r, c: (xh, xl)[r][:, p % 2, c, 0:n], lambda: None).then_inc(k_mm, 1)

            def first_max(e, p, j):
                n = p * QT + j
                if j == 0:
                    pe.wait_ge(khi, ONE + e * NP * KV1 + p * KV1 + 1)
                    if p == 0:
                        pe.wait_ge(q_in[0], ONE + e * 64 + 32)
                    if p + 1 < NP:
                        pe.wait_ge(xl_done, ONE + e * NP + p + 2)
                if n >= 4:
                    pe.wait_ge(mx_done, ONE + e * NP * QT + n - 3)
                k = rows[p] + rows[p] % 2
                pe.matmul(bank(j % 4)[:, 0:k], qh[0:HD1, 0, j * P:(j + 1) * P], kh[0:HD1, 0, p * T:p * T + k],
                          start=True, stop=True).then_inc(mx_mm, 1)

            def values_of(e, p):
                items = iter(range(QT))

                def fill():
                    j = next(items, None)
                    if j is not None:
                        first_max(e, p, j)

                for t in range(-(-rows[p] // P)):
                    i, m = 2 * p + t, min(P, rows[p] - t * P)
                    if i == KT - 1:
                        max_rows(e, 0)
                    if i >= 2:
                        pe.wait_ge(v_done, ONE + e * KT + i - 1)
                    else:
                        pe.wait_ge(ring_done, ONE + e * RING)
                    if p == 2:
                        pe.wait_ge(h_done, ONE + e * TT)
                    if p == 3:
                        pe.wait_ge(z_done, ONE + e)
                        pe.wait_ge(h8_done, ONE + e)
                    if p == 4:
                        pe.wait_ge(dl_done, ONE + e)
                    three(bank(M0 + i % 2)[0:m, 0:W],
                          lambda l, c: (xh, xl)[l][:, p % 2, c, t * P:t * P + m],
                          lambda r, c: (wkvh, wkvl)[r][:, c, W:2 * W], fill).then_inc(v_mm, 1)
                for _ in range(QT):
                    fill()

            def ring_item(e, kind, kv, i):
                n = ring[kind, kv, i]
                at = bank(M0 + n % 2)
                if n >= 2:
                    pe.wait_ge(ring_done, ONE + e * RING + n - 1)
                if kind == "max":
                    if i == 0:
                        pe.wait_ge(q_in[kv % 2], ONE + e * 64 + 32 * (kv // 2 + 1))
                    if i < 2:
                        pe.wait_ge(*((row_done, ONE + e * 2 * KV1 + 2 * kv) if kv > 1 else (v_done, ONE + (e + 1) * KT)))
                    j, (k0, _, k) = i // len(cuts), cuts[i % len(cuts)]
                    mm = pe.matmul(at[:, 0:k], qh[0:HD1, kv % 2, j * P:(j + 1) * P],
                                   kh[0:HD1, kv, k0:k0 + k], start=True, stop=True)
                elif kind == "sum":
                    pe.wait_ge(row_done, ONE + e * 2 * KV1 + 2 * min(kv + 2, KV1))
                    pe.wait_ge(o_done, ONE + e * 2 * KV1 + 2 * kv + 2)
                    for j in range(QT):
                        mm = pe.matmul(at[:, j:j + 1], o[HD1:HD1 + 1, j * P:(j + 1) * P], one[HD1:HD1 + 1, 0:1],
                                       start=True, stop=True)
                else:
                    if i == 0:
                        pe.wait_ge(wo_in, ONE + e * 16 * KV1 + 16 * (kv + 1))
                    h, t = i // TT, i % TT
                    mm = pe.matmul(at, o[0:HD1, h * T + t * P:h * T + (t + 1) * P], woT[:, h, :],
                                   start=True, stop=True)
                mm.then_inc(ring_mm, 1)

            def max_rows(e, kv):
                pe.wait_ge(mxr_done, ONE + e * KV1 + kv + 1)
                if kv == 0:
                    pe.wait_ge(klo, ONE + (e + 1) * NP * KV1)
                for half in range(2):
                    for j in range(4):
                        mm = pe.matmul(bank(row_bank(kv, half))[HD1:HD1 + 1, j * P:(j + 1) * P],
                                       mx[:, 4 * half + j:4 * half + j + 1], ident[:, :], start=True, stop=True)
                    mm.then_inc(row_mm, 1)

            def scores(e, kv, kt, fill):
                n = kv * KT + kt
                if kt == 0:
                    pe.wait_ge(row_done, ONE + e * 2 * KV1 + 2 * kv + 2)
                if n >= 2:
                    pe.wait_ge(exp_done, ONE + e * KV1 * KT * 2 + 2 * (n - 1))
                k0, m = kt * P, keys[kt]
                for half in range(2):
                    out = bank((n % 2) * 2 + half)[0:m, :]
                    cols = slice(half * BANK, (half + 1) * BANK)
                    pe.matmul(out, kh[:, kv, k0:k0 + m], qh[:, kv % 2, cols], start=True, stop=False)
                    pe.matmul(out, kl[:, kv, k0:k0 + m], qh[0:HD1, kv % 2, cols], start=False, stop=False)
                    mm = pe.matmul(out, kh[0:HD1, kv, k0:k0 + m], ql[:, kv % 2, cols], start=False, stop=True)
                    mm.then_inc(s_mm, 1)
                    if half == 0:
                        fill()

            def values(e, kv, kt, fill):
                n = kv * KT + kt
                if kt == 0:
                    pe.wait_ge(o_done, ONE + e * 2 * KV1 + 2 * kv)
                m = keys[kt]
                for half in range(2):
                    out, cols = bank(OB + half)[0:HD1 + 1, :], slice(half * BANK, (half + 1) * BANK)
                    pe.wait_ge(phi, ONE + e * KV1 * KT * 2 + 2 * n + half + 1)
                    pe.matmul(out, vh[0:m, kt, kv, :], ph[0:m, n % 2, cols], start=(kt == 0), stop=False)
                    pe.matmul(out, vl[0:m, kt, kv, :], ph[0:m, n % 2, cols], start=False, stop=False)
                    pe.wait_ge(plo, ONE + e * KV1 * KT * 2 + 2 * n + half + 1)
                    mm = pe.matmul(out, vh[0:m, kt, kv, :], pl[0:m, n % 2, cols], start=False, stop=(kt == KT - 1))
                    if half == 0:
                        fill()
                mm.then_inc(av_mm, 1)

            def attend(e):
                pe.wait_ge(klo, ONE + (e + 1) * NP * KV1)
                pe.wait_ge(mx_done, ONE + (e + 1) * NP * QT)
                for kv in range(KV1):
                    items = iter(beside(kv))

                    def fill():
                        item = next(items, None)
                        if item:
                            ring_item(e, *item)

                    scores(e, kv, 0, lambda: None)
                    for kt in range(KT):
                        if kt + 1 < KT:
                            scores(e, kv, kt + 1, fill)
                            fill()
                        if kv + 1 < KV1 and kt == KT - 2:
                            max_rows(e, kv + 1)
                        late = kt > KT - 4
                        values(e, kv, kt, (lambda: None) if late else fill)
                        if not late:
                            fill()

            def turn_x(e, f):
                pe.wait_ge(n_done, ONE + e + 1)
                if f is not None:
                    pe.wait_ge(v_done, ONE + f * KT + 4)
                for half in range(2):
                    for c in range(2):
                        for t in range(TT):
                            mm = pe.transpose(bank(M0 + half)[:, c * T + t * P:c * T + (t + 1) * P],
                                              xn[:, t, (2 * half + c) * P:(2 * half + c + 1) * P], ident[:, :])
                    mm.then_inc(xT_tp, 1)

            def forward(e, f, step):
                if f is not None:
                    pe.wait_ge(v_done, ONE + f * KT + 4 + 2 * step)
                if step == 0:
                    pe.wait_ge(xT_a, ONE + e + 1)
                    pe.wait_ge(xT_d, ONE + e + 1)
                    for t in range(TT):
                        for c in range(DC):
                            mm = pe.matmul(bank(M0 + t), xT[:, c, t * P:(t + 1) * P], w1T[:, c, :],
                                           start=(c == 0), stop=(c == DC - 1))
                        mm.then_inc(h_mm, 1)
                if step == 1:
                    pe.wait_ge(h_done, ONE + e * TT + TT)
                    for c in range(DC):
                        mm = pe.matmul(bank(M0)[0:R, 0:T], aw[:, c, :], xT[:, c, :],
                                       start=(c == 0), stop=(c == DC - 1))
                    mm.then_inc(z_mm, 1)
                    for c in range(DC):
                        mm = pe.matmul(bank(M0 + 1)[:, 0:NE], xT[:, c, 1:T:2], w1T[:, c, 0:NE],
                                       start=(c == 0), stop=(c == DC - 1))
                    mm.then_inc(h8_mm, 1)
                if step == 2:
                    pe.wait_ge(z_done, ONE + e + 1)
                    pe.matmul(bank(M0)[:, 0:NE], zb[:, 1:T:2], liT[:, :], start=True, stop=True).then_inc(dl_mm, 1)

            def between(e, f):
                outs = iter(beside(KV1) if e is not None else [])

                def out(n):
                    for _ in range(n):
                        item = next(outs, None)
                        if item:
                            ring_item(e, *item)

                for p in range(NP):
                    if p == NP - 1 and e is None:
                        pe.wait_ge(const, 2)
                    if p == 0:
                        if f is not None:
                            turn(f, 0)
                        out(4)
                    for kv in range(KV1):
                        if f is not None:
                            if kv == (2 if p == 0 else 0) and p + 1 < NP and p + 1 != LAT:
                                turn(f, p + 1)
                            keys_of(f, p, kv)
                        if p == 0:
                            out(1 if kv < KV1 - 1 else 2)
                        if kv == 1 and e is not None and 2 <= p < 5:
                            forward(e, f, p - 2)
                    if f is not None:
                        values_of(f, p)
                    if p == 1 and e is not None:
                        turn_x(e, f)

            between(None, 0)
            pe.wait_ge(w_small, 64)
            pe.wait_ge(const, 5)
            with pe.Fori(0, B - 1) as b:
                attend(b)
                between(b, b + 1)
            attend(B - 1)
            between(B - 1, None)

        def turned(n):
            return ps[:, 0:DC * BANK].rearrange("p (c m) -> p c m", c=DC)[:, :, 0:n]

        @block.scalar
        def _(act):
            def piece_hi(e, p):
                act.wait_ge(v_mm, ONE + e * KT + 2 * max(p - 1, 0))
                if p == LAT:
                    act.wait_ge(piece_in[p % 2], piece_loaded(e, p))
                else:
                    act.wait_ge(tp, ONE + e * 4 * (NP - 1) + 4 * (p + 1 if p < LAT else p))
                act.copy(xh[:, p % 2, :, 0:rows[p]], lt if p == LAT else turned(rows[p])).then_inc(xh_done, 1)

            def keys_hi(e, p, kv):
                i, n, c0 = p * KV1 + kv, rows[p] + rows[p] % 2, p * T
                act.wait_ge(k_mm, ONE + e * NP * KV1 + i + 1)
                act.copy(kh[0:HD1, kv, c0:c0 + n], bank(OB + i % 2)[0:HD1, 0:n]).then_inc(khi, 1)

            def copy_values(e, p):
                for t in range(-(-rows[p] // P)):
                    i, m = 2 * p + t, min(P, rows[p] - t * P)
                    if i == KT - 1:
                        rows_of(e, 0)
                    act.wait_ge(v_mm, ONE + e * KT + i + 1)
                    act.copy(vh[0:m, i, :, 0:HD1], bank(M0 + i % 2)[0:m, 0:W].rearrange("p (k e) -> p k e", e=HD1))\
                        .then_inc(vhi, 1)

            def rows_of(e, kv):
                for half in range(2):
                    act.wait_ge(row_mm, ONE + e * 2 * KV1 + 2 * kv + half + 1)
                    act.mul(qh[HD1:HD1 + 1, kv % 2, half * BANK:(half + 1) * BANK],
                            bank(row_bank(kv, half))[HD1:HD1 + 1, :], -1.0).then_inc(row_done, 1)

            def attend(e):
                act.wait_ge(v_mm, ONE + (e + 1) * KT)
                act.wait_ge(h_mm, ONE + e * TT)
                act.wait_ge(h8_mm, ONE + e)
                act.wait_ge(xT_tp, ONE + e * 2)
                for kv in range(KV1):
                    for kt in range(KT):
                        n = kv * KT + kt
                        act.wait_ge(av_mm, ONE + e * KV1 * KT + max(n - 1, 0))
                        for half in range(2):
                            src = bank((n % 2) * 2 + half)[0:keys[kt], :]
                            cols = slice(half * BANK, (half + 1) * BANK)
                            act.wait_ge(s_mm, ONE + e * KV1 * KT * 2 + 2 * n + half + 1)
                            act.activation(ph[0:keys[kt], n % 2, cols], src, ACT.Exp, scale=S1).then_inc(phi, 1)
                            act.wait_ge(plo, ONE + e * KV1 * KT * 2 + max(2 * n + half - 1, 0))
                            act.activation(pf[0:keys[kt], half, :], src, ACT.Exp, scale=S1)\
                                .then_inc(exp_done, 1)
                    if kv + 1 < KV1:
                        rows_of(e, kv + 1)
                    act.wait_ge(av_mm, ONE + e * KV1 * KT + (kv + 1) * KT)
                    if kv:
                        act.wait_ge(ring_mm, ONE + e * RING + ring["out", kv - 1, TT * G - 1] + 1)
                    for half in range(2):
                        act.copy(o[0:HD1 + 1, half * BANK:(half + 1) * BANK], bank(OB + half)[0:HD1 + 1, :])\
                            .then_inc(o_done, 1)

            def forward(e, step):
                if step == 1:
                    act.wait_ge(z_mm, ONE + e + 1)
                    act.wait_ge(z_st, ONE + e * 16)
                    act.copy(zb[:, :], bank(M0)[0:R, 0:T]).then_inc(z_done, 1)
                    act.wait_ge(z_done, ONE + e + 1)
                    act.dma_start(z_scr[ds(e, 1), :, :].rearrange("o p n -> p (o n)"), zb[:, :]).then_inc(z_st, 16)
                    act.wait_ge(h_done, ONE + e * TT + TT)
                    act.dma_start(y_scr[ds(e, 1), :, :].rearrange("o p n -> p (o n)"),
                                  x[:, :, :].rearrange("p a b -> p (a b)")).then_inc(y_st, 16)

            def between(e, f):
                if f is not None:
                    piece_hi(f, 0)
                for p in range(NP):
                    for kv in range(KV1):
                        if f is not None:
                            if kv == (2 if p == 0 else 0) and p + 1 < NP:
                                piece_hi(f, p + 1)
                            keys_hi(f, p, kv)
                        if kv == 1 and e is not None and 2 <= p < 5:
                            forward(e, p - 2)
                    if f is not None:
                        copy_values(f, p)
                    if p == 1 and e is not None:
                        act.wait_ge(xT_tp, ONE + e * 2 + 1)
                        act.copy(xT[:, 0:2, :], bank(M0).rearrange("p (c m) -> p c m", c=2)).then_inc(xT_a, 1)

            act.dma_start(aw[:, :, :], A["L1_ffn_A"].rearrange("(c p) r -> p c r", p=P)).then_inc(w_small, 16)
            with nc.allow_non_contiguous_dma(reason="256 values"):
                act.dma_start(liT[:, :], A["L1_ffn_LiMEs"].rearrange("e r -> r e")).then_inc(w_small, 16)
            act.dma_start(bias8[:, :], A["L1_ffn_b"][0:NE].rearrange("(a n) -> a n", a=1).to_broadcast([P, NE]))\
                .then_inc(w_small, 16)
            act.dma_start(w1T[:, :, :].rearrange("p a b -> p (a b)"), w1_scr).then_inc(w_small, 16)
            between(None, 0)
            with act.Fori(0, B - 1) as b:
                attend(b)
                between(b, b + 1)
            attend(B - 1)
            between(B - 1, None)

        @block.vector
        def _(dve):
            def piece_lo(e, p):
                dve.wait_ge(xh_done, ONE + e * NP + p + 1)
                whole, hi = (lt if p == LAT else turned(rows[p])), xh[:, p % 2, :, 0:rows[p]]
                dve.tensor_tensor(xl[:, p % 2, :, 0:rows[p]], whole, hi.bitcast(F32) if p == LAT else hi,
                                  ALU.subtract).then_inc(xl_done, 1)

            def keys_lo(e, p, kv):
                i, n, c0 = p * KV1 + kv, rows[p] + rows[p] % 2, p * T
                dve.wait_ge(khi, ONE + e * NP * KV1 + i + 1)
                dve.tensor_tensor(kl[:, kv, c0:c0 + n], bank(OB + i % 2)[0:HD1, 0:n], kh[0:HD1, kv, c0:c0 + n],
                                  ALU.subtract).then_inc(klo, 1)

            def values_lo(e, p, t):
                i, m = 2 * p + t, min(P, rows[p] - t * P)
                hi, lo = (a[0:m, i, :, 0:HD1] for a in (vh, vl))
                dve.wait_ge(vhi, ONE + e * KT + i + 1)
                dve.tensor_tensor(lo, bank(M0 + i % 2)[0:m, 0:W].rearrange("p (k e) -> p k e", e=HD1), hi,
                                  ALU.subtract).then_inc(v_done, 1)

            def first_max(e, p):
                for j in range(QT):
                    if j % 4 == 0 and j:
                        values_lo(e, p, j // 4 - 1)
                    if p == 0 and j == 0:
                        dve.wait_ge(mxr_done, ONE + e * KV1)
                    dve.wait_ge(mx_mm, ONE + e * NP * QT + p * QT + j + 1)
                    dve.reduce_max(pm[:, j, p:p + 1], bank(j % 4)[:, 0:rows[p]], AX).then_inc(mx_done, 1)
                values_lo(e, p, 1)
                if p == NP - 1:
                    max_all(e, 0)
                    values_lo(e, p, 2)

            def max_all(e, kv):
                if kv == 0:
                    dve.wait_ge(mx_done, ONE + (e + 1) * NP * QT)
                else:
                    dve.wait_ge(ring_done, ONE + e * RING + ring["max", kv, NI - 1] + 1)
                dve.wait_ge(row_mm, ONE + e * 2 * KV1 + 2 * kv)
                dve.reduce_max(mx[:, :], pm[:, :, 0:(NP if kv == 0 else len(cuts))], AX).then_inc(mxr_done, 1)

            def ring_item(e, kind, kv, i):
                n = ring[kind, kv, i]
                at = bank(M0 + n % 2)
                if kind == "max" and i == 0:
                    dve.wait_ge(mxr_done, ONE + e * KV1 + kv)
                if kind == "sum" and kv:
                    dve.wait_ge(ring_done, ONE + e * RING + ring["out", kv - 1, TT * G - 1] + 1)
                if kind == "sum" and not kv:
                    dve.wait_ge(ring_done, ONE + e * RING)
                if kind == "out":
                    before = ring["out", kv, i - TT] if i >= TT else ring["sum", kv, 0]
                    dve.wait_ge(ring_done, ONE + e * RING + before + 1)
                    if kv == 0 and i == 0:
                        dve.wait_ge(x_in, ONE + e * 16 + 16)
                dve.wait_ge(ring_mm, ONE + e * RING + n + 1)
                if kind == "max":
                    j, ch = i // len(cuts), i % len(cuts)
                    ins = dve.reduce_max(pm[:, j, ch:ch + 1], at[:, 0:cuts[ch][1]], AX)
                elif kind == "sum":
                    ins = dve.reciprocal(rec[:, :], at[:, 0:QT])
                else:
                    h, t = i // TT, i % TT
                    ins = dve.scalar_tensor_tensor(x[:, t, :], at, rec[:, i:i + 1], x[:, t, :], ALU.mult, ALU.add)
                ins.then_inc(ring_done, 1)

            def attend(e):
                for kv in range(KV1):
                    items = iter(beside(kv))

                    def fill(n):
                        for _ in range(n):
                            item = next(items, None)
                            if item:
                                ring_item(e, *item)

                    for kt in range(KT):
                        late = kt > KT - 4
                        if kt + 1 < KT:
                            fill(1)
                        if kt + 1 < KT:
                            fill(1)
                        if not late:
                            fill(2)
                        if kv + 1 < KV1 and kt == KT - 3:
                            max_all(e, kv + 1)

            def normalise(chain, e, pause):
                dve.wait_ge(ring_done, ONE + (e + 1) * RING)
                layernorm(dve, chain, xn, x, ln["st"], ln["mv"], ln["v"], ln["t"], ln["u"], ln["y"], pause)\
                    .then_inc(n_done, 1)

            def forward(e, step):
                if step == 0:
                    for t in range(TT):
                        dve.wait_ge(h_mm, ONE + e * TT + t + 1)
                        dve.tensor_tensor(x[:, t, :], bank(M0 + t), x[:, t, :], ALU.add).then_inc(h_done, 1)
                if step == 1:
                    dve.wait_ge(h8_mm, ONE + e + 1)
                    dve.tensor_tensor(h8all[:, ds(e, 1), :].rearrange("p o e -> p (o e)"), bank(M0 + 1)[:, 0:NE],
                                      bias8[:, :], ALU.add).then_inc(h8_done, 1)
                if step == 2:
                    dve.wait_ge(dl_mm, ONE + e + 1)
                    dve.tensor_copy(dlall[:, ds(e, 1), :].rearrange("p o e -> p (o e)"), bank(M0)[:, 0:NE])\
                        .then_inc(dl_done, 1)

            def between(chain, e, f):
                outs = iter(beside(KV1) if e is not None else [])

                def out(n):
                    for _ in range(n):
                        item = next(outs, None)
                        if item:
                            ring_item(e, *item)

                if f is not None:
                    piece_lo(f, 0)
                out(4)
                for p in range(NP):
                    kvs = iter(range(KV1))

                    def next_keys():
                        kv = next(kvs, None)
                        if kv is not None and f is not None:
                            if kv == 2 and p == 0:
                                piece_lo(f, 1)
                            keys_lo(f, p, kv)
                            if kv == 0 and 0 < p < NP - 1:
                                piece_lo(f, p + 1)

                    for kv in range(KV1):
                        next_keys()
                        if p == 0:
                            out(1 if kv < KV1 - 1 else 2)
                        if kv == 0 and p == 1 and e is not None:
                            normalise(chain, e, next_keys)
                        if kv == 1 and e is not None and 2 <= p < 5:
                            forward(e, p - 2)
                    if f is not None:
                        first_max(f, p)
                    if p == 1 and e is not None:
                        dve.wait_ge(xT_tp, ONE + e * 2 + 2)
                        dve.tensor_copy(xT[:, 2:4, :], bank(M0 + 1).rearrange("p (c m) -> p c m", c=2)).then_inc(xT_d, 1)

            between(None, None, 0)
            with dve.Fori(0, B - 1) as b:
                attend(b)
                between(Chain(dve, step, LN_STEPS, b), b, b + 1)
            attend(B - 1)
            between(Chain(dve, step, LN_STEPS, B - 1), B - 1, None)


def mixture(nc, A, ident, ps, y_scr, z_scr, h8all, dlall, out):
    NA = B * NE
    with ExitStack() as ctx:
        def sb(name, shape, dt=F32):
            return ctx.enter_context(nc.sbuf_tensor(name, shape, dt))

        def sem(name):
            return ctx.enter_context(nc.semaphore(name))

        y = sb("y", [P, B, TT, D])
        z = sb("z", [R, B, T])
        zp = sb("zp", [R + 1, B, T])
        li = sb("li", [NE, R])
        bm = sb("bm", [R + 1, D])
        ones = sb("ones", [2, P])
        ab = sb("ab", [P, 2, NA])
        pmx = sb("pmx", [P, 2])
        rows2 = sb("rows2", [2, P])
        sc = sb("sc", [2, 4])
        dg = sb("dg", [2, 2])
        scl = sb("scl", [P, 2])
        lg = sb("lg", [P, B, NE])
        pb = sb("pb", [P, B, NE])
        top = sb("top", [P, B, NE])
        wt = sb("wt", [P, B, NE])
        r4 = sb("r4", [P, B])
        wT = sb("wT", [NE, B * P])
        y_in, z_in, w_in, const = sem("y_in"), sem("z_in"), sem("w_in"), sem("const2")
        step, a_in, a_out = sem("dve_step2"), sem("act_asked"), sem("act_done")
        to_pe, from_pe = sem("pe_asked"), sem("pe_done")
        zp_done, d_mm, y_done, o_st = sem("zp_ready"), sem("delta_product"), sem("y_ready"), sem("out_stored")
        block = ctx.enter_context(nc.Block())

        def bank(i, n=BANK):
            return ps[:, i * BANK:i * BANK + n]

        @block.sync
        def _(sp):
            sp.dma_start(bm[0:R, :], A["L1_ffn_Bmat"]).then_inc(w_in, 16)
            sp.dma_start(bm[R:R + 1, :], A["L1_ffn_b"].rearrange("(a n) -> a n", a=1)).then_inc(w_in, 16)
            sp.dma_start(li[:, :], A["L1_ffn_LiMEs"]).then_inc(w_in, 16)
            sp.dma_start(z[:, :, :], z_scr.rearrange("b r t -> r b t")).then_inc(z_in, 16)
            sp.dma_start(y[:, :, :, :].rearrange("p b t d -> p b (t d)"), y_scr.rearrange("b p n -> p b n"))\
                .then_inc(y_in, 16)
            for b in range(B):
                sp.wait_ge(y_done, (b + 1) * TT)
                sp.dma_start(out[b].rearrange("(t p) d -> p t d", p=P), y[:, b, :, :]).then_inc(o_st, 16)
            sp.wait_ge(o_st, 16 * B)

        @block.gpsimd
        def _(pool):
            pool.memset(ones[:, :], 1.0).then_inc(const, 1)
            pool.memset(zp[R:R + 1, :, :], 1.0).then_inc(const, 1)

        @block.tensor
        def _(pe):
            pe.wait_ge(const, 2)
            pe.wait_ge(to_pe, 1)
            pe.matmul(bank(0)[0:2, 0:P], pmx[:, :], ident[:, :], start=True, stop=True).then_inc(from_pe, 1)
            pe.wait_ge(to_pe, 2)
            pe.matmul(bank(1)[:, 0:2], ones[:, :], dg[:, :], start=True, stop=True).then_inc(from_pe, 1)
            pe.wait_ge(to_pe, 3)
            for b in range(B):
                mm = pe.matmul(bank(2)[0:NE, b * P:(b + 1) * P], wt[:, b, :], ident[:, :], start=True, stop=True)
            mm.then_inc(from_pe, 1)
            pe.wait_ge(to_pe, 4)
            pe.wait_ge(w_in, 48)
            pe.matmul(bank(3)[0:R, :], li[:, :], wT[:, :], start=True, stop=True).then_inc(from_pe, 1)
            pe.wait_ge(zp_done, 2)
            for n in range(B * TT):
                if n >= 4:
                    pe.wait_ge(y_done, n - 3)
                b, t = n // TT, n % TT
                pe.matmul(bank(4 + n % 4), zp[:, b, t * P:(t + 1) * P], bm[:, :], start=True, stop=True)\
                    .then_inc(d_mm, 1)

        @block.scalar
        def _(act):
            act.wait_ge(a_in, 1)
            act.activation(pb[:, :, :], lg[:, :, :], ACT.Exp).then_inc(a_out, 1)
            act.wait_ge(a_in, 2)
            act.activation(wt[:, :, :], lg[:, :, :], ACT.Exp, scale=-2.0).then_inc(a_out, 1)

        @block.vector
        def _(dve):
            chain = Chain(dve, step, 0)
            link = chain.link
            flat = "p b e -> p (b e)"
            for i, s in enumerate((h8all, dlall)):
                sf = s[:, :, :].rearrange(flat)
                link(dve.scalar_tensor_tensor(ab[:, i, :], sf, -1.0, sf, ALU.mult, ALU.max))
            dve.reduce_max(pmx[:, :], ab[:, :, :], AX).then_inc(to_pe, 1)
            dve.wait_ge(from_pe, 1)
            link(dve.reduce_max(sc[:, 0:1], bank(0)[0:2, 0:P], AX))
            link(dve.tensor_scalar(sc[:, 1:2], sc[:, 0:1], 1e-6, None, ALU.max))
            link(dve.reciprocal(sc[:, 2:3], sc[:, 1:2]))
            dve.tensor_scalar(dg[:, :], ident[0:2, 0:2], sc[:, 2:3], 0.5, ALU.mult, ALU.mult).then_inc(to_pe, 1)
            dve.wait_ge(from_pe, 2)
            link(dve.tensor_copy(scl[:, :], bank(1)[:, 0:2]))
            link(dve.tensor_scalar(pb[:, :, :], dlall[:, :, :], scl[:, 1:2], None, ALU.mult))
            link(dve.scalar_tensor_tensor(lg[:, :, :], h8all[:, :, :], scl[:, 0:1], pb[:, :, :], ALU.mult, ALU.add))

            def over(a):
                return a.rearrange("p (b o) -> p b o", o=1).broadcast_to([P, B, NE])

            link(dve.reduce_max(r4[:, :], lg[:, :, :], AX))
            dve.tensor_tensor(lg[:, :, :], lg[:, :, :], over(r4[:, :]), ALU.subtract).then_inc(a_in, 1)
            dve.wait_ge(a_out, 1)
            link(dve.reduce_sum(r4[:, :], pb[:, :, :], AX))
            link(dve.reciprocal(r4[:, :], r4[:, :]))
            link(dve.tensor_tensor(pb[:, :, :], pb[:, :, :], over(r4[:, :]), ALU.mult))
            for b in range(B):
                link(dve.max(top[:, b, :], pb[:, b, :]))
            dve.tensor_tensor(lg[:, :, :], pb[:, :, :], top[:, :, 1:2].broadcast_to([P, B, NE]), ALU.subtract)\
                .then_inc(a_in, 1)
            dve.wait_ge(a_out, 2)
            link(dve.tensor_scalar(wt[:, :, :], wt[:, :, :], 1.0, None, ALU.add))
            link(dve.reciprocal(wt[:, :, :], wt[:, :, :]))
            link(dve.tensor_tensor(wt[:, :, :], wt[:, :, :], pb[:, :, :], ALU.mult))
            link(dve.reduce_sum(r4[:, :], wt[:, :, :], AX))
            link(dve.tensor_scalar(r4[:, :], r4[:, :], 1e-9, None, ALU.add))
            link(dve.reciprocal(r4[:, :], r4[:, :]))
            dve.tensor_tensor(wt[:, :, :], wt[:, :, :], over(r4[:, :]), ALU.mult).then_inc(to_pe, 1)
            dve.wait_ge(from_pe, 3)
            dve.tensor_copy(wT[:, :], bank(2)[0:NE, :]).then_inc(to_pe, 1)
            dve.wait_ge(w_in, 48)
            dve.tensor_scalar(bm[0:R, :], bm[0:R, :], 16.0 / R, None, ALU.mult).then_inc(zp_done, 1)
            dve.wait_ge(from_pe, 4)
            dve.wait_ge(z_in, 16)
            dve.tensor_tensor(zp[0:R, :, :].rearrange("r b (a n) -> r (b a) n", n=2),
                              z[:, :, :].rearrange("r b (a n) -> r (b a) n", n=2),
                              bank(3)[0:R, :].rearrange("r (a o) -> r a o", o=1).broadcast_to([R, BANK, 2]), ALU.mult)\
                .then_inc(zp_done, 1)
            dve.wait_ge(y_in, 16)
            for n in range(B * TT):
                dve.wait_ge(d_mm, n + 1)
                dve.tensor_tensor(y[:, n // TT, n % TT, :], bank(4 + n % 4), y[:, n // TT, n % TT, :], ALU.add)\
                    .then_inc(y_done, 1)


_INS = ["x", "ctx_4096", "L0_xattn_Wq_d", "L0_xattn_W_qk", "L0_xattn_Wkv_d", "L0_xattn_Wv_u", "L0_ffn_weight_q",
        "L0_ffn_scale", "L0_ffn_zero_point", "L0_ffn_bias", "L1_xattn_Wq", "L1_xattn_Wk", "L1_xattn_Wv",
        "L1_xattn_Wo", "L1_ffn_W", "L1_ffn_b", "L1_ffn_A", "L1_ffn_Bmat", "L1_ffn_LiMEs"]


def kernel(**inputs):
    import numpy as _np
    import concourse.bacc as _bacc
    from concourse import mybir as _mybir
    from concourse.bass_utils import run_bass_kernel_spmd as _run

    nc = _bacc.Bacc("TRN2", target_bir_lowering=False, num_devices=1)
    arrays, args = {}, {}
    for name in _INS:
        a = _np.ascontiguousarray(inputs[name])
        arrays[f"in_{name}_dram"] = a
        args[name] = nc.dram_tensor(f"in_{name}_dram", a.shape, _mybir.dt.from_np(a.dtype), kind="ExternalInput").ap()
    out = nc.dram_tensor("out_0_dram", (B, T, D), F32, kind="ExternalOutput").ap()
    build(nc, args, out)
    r = _run(nc, [arrays], core_ids=[0])
    return r.results[0]["out_0_dram"]
```
